# Optimizing a Trainium2 kernel written in Bass

```python
import numpy as np
import jax
import jax.numpy as jnp

def _softmax(x, axis=-1):
    return jax.nn.softmax(x, axis=axis)

def _gelu(x):
    return jax.nn.gelu(x, approximate=True)

def _silu(x):
    return jax.nn.silu(x)

def _sigmoid(x):
    return jax.nn.sigmoid(x)

def _layernorm(x, axis=-1, eps=1e-05):
    m = jnp.mean(x, axis=axis, keepdims=True)
    v = jnp.var(x, axis=axis, keepdims=True)
    return (x - m) / jnp.sqrt(v + eps)

def _scatter_add(tgt, idx, src, axis=0):
    return tgt.at[idx].add(src)

def _segment_sum(src, seg, n):
    return jax.ops.segment_sum(src, seg, n)
kernel_name = 'mk_perceiver_d1_seqx_r2_692168'

def setup_inputs(seed: int=0):
    np.random.seed(seed)
    _w = jnp.asarray

    def _rec_inputs():
        import jax
        import jax.numpy as jnp
        _rk = jax.random.key(seed)
        x = -0.0003929 + 0.9999 * jax.random.normal(jax.random.fold_in(_rk, 1), (128, 32, 512), jnp.float32)
        _lenS = 32 - jax.random.randint(jax.random.fold_in(_rk, 7), (128,), 0, max(1, 32 // 4) + 1, jnp.int32)
        _lenS2 = 257 - jax.random.randint(jax.random.fold_in(_rk, 8), (128,), 0, max(1, 257 // 4) + 1, jnp.int32)
        _ctx_1024P = jax.random.normal(jax.random.fold_in(_rk, 11), (128, 16, 512), jnp.float32)
        _ctx_1024c = jax.random.dirichlet(jax.random.fold_in(_rk, 511), 0.3 * jnp.ones((16,), jnp.float32), (128, 257))
        _ctx_1024t = jnp.einsum('bsk,bkd->bsd', _ctx_1024c, _ctx_1024P)
        _ctx_1024t = _ctx_1024t * jax.lax.rsqrt(jnp.mean(jnp.square(_ctx_1024t)) + 1e-12) * 0.953939
        ctx_1024 = 2.81802e-05 + 1.00001 * (_ctx_1024t + 0.3 * jax.random.normal(jax.random.fold_in(_rk, 611), (128, 257, 512), jnp.float32))
        return (x, ctx_1024)
    x, ctx_1024 = _rec_inputs()

    def _L0_xattn_setup():
        import jax, jax.numpy as jnp
        import numpy as np
        B, S, E = (8, 1024, 512)
        EPS = 0.001

        def _layer_norm(x, gamma, beta):
            mu = jnp.mean(x, axis=-1, keepdims=True)
            var = jnp.mean(jnp.square(x - mu), axis=-1, keepdims=True)
            return gamma * (x - mu) * jax.lax.rsqrt(var + EPS) + beta

        def _attention(q_in, k_in, v_in, WQ, WK, WV, causal):
            Q = jnp.einsum('bse,ed->bsd', q_in, WQ)
            K = jnp.einsum('bse,ed->bsd', k_in, WK)
            V = jnp.einsum('bse,ed->bsd', v_in, WV)
            d = K.shape[-1]
            scores = jnp.einsum('bqd,bkd->bqk', Q, K) / jnp.sqrt(jnp.float32(d))
            if causal:
                qlen, klen = (scores.shape[-2], scores.shape[-1])
                mask = jnp.triu(jnp.ones((qlen, klen), bool), k=1)
                scores = jnp.where(mask[None], -jnp.inf, scores)
            p = jax.nn.softmax(scores, axis=-1)
            return jnp.einsum('bqk,bkd->bqd', p, V)
        key = jax.random.key(seed)
        ks = jax.random.split(key, 10)
        sc = 1.0 / np.sqrt(E)
        return {'inputs': jax.random.normal(ks[0], (B, S, E), jnp.float32), 'context': jax.random.normal(ks[1], (B, S, E), jnp.float32), 'Wq': jax.random.normal(ks[2], (E, E), jnp.float32) * sc, 'Wk': jax.random.normal(ks[3], (E, E), jnp.float32) * sc, 'Wv': jax.random.normal(ks[4], (E, E), jnp.float32) * sc, 'Wcq': jax.random.normal(ks[5], (E, E), jnp.float32) * sc, 'Wck': jax.random.normal(ks[6], (E, E), jnp.float32) * sc, 'Wcv': jax.random.normal(ks[7], (E, E), jnp.float32) * sc, 'gamma': jnp.ones((E,), jnp.float32), 'beta': jnp.zeros((E,), jnp.float32), 'W1': jax.random.normal(ks[8], (E, E), jnp.float32) * sc, 'b1': jnp.zeros((E,), jnp.float32)}
    _L0_xattn_all = _L0_xattn_setup()
    _L0_xattn_in = {k: v for k, v in _L0_xattn_all.items() if k in ('Wq', 'Wk', 'Wv', 'Wcq', 'Wck', 'Wcv', 'gamma', 'beta', 'W1', 'b1')}
    del _L0_xattn_all

    def _L0_attn_setup():
        import jax, jax.numpy as jnp
        import numpy as np
        import math
        N_HEAD = 16
        HEAD_QKV = 512
        WM_DECAY_LENGTH = 1024
        WM_DECAY_RATE = 1.0
        WM_ECHOIC = 16

        def decay_weight_matrix(n):
            dl = WM_DECAY_LENGTH - WM_ECHOIC + 1
            nums = jnp.linspace(0.0, 1.0, dl)
            decay_values = 1.0 - jnp.power(nums, 1.0 / (np.e * WM_DECAY_RATE))
            decay_values = jnp.concatenate([jnp.ones(WM_ECHOIC - 1), decay_values])
            decay_values = decay_values[:n]
            idx = jnp.arange(n)[:, None] - jnp.arange(n)[None, :]
            mat = decay_values[jnp.clip(idx, 0, n - 1)]
            return jnp.tril(mat).astype(jnp.float32)
        key = jax.random.key(seed)
        k1, k2, k3 = jax.random.split(key, 3)
        B, T, C = (2, 1024, 512)
        x = jax.random.normal(k1, (B, T, C), dtype=jnp.float32)
        W_attn = jax.random.normal(k2, (C, 3 * HEAD_QKV), dtype=jnp.float32) * (1.0 / math.sqrt(C))
        W_proj = jax.random.normal(k3, (HEAD_QKV, C), dtype=jnp.float32) * (1.0 / math.sqrt(HEAD_QKV))
        return {'x': x, 'W_attn': W_attn, 'W_proj': W_proj}
    _L0_attn_all = _L0_attn_setup()
    _L0_attn_in = {k: v for k, v in _L0_attn_all.items() if k in ('W_attn', 'W_proj')}
    del _L0_attn_all

    def _L0_ffn_setup():
        import jax, jax.numpy as jnp
        import numpy as np
        EPS = 1e-05

        def _ln(x, g, b):
            mu = jnp.mean(x, axis=-1, keepdims=True)
            var = jnp.mean(jnp.square(x - mu), axis=-1, keepdims=True)
            return (x - mu) * jax.lax.rsqrt(var + EPS) * g + b

        def _forward(x, index_b, index_t, sw1, sb1, sw2, sb2, sw3, sb3, s_ln_g, s_ln_b, sg_w, sg_b, eg_w, eg_b, exp_bias, ew1, eb1, ew2, eb2, ew3, eb3, sel_ln_g, sel_ln_b):
            x1 = jnp.einsum('btd,hd->bth', x, sw1) + sb1
            x2 = jnp.einsum('btd,hd->bth', x, sw2) + sb2
            sh = _ln(jax.nn.silu(x1) * x2, s_ln_g, s_ln_b)
            shared_out = jnp.einsum('bth,dh->btd', sh, sw3) + sb3
            x_moe = x[index_b, index_t]
            shared_scores = jax.nn.sigmoid(x_moe @ sg_w.T + sg_b)
            expert_scores = jax.nn.sigmoid(x_moe @ eg_w.T + eg_b)
            top1_idx = jnp.argmax(expert_scores + exp_bias, axis=-1)
            top1_score = jnp.take_along_axis(expert_scores, top1_idx[:, None], axis=-1)
            weights = jax.nn.softmax(jnp.concatenate([shared_scores, top1_score], axis=-1), axis=-1)
            shared_w, expert_w = (weights[:, 0], weights[:, 1])
            shared_moe_out = shared_out[index_b, index_t] * shared_w[:, None]
            h1 = jnp.einsum('md,ehd->meh', x_moe, ew1) + eb1
            h2 = jnp.einsum('md,ehd->meh', x_moe, ew2) + eb2
            z = _ln(jax.nn.silu(h1) * h2, sel_ln_g, sel_ln_b)
            out_all = jnp.einsum('meh,edh->med', z, ew3) + eb3
            expert_out = jnp.take_along_axis(out_all, top1_idx[:, None, None], axis=1)[:, 0]
            expert_moe_out = expert_out * expert_w[:, None]
            final_out = shared_out.at[index_b, index_t].set(shared_moe_out + expert_moe_out)
            return final_out
        B, T, D, E, H, M = (2, 1024, 512, 8, 256, 1024)
        key = jax.random.key(seed)
        ks = jax.random.split(key, 24)
        s = 0.02
        inp = {}
        inp['x'] = jax.random.normal(ks[0], (B, T, D), jnp.float32)
        flat = jnp.arange(M, dtype=jnp.int32) * 2
        inp['index_b'] = flat // T
        inp['index_t'] = flat % T
        inp['sw1'] = jax.random.normal(ks[1], (H, D), jnp.float32) * s
        inp['sb1'] = jnp.zeros((H,), jnp.float32)
        inp['sw2'] = jax.random.normal(ks[2], (H, D), jnp.float32) * s
        inp['sb2'] = jnp.zeros((H,), jnp.float32)
        inp['sw3'] = jax.random.normal(ks[3], (D, H), jnp.float32) * s
        inp['sb3'] = jnp.zeros((D,), jnp.float32)
        inp['s_ln_g'] = jnp.ones((H,), jnp.float32)
        inp['s_ln_b'] = jnp.zeros((H,), jnp.float32)
        inp['sg_w'] = jax.random.normal(ks[4], (1, D), jnp.float32) * s
        inp['sg_b'] = jnp.zeros((1,), jnp.float32)
        inp['eg_w'] = jax.random.normal(ks[5], (E, D), jnp.float32) * s
        inp['eg_b'] = jnp.zeros((E,), jnp.float32)
        inp['exp_bias'] = jnp.zeros((E,), jnp.float32)
        inp['ew1'] = jax.random.normal(ks[6], (E, H, D), jnp.float32) * s
        inp['eb1'] = jnp.zeros((E, H), jnp.float32)
        inp['ew2'] = jax.random.normal(ks[7], (E, H, D), jnp.float32) * s
        inp['eb2'] = jnp.zeros((E, H), jnp.float32)
        inp['ew3'] = jax.random.normal(ks[8], (E, D, H), jnp.float32) * s
        inp['eb3'] = jnp.zeros((E, D), jnp.float32)
        inp['sel_ln_g'] = jnp.ones((H,), jnp.float32)
        inp['sel_ln_b'] = jnp.zeros((H,), jnp.float32)
        return inp
    _L0_ffn_all = _L0_ffn_setup()
    _L0_ffn_in = {k: v for k, v in _L0_ffn_all.items() if k in ('index_b', 'index_t', 'sw1', 'sb1', 'sw2', 'sb2', 'sw3', 'sb3', 's_ln_g', 's_ln_b', 'sg_w', 'sg_b', 'eg_w', 'eg_b', 'exp_bias', 'ew1', 'eb1', 'ew2', 'eb2', 'ew3', 'eb3', 'sel_ln_g', 'sel_ln_b')}
    del _L0_ffn_all
    return {'x': x, 'ctx_1024': ctx_1024, 'L0_xattn_Wq': _L0_xattn_in['Wq'], 'L0_xattn_Wk': _L0_xattn_in['Wk'], 'L0_xattn_Wv': _L0_xattn_in['Wv'], 'L0_xattn_Wcq': _L0_xattn_in['Wcq'], 'L0_xattn_Wck': _L0_xattn_in['Wck'], 'L0_xattn_Wcv': _L0_xattn_in['Wcv'], 'L0_xattn_gamma': _L0_xattn_in['gamma'], 'L0_xattn_beta': _L0_xattn_in['beta'], 'L0_xattn_W1': _L0_xattn_in['W1'], 'L0_xattn_b1': _L0_xattn_in['b1'], 'L0_attn_W_attn': _L0_attn_in['W_attn'], 'L0_attn_W_proj': _L0_attn_in['W_proj'], 'L0_ffn_index_b': _L0_ffn_in['index_b'], 'L0_ffn_index_t': _L0_ffn_in['index_t'], 'L0_ffn_sw1': _L0_ffn_in['sw1'], 'L0_ffn_sb1': _L0_ffn_in['sb1'], 'L0_ffn_sw2': _L0_ffn_in['sw2'], 'L0_ffn_sb2': _L0_ffn_in['sb2'], 'L0_ffn_sw3': _L0_ffn_in['sw3'], 'L0_ffn_sb3': _L0_ffn_in['sb3'], 'L0_ffn_s_ln_g': _L0_ffn_in['s_ln_g'], 'L0_ffn_s_ln_b': _L0_ffn_in['s_ln_b'], 'L0_ffn_sg_w': _L0_ffn_in['sg_w'], 'L0_ffn_sg_b': _L0_ffn_in['sg_b'], 'L0_ffn_eg_w': _L0_ffn_in['eg_w'], 'L0_ffn_eg_b': _L0_ffn_in['eg_b'], 'L0_ffn_exp_bias': _L0_ffn_in['exp_bias'], 'L0_ffn_ew1': _L0_ffn_in['ew1'], 'L0_ffn_eb1': _L0_ffn_in['eb1'], 'L0_ffn_ew2': _L0_ffn_in['ew2'], 'L0_ffn_eb2': _L0_ffn_in['eb2'], 'L0_ffn_ew3': _L0_ffn_in['ew3'], 'L0_ffn_eb3': _L0_ffn_in['eb3'], 'L0_ffn_sel_ln_g': _L0_ffn_in['sel_ln_g'], 'L0_ffn_sel_ln_b': _L0_ffn_in['sel_ln_b']}

def reference(x, ctx_1024, L0_xattn_Wq, L0_xattn_Wk, L0_xattn_Wv, L0_xattn_Wcq, L0_xattn_Wck, L0_xattn_Wcv, L0_xattn_gamma, L0_xattn_beta, L0_xattn_W1, L0_xattn_b1, L0_attn_W_attn, L0_attn_W_proj, L0_ffn_index_b, L0_ffn_index_t, L0_ffn_sw1, L0_ffn_sb1, L0_ffn_sw2, L0_ffn_sb2, L0_ffn_sw3, L0_ffn_sb3, L0_ffn_s_ln_g, L0_ffn_s_ln_b, L0_ffn_sg_w, L0_ffn_sg_b, L0_ffn_eg_w, L0_ffn_eg_b, L0_ffn_exp_bias, L0_ffn_ew1, L0_ffn_eb1, L0_ffn_ew2, L0_ffn_eb2, L0_ffn_ew3, L0_ffn_eb3, L0_ffn_sel_ln_g, L0_ffn_sel_ln_b):
    import jax
    import jax.numpy as jnp

    def _L0_xattn_ref(inputs, context, Wq, Wk, Wv, Wcq, Wck, Wcv, gamma, beta, W1, b1):
        import jax, jax.numpy as jnp
        import numpy as np
        B, S, E = (8, 1024, 512)
        EPS = 0.001

        def _layer_norm(x, gamma, beta):
            mu = jnp.mean(x, axis=-1, keepdims=True)
            var = jnp.mean(jnp.square(x - mu), axis=-1, keepdims=True)
            return gamma * (x - mu) * jax.lax.rsqrt(var + EPS) + beta

        def _attention(q_in, k_in, v_in, WQ, WK, WV, causal):
            Q = jnp.einsum('bse,ed->bsd', q_in, WQ)
            K = jnp.einsum('bse,ed->bsd', k_in, WK)
            V = jnp.einsum('bse,ed->bsd', v_in, WV)
            d = K.shape[-1]
            scores = jnp.einsum('bqd,bkd->bqk', Q, K) / jnp.sqrt(jnp.float32(d))
            if causal:
                qlen, klen = (scores.shape[-2], scores.shape[-1])
                mask = jnp.triu(jnp.ones((qlen, klen), bool), k=1)
                scores = jnp.where(mask[None], -jnp.inf, scores)
            p = jax.nn.softmax(scores, axis=-1)
            return jnp.einsum('bqk,bkd->bqd', p, V)
        a = _attention(inputs, inputs, inputs, Wq, Wk, Wv, causal=True) + inputs
        h = _layer_norm(a, gamma, beta)
        c = _attention(h, context, context, Wcq, Wck, Wcv, causal=False) + h
        h = _layer_norm(c, gamma, beta)
        f = jax.nn.relu(jnp.einsum('bse,ed->bsd', h, W1) + b1)
        out = _layer_norm(f + h, gamma, beta)
        return jax.nn.relu(out)

    def _L0_attn_ref(x, W_attn, W_proj):
        import jax, jax.numpy as jnp
        import numpy as np
        import math
        N_HEAD = 16
        HEAD_QKV = 512
        WM_DECAY_LENGTH = 1024
        WM_DECAY_RATE = 1.0
        WM_ECHOIC = 16

        def decay_weight_matrix(n):
            dl = WM_DECAY_LENGTH - WM_ECHOIC + 1
            nums = jnp.linspace(0.0, 1.0, dl)
            decay_values = 1.0 - jnp.power(nums, 1.0 / (np.e * WM_DECAY_RATE))
            decay_values = jnp.concatenate([jnp.ones(WM_ECHOIC - 1), decay_values])
            decay_values = decay_values[:n]
            idx = jnp.arange(n)[:, None] - jnp.arange(n)[None, :]
            mat = decay_values[jnp.clip(idx, 0, n - 1)]
            return jnp.tril(mat).astype(jnp.float32)
        B, T, C = x.shape
        hd = HEAD_QKV // N_HEAD
        qkv = x @ W_attn
        q, k, v = jnp.split(qkv, 3, axis=-1)
        q = q.reshape(B, T, N_HEAD, hd).transpose(0, 2, 1, 3)
        k = k.reshape(B, T, N_HEAD, hd).transpose(0, 2, 1, 3)
        v = v.reshape(B, T, N_HEAD, hd).transpose(0, 2, 1, 3)
        att = jnp.einsum('bhqd,bhkd->bhqk', q, k) * (1.0 / math.sqrt(hd))
        causal = jnp.tril(jnp.ones((T, T), dtype=bool))
        att = jnp.where(causal, att, -jnp.inf)
        att = jax.nn.softmax(att, axis=-1)
        att = att * decay_weight_matrix(T)
        y = jnp.einsum('bhqk,bhkd->bhqd', att, v)
        y = y.transpose(0, 2, 1, 3).reshape(B, T, HEAD_QKV)
        return y @ W_proj

    def _L0_ffn_ref(x, index_b, index_t, sw1, sb1, sw2, sb2, sw3, sb3, s_ln_g, s_ln_b, sg_w, sg_b, eg_w, eg_b, exp_bias, ew1, eb1, ew2, eb2, ew3, eb3, sel_ln_g, sel_ln_b):
        import jax, jax.numpy as jnp
        import numpy as np
        EPS = 1e-05

        def _ln(x, g, b):
            mu = jnp.mean(x, axis=-1, keepdims=True)
            var = jnp.mean(jnp.square(x - mu), axis=-1, keepdims=True)
            return (x - mu) * jax.lax.rsqrt(var + EPS) * g + b

        def _forward(x, index_b, index_t, sw1, sb1, sw2, sb2, sw3, sb3, s_ln_g, s_ln_b, sg_w, sg_b, eg_w, eg_b, exp_bias, ew1, eb1, ew2, eb2, ew3, eb3, sel_ln_g, sel_ln_b):
            x1 = jnp.einsum('btd,hd->bth', x, sw1) + sb1
            x2 = jnp.einsum('btd,hd->bth', x, sw2) + sb2
            sh = _ln(jax.nn.silu(x1) * x2, s_ln_g, s_ln_b)
            shared_out = jnp.einsum('bth,dh->btd', sh, sw3) + sb3
            x_moe = x[index_b, index_t]
            shared_scores = jax.nn.sigmoid(x_moe @ sg_w.T + sg_b)
            expert_scores = jax.nn.sigmoid(x_moe @ eg_w.T + eg_b)
            top1_idx = jnp.argmax(expert_scores + exp_bias, axis=-1)
            top1_score = jnp.take_along_axis(expert_scores, top1_idx[:, None], axis=-1)
            weights = jax.nn.softmax(jnp.concatenate([shared_scores, top1_score], axis=-1), axis=-1)
            shared_w, expert_w = (weights[:, 0], weights[:, 1])
            shared_moe_out = shared_out[index_b, index_t] * shared_w[:, None]
            h1 = jnp.einsum('md,ehd->meh', x_moe, ew1) + eb1
            h2 = jnp.einsum('md,ehd->meh', x_moe, ew2) + eb2
            z = _ln(jax.nn.silu(h1) * h2, sel_ln_g, sel_ln_b)
            out_all = jnp.einsum('meh,edh->med', z, ew3) + eb3
            expert_out = jnp.take_along_axis(out_all, top1_idx[:, None, None], axis=1)[:, 0]
            expert_moe_out = expert_out * expert_w[:, None]
            final_out = shared_out.at[index_b, index_t].set(shared_moe_out + expert_moe_out)
            return final_out
        return _forward(x, index_b, index_t, sw1, sb1, sw2, sb2, sw3, sb3, s_ln_g, s_ln_b, sg_w, sg_b, eg_w, eg_b, exp_bias, ew1, eb1, ew2, eb2, ew3, eb3, sel_ln_g, sel_ln_b)
    x = x + _L0_xattn_ref(_layernorm(x, axis=-1), ctx_1024, L0_xattn_Wq, L0_xattn_Wk, L0_xattn_Wv, L0_xattn_Wcq, L0_xattn_Wck, L0_xattn_Wcv, L0_xattn_gamma, L0_xattn_beta, L0_xattn_W1, L0_xattn_b1)
    x = x + _L0_attn_ref(_layernorm(x, axis=-1), L0_attn_W_attn, L0_attn_W_proj)
    x = x + _L0_ffn_ref(_layernorm(x, axis=-1), L0_ffn_index_b, L0_ffn_index_t, L0_ffn_sw1, L0_ffn_sb1, L0_ffn_sw2, L0_ffn_sb2, L0_ffn_sw3, L0_ffn_sb3, L0_ffn_s_ln_g, L0_ffn_s_ln_b, L0_ffn_sg_w, L0_ffn_sg_b, L0_ffn_eg_w, L0_ffn_eg_b, L0_ffn_exp_bias, L0_ffn_ew1, L0_ffn_eb1, L0_ffn_ew2, L0_ffn_eb2, L0_ffn_ew3, L0_ffn_eb3, L0_ffn_sel_ln_g, L0_ffn_sel_ln_b)
    return x

_drawn_inputs = setup_inputs


def setup_inputs(seed=0):
    import zlib

    import numpy as np

    out = dict(_drawn_inputs(seed))
    spreads = {'L0_xattn_gamma': (1.0, 0.2),
     'L0_xattn_beta': (0.0, 0.1),
     'L0_xattn_b1': (0.0, 0.272),
     'L0_ffn_sb1': (0.0, 0.1),
     'L0_ffn_sb2': (0.0, 0.1),
     'L0_ffn_sb3': (0.0, 0.1),
     'L0_ffn_s_ln_g': (1.0, 0.2),
     'L0_ffn_s_ln_b': (0.0, 0.419),
     'L0_ffn_eg_b': (0.0, 2.0),
     'L0_ffn_exp_bias': (0.0, 0.65),
     'L0_ffn_eb1': (0.0, 2.0),
     'L0_ffn_eb2': (0.0, 2.0),
     'L0_ffn_eb3': (0.0, 2.0),
     'L0_ffn_sel_ln_g': (1.0, 0.6),
     'L0_ffn_sel_ln_b': (0.0, 0.8)}
    factors = {'L0_ffn_sg_w': 24.388,
     'L0_ffn_eg_w': 6.792,
     'L0_ffn_ew1': 6.198,
     'L0_ffn_ew2': 6.116,
     'L0_ffn_ew3': 5.899}
    for name, (base, spread) in spreads.items():
        noise = np.random.default_rng([zlib.crc32(name.encode()), seed]).standard_normal(out[name].shape)
        drawn = base * np.exp(spread * noise) if base else spread * noise
        out[name] = jnp.asarray(drawn.astype(out[name].dtype))
    for name, factor in factors.items():
        out[name] = (out[name] * factor).astype(out[name].dtype)
    return out
```

```python
from contextlib import ExitStack

import numpy as np

import concourse.bass as bass
from concourse import mybir

F32 = mybir.dt.float32
BF16 = mybir.dt.bfloat16
I32 = mybir.dt.int32
ALU = mybir.AluOpType
ACT = mybir.ActivationFunctionType
AX = mybir.AxisListType

P = 128
B, T, D = 128, 32, 512
S = 257
G = P // T
TILES = B // G
PAIRS = TILES // 2
C = D // P
SC = (S - 1) // P
NH = 16
HD = D // NH
HPC = P // HD
H = 256
HC = H // P
NE = 8
M = 1024
MC = M // P
NEG = -1.0e30
XSCALE = float(D) ** -0.5
HSCALE = float(HD) ** -0.5
SLOTS = (0, 1)


def build(nc, a):
    ctx = ExitStack()
    with ctx:
        def sem(name):
            return ctx.enter_context(nc.semaphore(name))

        def pair(name):
            return [sem(f"{name}{s}") for s in SLOTS]

        def sb(stack, name, shape, dt=F32):
            return stack.enter_context(nc.sbuf_tensor(name, shape, dt))

        def two(stack, name, shape, dt=F32):
            return [sb(stack, f"{name}{s}", shape, dt) for s in SLOTS]

        ps_t = [ctx.enter_context(nc.psum_tensor(f"ps_t{s}", [P, 512], F32)) for s in SLOTS]
        ps_a = [ctx.enter_context(nc.psum_tensor(f"ps_a{s}", [P, 512], F32)) for s in SLOTS]
        ps_b = [ctx.enter_context(nc.psum_tensor(f"ps_b{s}", [P, 512], F32)) for s in SLOTS]
        ps_c = [ctx.enter_context(nc.psum_tensor(f"ps_c{s}", [P, 512], F32)) for s in SLOTS]

        ident = sb(ctx, "ident", [P, P])
        sel = sb(ctx, "sel", [P, TILES])
        flags = sb(ctx, "flags", [1, TILES], I32)
        mhalf = sb(ctx, "mhalf", [P, 1])
        stats = two(ctx, "stats", [P, 6])
        mv = two(ctx, "mv", [P, 2])
        var = two(ctx, "var", [P, 1])
        rstd = two(ctx, "rstd", [P, 1])

        weights_loaded = sem("weights_loaded")
        stats_seen = sem("stats_seen")
        consts_ready = sem("consts_ready")
        x2_stored = pair("x2_stored")
        at = ExitStack()
        with at:
            wqk = sb(at, "wqk", [P, C, D])
            wcqk = sb(at, "wcqk", [P, C, D])
            wv = sb(at, "wv", [P, C, D])
            wcv = sb(at, "wcv", [P, C, D])
            w1 = sb(at, "w1", [P, C, D])
            wattn = sb(at, "wattn", [P, C, 3 * D])
            wproj = sb(at, "wproj", [P, C, D])
            gamma = sb(at, "gamma", [P, D])
            beta = sb(at, "beta", [P, D])
            b1 = sb(at, "b1", [P, D])
            mask_self = sb(at, "mask_self", [P, P])
            mask_head = sb(at, "mask_head", [P, T])
            decay = sb(at, "decay", [P, T])
            mask_entry = sb(at, "mask_entry", [P, G])
            kbd = sb(at, "kbd", [P, C, G, HPC, T])
            pbd = sb(at, "pbd", [P, NH, G, T])

            qk_loaded = [sem("wqk_loaded"), sem("wcqk_loaded")]
            idx_loaded, idx_step = sem("idx_loaded"), sem("idx_step")
            onehots_ready, sel_counted, sel_ready = sem("onehots_ready"), sem("sel_counted"), sem("sel_ready")
            flags_counted, product_done, product_copied = sem("flags_counted"), sem("product_done"), sem("product_copied")
            with ExitStack() as st:
                wq_t = [sb(st, f"wq_t{n}", [P, C, D]) for n in range(2)]
                wk_t = [sb(st, f"wk_t{n}", [P, C, D]) for n in range(2)]
                entry_of = sb(st, "entry_of", [P, B])
                iota_t = sb(st, "iota_t", [P, T])
                idx_i = sb(st, "idx_i", [P, 2, MC], I32)
                idx = sb(st, "idx", [P, 2, MC])
                idx_neg = sb(st, "idx_neg", [P, 2, MC])
                hot_b = sb(st, "hot_b", [P, MC, B], BF16)
                hot_t = sb(st, "hot_t", [P, MC, T], BF16)
                ones = sb(st, "ones", [P, 1])

                block = st.enter_context(nc.Block())

                @block.sync
                def _(sp):
                    sp.dma_start(wq_t[0][:], a["wq_t"]).then_inc(qk_loaded[0], 16)
                    sp.dma_start(wk_t[0][:], a["wk_t"]).then_inc(qk_loaded[0], 16)
                    sp.dma_start(idx_i[:, 0, :], a["index_b"]).then_inc(idx_loaded, 16)
                    sp.dma_start(idx_i[:, 1, :], a["index_t"]).then_inc(idx_loaded, 16)
                    sp.dma_start(entry_of[:], a["entry_of"].partition_broadcast(P)).then_inc(idx_loaded, 16)
                    sp.dma_start(iota_t[:], a["iota_t"].partition_broadcast(P)).then_inc(idx_loaded, 16)
                    sp.dma_start(wq_t[1][:], a["wcq_t"]).then_inc(qk_loaded[1], 16)
                    sp.dma_start(wk_t[1][:], a["wck_t"]).then_inc(qk_loaded[1], 16)
                    for name, dst in (("ident", ident), ("wv", wv), ("wcv", wcv), ("w1", w1),
                                      ("wattn", wattn), ("wproj", wproj), ("mask_self", mask_self),
                                      ("mask_head", mask_head), ("decay", decay), ("mask_entry", mask_entry)):
                        sp.dma_start(dst[:], a[name]).then_inc(weights_loaded, 16)
                    for name, dst in (("gamma", gamma), ("beta", beta), ("b1", b1)):
                        sp.dma_start(dst[:], a[name].partition_broadcast(P)).then_inc(weights_loaded, 16)
                    sp.wait_ge(weights_loaded, 16 * 13)

                @block.gpsimd
                def _(pool):
                    nc.gpsimd.memset(kbd[:], 0.0).then_inc(consts_ready, 1)
                    nc.gpsimd.memset(pbd[:], 0.0).then_inc(consts_ready, 1)
                    nc.gpsimd.memset(mhalf[:], -0.5).then_inc(consts_ready, 1)
                    pool.wait_ge(consts_ready, 4)

                @block.vector
                def _(dve):
                    steps = [0]

                    def step(ins):
                        steps[0] += 1
                        ins.then_inc(idx_step, 1)
                        dve.wait_ge(idx_step, steps[0])

                    nc.vector.memset(ones[:], 1.0).then_inc(consts_ready, 1)
                    dve.wait_ge(idx_loaded, 64)
                    step(nc.vector.tensor_copy(idx[:], idx_i[:]))
                    for k, size in ((0, B), (1, T)):
                        step(nc.vector.tensor_scalar(idx_neg[:, k, :], idx[:, k, :], 0.0, float(size), ALU.is_lt, ALU.mult))
                    step(nc.vector.tensor_tensor(idx[:], idx[:], idx_neg[:], ALU.add))
                    for k, hot, values, size in ((0, hot_b, entry_of, B), (1, hot_t, iota_t, T)):
                        nc.vector.tensor_tensor(hot[:], values[:].unsqueeze(1).to_broadcast([P, MC, size]),
                                                idx[:, k, :].unsqueeze(2).to_broadcast([P, MC, size]),
                                                ALU.is_equal).then_inc(onehots_ready, 1)
                    dve.wait_ge(sel_counted, 1)
                    nc.vector.tensor_scalar(sel[:], ps_b[0][:, 0:TILES], 0.0, None, ALU.is_gt).then_inc(sel_ready, 1)
                    dve.wait_ge(flags_counted, 1)
                    nc.vector.tensor_copy(flags[:], ps_b[1][0:1, 0:TILES]).then_inc(idx_step, 1)

                @block.scalar
                def _(act):
                    for n, w in ((0, wqk), (1, wcqk)):
                        for c in range(C):
                            act.wait_ge(product_done, n * C + c + 1)
                            nc.scalar.copy(w[:, c, :], (ps_a, ps_c)[c % 2][c // 2][:]).then_inc(product_copied, 1)

                @block.tensor
                def _(pe):
                    def product(n):
                        pe.wait_ge(qk_loaded[n], 32)
                        for c in range(C):
                            if n:
                                pe.wait_ge(product_copied, c + 1)
                            for d in range(C):
                                mm = nc.tensor.matmul((ps_a, ps_c)[c % 2][c // 2][:], wq_t[n][:, d, c * P:(c + 1) * P],
                                                      wk_t[n][:, d, :], start=(d == 0), stop=(d == C - 1))
                            mm.then_inc(product_done, 1)

                    product(0)
                    pe.wait_ge(onehots_ready, 2)
                    for g in range(G):
                        for c in range(MC):
                            mm = nc.tensor.matmul(ps_b[0][T * g:T * (g + 1), 0:TILES], hot_t[:, c, :], hot_b[:, c, g::G],
                                                  start=(c == 0), stop=(c == MC - 1), skip_group_check=True)
                    mm.then_inc(sel_counted, 1)
                    product(1)
                    pe.wait_ge(sel_ready, 1)
                    pe.wait_ge(consts_ready, 4)
                    nc.tensor.matmul(ps_b[1][0:1, 0:TILES], ones[:], sel[:], start=True, stop=True).then_inc(flags_counted, 1)


            ctx_t = two(at, "ctx_t", [P, C, G, S])
            ctx_n = two(at, "ctx_n", [P, G, SC, D])
            ctx_last = two(at, "ctx_last", [G, D])
            x_in = two(at, "x_in", [P, D])
            rows1 = two(at, "rows1", [P, D])
            rows2 = two(at, "rows2", [P, D])
            rows3 = two(at, "rows3", [P, D])
            act_t = two(at, "act_t", [P, C, P])
            q_t = two(at, "q_t", [P, C, P])
            v_n = two(at, "v_n", [P, D])
            p_n = two(at, "p_n", [P, S + G])
            p_t = two(at, "p_t", [P, SC * P + P])
            top = two(at, "top", [P, NH])
            ntop = two(at, "ntop", [P, 1])
            total = two(at, "total", [P, NH])
            inv = two(at, "inv", [P, NH])

            x_loaded, ctx_t_loaded, ctx_n_loaded = pair("x_loaded"), pair("ctx_t_loaded"), pair("ctx_n_loaded")
            x_used = pair("x_used")
            var_ready, rstd_ready = pair("var_ready"), pair("rstd_ready")
            rows_ready = pair("rows_ready")
            turned = pair("turned")
            act_t_ready = pair("act_t_ready")
            q_done, q_ready = pair("q_done"), pair("q_ready")
            v_done, v_ready = pair("v_done"), pair("v_ready")
            scored = pair("scored")
            ntop_ready = pair("ntop_ready")
            p_ready = pair("p_ready")
            p4_ready, inv_ready = pair("p4_ready"), pair("inv_ready")
            p_turned, p_t_ready = pair("p_turned"), pair("p_t_ready")
            mixed = pair("mixed")
            f_done = pair("f_done")
            k_done, k_ready = pair("k_done"), pair("k_ready")
            decayed, pbd_ready, y_done, y_ready = pair("decayed"), pair("pbd_ready"), pair("y_done"), pair("y_ready")
            proj_done, x2_ready = pair("proj_done"), pair("x2_ready")
            heads_shifted = pair("heads_shifted")
            dve_step = sem("dve_step")

            block = at.enter_context(nc.Block())

            @block.sync
            def _(sp):
                for s in SLOTS:
                    sp.sem_inc(x2_stored[s], 16)

                def load(i, s, first):
                    if not first:
                        sp.wait_ge(scored[s], 3 * i + 2)
                    sp.dma_start(ctx_t[s][:], a["ctx_t"][bass.ds(2 * i + s, 1)].rearrange("a p c g k -> (a p) c g k")
                                 ).then_inc(ctx_t_loaded[s], 16)
                    if not first:
                        sp.wait_ge(v_done[s], 3 * i - 1)
                    sp.dma_start(ctx_n[s][:], a["ctx_n"][bass.ds(2 * i + s, 1)].rearrange("a p g c d -> (a p) g c d")
                                 ).then_inc(ctx_n_loaded[s], 16)
                    sp.dma_start(ctx_last[s][:], a["ctx_last"][bass.ds(2 * i + s, 1)].rearrange("a g d -> (a g) d")
                                 ).then_inc(ctx_n_loaded[s], 16)

                def load_x(i, s, first):
                    if not first:
                        sp.wait_ge(x_used[s], i)
                    sp.dma_start(x_in[s][:], a["x"][bass.ds(2 * i + s, 1)].rearrange("a p d -> (a p) d")
                                 ).then_inc(x_loaded[s], 16)

                def store(i, s):
                    sp.wait_ge(x2_ready[s], i + 1)
                    sp.dma_start(a["x2"][bass.ds(2 * i + s, 1)].rearrange("a p d -> (a p) d"), rows3[s][:]
                                 ).then_inc(x2_stored[s], 16)

                for s in SLOTS:
                    load_x(0, s, True)
                for s in SLOTS:
                    load(0, s, True)
                with sp.Fori(1, PAIRS) as i:
                    for s in SLOTS:
                        load(i, s, False)
                    for s in SLOTS:
                        load_x(i, s, False)
                    for s in SLOTS:
                        store(i - 1, s)
                for s in SLOTS:
                    store(PAIRS - 1, s)
                for s in SLOTS:
                    sp.wait_ge(x2_stored[s], 16 * PAIRS + 16)

            @block.gpsimd
            def _(pool):
                with pool.Fori(0, PAIRS) as i:
                    def inverse_std(s, n):
                        pool.wait_ge(var_ready[s], 5 * i + n)
                        nc.gpsimd.tensor_tensor(rstd[s][:], var[s][:], mhalf[:], ALU.pow).then_inc(rstd_ready[s], 1)

                    for n in (1, 2, 3):
                        for s in SLOTS:
                            inverse_std(s, n)
                    for s in SLOTS:
                        inverse_std(s, 4)
                        inverse_std(s, 5)
                    for s in SLOTS:
                        pool.wait_ge(p_ready[s], 3 * i + 3)
                        nc.gpsimd.tensor_tensor(rows3[s][:].rearrange("p (h k) -> p h k", k=T),
                                                rows1[s][:].rearrange("p (h k) -> p h k", k=T),
                                                decay[:].unsqueeze(1).to_broadcast([P, NH, T]), ALU.mult
                                                ).then_inc(decayed[s], 1)

            @block.scalar
            def _(act):
                with act.Fori(0, PAIRS) as i:
                    def copy_turned(n):
                        for s in SLOTS:
                            act.wait_ge(turned[s], 5 * i + n)
                            nc.scalar.copy(act_t[s][:].rearrange("p c r -> p (c r)"), ps_t[s][:]).then_inc(act_t_ready[s], 1)

                    copy_turned(1)
                    for s in SLOTS:
                        act.wait_ge(v_done[s], 3 * i + 1)
                        nc.scalar.copy(v_n[s][:], ps_b[s][:]).then_inc(v_ready[s], 1)
                    for s in SLOTS:
                        act.wait_ge(ntop_ready[s], 2 * i + 1)
                        nc.scalar.activation(p_n[s][:, 0:P], rows3[s][:, 0:P], ACT.Exp, bias=ntop[s][:], scale=XSCALE,
                                             accum_out=total[s][:, 0:1]).then_inc(p_ready[s], 1)
                    for s in SLOTS:
                        act.wait_ge(p_turned[s], 2 * i + 1)
                        nc.scalar.copy(p_t[s][:, 0:P], ps_t[s][:, 0:P]).then_inc(p_t_ready[s], 1)
                    copy_turned(2)
                    for s in SLOTS:
                        act.wait_ge(q_done[s], 3 * i + 2)
                        nc.scalar.copy(q_t[s][:].rearrange("p c r -> p (c r)"), ps_b[s][:]).then_inc(q_ready[s], 1)
                    for s in SLOTS:
                        act.wait_ge(ntop_ready[s], 2 * i + 2)
                        nc.scalar.activation(p_n[s][:, 0:S], ps_c[s][:, 0:S], ACT.Exp, bias=ntop[s][:], scale=XSCALE,
                                             accum_out=total[s][:, 0:1]).then_inc(p_ready[s], 1)
                    for s in SLOTS:
                        act.wait_ge(p_turned[s], 2 * i + 2)
                        nc.scalar.copy(p_t[s][:, 0:SC * P], ps_t[s][:, 0:SC * P])
                        nc.scalar.copy(p_t[s][0:G, SC * P:], ps_t[s][0:G, SC * P:SC * P + P]).then_inc(p_t_ready[s], 1)
                    for s in SLOTS:
                        act.wait_ge(v_done[s], 3 * i + 2)
                        act.wait_ge(inv_ready[s], i + 1)
                        nc.scalar.activation(v_n[s][:], ps_a[s][:], ACT.Copy, scale=inv[s][:, 0:1]).then_inc(v_ready[s], 1)
                    copy_turned(3)
                    copy_turned(4)
                    copy_turned(5)
                    for s in SLOTS:
                        act.wait_ge(q_done[s], 3 * i + 3)
                        nc.scalar.copy(q_t[s][:].rearrange("p c r -> p (c r)"), ps_a[s][:]).then_inc(q_ready[s], 1)
                        act.wait_ge(k_done[s], i + 1)
                        act.wait_ge(scored[1 - s], 3 * i + 3 + 3 * s)
                        for h in (0, 1):
                            nc.scalar.copy(kbd[HD * h:HD * (h + 1), :, :, h, :],
                                           ps_b[s][HD * h:HD * (h + 1), :].rearrange("p (c g k) -> p c g k", c=C, g=G)
                                           ).then_inc(k_ready[s], 1)
                        act.wait_ge(v_done[s], 3 * i + 3)
                        nc.scalar.copy(v_n[s][:], ps_c[s][:]).then_inc(v_ready[s], 1)
                    for s in SLOTS:
                        act.wait_ge(heads_shifted[s], i + 1)
                        nc.scalar.activation(rows1[s][:], rows3[s][:], ACT.Exp, scale=HSCALE).then_inc(p_ready[s], 1)
                    for s in SLOTS:
                        act.wait_ge(y_done[s], i + 2)
                        nc.scalar.copy(act_t[s][:].rearrange("p c r -> p (c r)"), ps_a[s][:]).then_inc(y_ready[s], 1)

            def bcast_heads(ap):
                return ap.unsqueeze(2).to_broadcast([P, NH, T])

            DVE_STEPS = 2 * 27

            @block.vector
            def _(dve):
                with dve.Fori(0, PAIRS) as i:
                    count = [0]

                    def step(ins):
                        count[0] += 1
                        ins.then_inc(dve_step, 1)
                        dve.wait_ge(dve_step, DVE_STEPS * i + count[0])

                    def moments(s, n, rows, eps):
                        step(nc.vector.bn_stats(stats[s][:], rows))
                        dve.sem_inc(stats_seen, 1)
                        step(nc.vector.bn_aggr(mv[s][:], stats[s][:]))
                        nc.vector.tensor_scalar(var[s][:], mv[s][:, 1:2], eps, None, ALU.add).then_inc(var_ready[s], 1)
                        dve.wait_ge(rstd_ready[s], 5 * i + n)

                    def plain_norm(s, out, rows):
                        return nc.vector.tensor_scalar(out, rows, mv[s][:, 0:1], rstd[s][:], ALU.subtract, ALU.mult)

                    def affine_norm(s, out, rows):
                        step(nc.vector.scalar_tensor_tensor(out, rows, mv[s][:, 0:1], gamma[:], ALU.subtract, ALU.mult))
                        return nc.vector.scalar_tensor_tensor(out, out, rstd[s][:], beta[:], ALU.mult, ALU.add)

                    for s in SLOTS:
                        dve.wait_ge(x_loaded[s], 16 * i + 16)
                        moments(s, 1, x_in[s][:], 1e-5)
                        plain_norm(s, rows1[s][:], x_in[s][:]).then_inc(rows_ready[s], 1)
                    for s in SLOTS:
                        dve.wait_ge(q_done[s], 3 * i + 1)
                        nc.vector.tensor_copy(q_t[s][:].rearrange("p c r -> p (c r)"), ps_a[s][:]).then_inc(q_ready[s], 1)
                    for s in SLOTS:
                        dve.wait_ge(scored[s], 3 * i + 4)
                        dve.wait_ge(x2_stored[s], 16 * i + 16)
                        step(nc.vector.tensor_tensor(rows3[s][:, 0:P], ps_c[s][:, 0:P], mask_self[:], ALU.add))
                        step(nc.vector.reduce_max(top[s][:, 0:1], rows3[s][:, 0:P], AX.X))
                        nc.vector.tensor_scalar(ntop[s][:], top[s][:, 0:1], -XSCALE, None, ALU.mult).then_inc(ntop_ready[s], 1)
                    for s in SLOTS:
                        dve.wait_ge(p_ready[s], 3 * i + 1)
                        step(nc.vector.reciprocal(inv[s][:, 0:1], total[s][:, 0:1]))
                        dve.wait_ge(mixed[s], 2 * i + 1)
                        step(nc.vector.scalar_tensor_tensor(rows2[s][:], ps_a[s][:], inv[s][:, 0:1], rows1[s][:],
                                                            ALU.mult, ALU.add))
                        moments(s, 2, rows2[s][:], 1e-3)
                        affine_norm(s, rows2[s][:], rows2[s][:]).then_inc(rows_ready[s], 1)
                    for s in SLOTS:
                        dve.wait_ge(scored[s], 3 * i + 5)
                        step(nc.vector.reduce_max(top[s][:, 0:1], ps_c[s][:, 0:S], AX.X))
                        nc.vector.tensor_scalar(ntop[s][:], top[s][:, 0:1], -XSCALE, None, ALU.mult).then_inc(ntop_ready[s], 1)
                    for s in SLOTS:
                        dve.wait_ge(p_ready[s], 3 * i + 2)
                        nc.vector.tensor_scalar(p_n[s][:, S:S + G], mask_entry[:], p_n[s][:, S - 1:S], None, ALU.mult
                                                ).then_inc(p4_ready[s], 1)
                        nc.vector.reciprocal(inv[s][:, 0:1], total[s][:, 0:1]).then_inc(inv_ready[s], 1)
                    for s in SLOTS:
                        dve.wait_ge(mixed[s], 2 * i + 2)
                        step(nc.vector.tensor_tensor(rows3[s][:], ps_b[s][:], rows2[s][:], ALU.add))
                        moments(s, 3, rows3[s][:], 1e-3)
                        affine_norm(s, rows1[s][:], rows3[s][:]).then_inc(rows_ready[s], 1)
                    for s in SLOTS:
                        dve.wait_ge(f_done[s], i + 1)
                        step(nc.vector.tensor_tensor(rows3[s][:], ps_c[s][:], b1[:], ALU.add))
                        step(nc.vector.scalar_tensor_tensor(rows3[s][:], rows3[s][:], 0.0, rows1[s][:], ALU.max, ALU.add))
                        moments(s, 4, rows3[s][:], 1e-3)
                        step(affine_norm(s, rows2[s][:], rows3[s][:]))
                        nc.vector.scalar_tensor_tensor(rows2[s][:], rows2[s][:], 0.0, x_in[s][:], ALU.max, ALU.add
                                                       ).then_inc(x_used[s], 1)
                        dve.wait_ge(x_used[s], i + 1)
                        moments(s, 5, rows2[s][:], 1e-5)
                        plain_norm(s, rows1[s][:], rows2[s][:]).then_inc(rows_ready[s], 1)
                    for s in SLOTS:
                        dve.wait_ge(k_done[s], i + 1)
                        dve.wait_ge(scored[1 - s], 3 * i + 3 + 3 * s)
                        for h in (2, 3):
                            nc.vector.tensor_copy(kbd[HD * h:HD * (h + 1), :, :, h, :],
                                                  ps_b[s][HD * h:HD * (h + 1), :].rearrange("p (c g k) -> p c g k", c=C, g=G)
                                                  ).then_inc(k_ready[s], 1)
                    for s in SLOTS:
                        dve.wait_ge(scored[s], 3 * i + 6)
                        sc = rows3[s][:].rearrange("p (h k) -> p h k", k=T)
                        step(nc.vector.tensor_tensor(sc, ps_t[s][:].rearrange("p (h k) -> p h k", k=T),
                                                     mask_head[:].unsqueeze(1).to_broadcast([P, NH, T]), ALU.add))
                        step(nc.vector.tensor_reduce(top[s][:], sc, AX.X, ALU.max))
                        nc.vector.tensor_tensor(sc, sc, bcast_heads(top[s][:]), ALU.subtract).then_inc(heads_shifted[s], 1)
                    for s in SLOTS:
                        dve.wait_ge(p_ready[s], 3 * i + 3)
                        step(nc.vector.tensor_reduce(total[s][:], rows1[s][:].rearrange("p (h k) -> p h k", k=T), AX.X,
                                                     ALU.add))
                        step(nc.vector.reciprocal(inv[s][:], total[s][:]))
                        dve.wait_ge(decayed[s], i + 1)
                        step(nc.vector.tensor_tensor(rows1[s][:].rearrange("p (h k) -> p h k", k=T),
                                                     rows3[s][:].rearrange("p (h k) -> p h k", k=T),
                                                     bcast_heads(inv[s][:]), ALU.mult))
                        if s:
                            dve.wait_ge(y_done[0], i + 2)
                        else:
                            dve.wait_ge(y_done[1], i + 1)
                        for g in range(G):
                            rows = slice(T * g, T * (g + 1))
                            nc.vector.transpose(pbd[rows, :, g, :], rows1[s][rows, :].rearrange("p (h k) -> p h k", k=T)
                                                ).then_inc(pbd_ready[s], 1)
                    for s in SLOTS:
                        dve.wait_ge(proj_done[s], i + 1)
                        nc.vector.tensor_tensor(rows3[s][:], ps_b[s][:], rows2[s][:], ALU.add).then_inc(x2_ready[s], 1)
                    assert count[0] == DVE_STEPS

            @block.tensor
            def _(pe):
                for s in SLOTS:
                    pe.sem_inc(scored[s], 3)
                    pe.sem_inc(y_done[s], 1)
                with pe.Fori(0, PAIRS) as i:
                    def turn(n, rows, ready, value):
                        for s in SLOTS:
                            pe.wait_ge(ready[s], value)
                            for c in range(C):
                                mm = nc.tensor.transpose(ps_t[s][:, c * P:(c + 1) * P], rows[s][:, c * P:(c + 1) * P],
                                                         ident[:])
                            mm.then_inc(turned[s], 1)

                    def product(s, out, w, lo=0):
                        for c in range(C):
                            mm = nc.tensor.matmul(out[s][:], act_t[s][:, c, :], w[:, c, lo:lo + D],
                                                  start=(c == 0), stop=(c == C - 1))
                        return mm

                    def product_t(s, out, w, lo=0):
                        for n in range(C):
                            for c in range(C):
                                mm = nc.tensor.matmul(out[s][:, n * P:(n + 1) * P], w[:, c, lo + n * P:lo + (n + 1) * P],
                                                      act_t[s][:, c, :], start=(c == 0), stop=(c == C - 1))
                        return mm

                    turn(1, rows1, rows_ready, 4 * i + 1)
                    for s in SLOTS:
                        pe.wait_ge(act_t_ready[s], 5 * i + 1)
                        product_t(s, ps_a, wqk).then_inc(q_done[s], 1)
                        product(s, ps_b, wv).then_inc(v_done[s], 1)
                    for s in SLOTS:
                        pe.wait_ge(q_ready[s], 3 * i + 1)
                        for c in range(C):
                            mm = nc.tensor.matmul(ps_c[s][:, 0:P], q_t[s][:, c, :], act_t[s][:, c, :],
                                                  start=(c == 0), stop=(c == C - 1))
                        mm.then_inc(scored[s], 1)
                    for s in SLOTS:
                        pe.wait_ge(p_ready[s], 3 * i + 1)
                        nc.tensor.transpose(ps_t[s][:, 0:P], p_n[s][:, 0:P], ident[:]).then_inc(p_turned[s], 1)
                    for s in SLOTS:
                        pe.wait_ge(p_t_ready[s], 2 * i + 1)
                        pe.wait_ge(v_ready[s], 3 * i + 1)
                        nc.tensor.matmul(ps_a[s][:], p_t[s][:, 0:P], v_n[s][:], start=True, stop=True).then_inc(mixed[s], 1)
                    turn(2, rows2, rows_ready, 4 * i + 2)
                    for s in SLOTS:
                        pe.wait_ge(act_t_ready[s], 5 * i + 2)
                        product_t(s, ps_b, wcqk).then_inc(q_done[s], 1)
                    for s in SLOTS:
                        pe.wait_ge(q_ready[s], 3 * i + 2)
                        pe.wait_ge(ctx_t_loaded[s], 16 * i + 16)
                        for c in range(C):
                            for g in range(G):
                                mm = nc.tensor.matmul(ps_c[s][T * g:T * (g + 1), 0:S], q_t[s][:, c, T * g:T * (g + 1)],
                                                      ctx_t[s][:, c, g, :], start=(c == 0), stop=(c == C - 1),
                                                      skip_group_check=True)
                        mm.then_inc(scored[s], 1)
                    for s in SLOTS:
                        pe.wait_ge(p_ready[s], 3 * i + 2)
                        for c in range(SC):
                            nc.tensor.transpose(ps_t[s][:, c * P:(c + 1) * P], p_n[s][:, c * P:(c + 1) * P], ident[:])
                        pe.wait_ge(p4_ready[s], i + 1)
                        nc.tensor.transpose(ps_t[s][0:G, SC * P:SC * P + P], p_n[s][:, S:S + G], ident[:]
                                            ).then_inc(p_turned[s], 1)
                    for s in SLOTS:
                        pe.wait_ge(p_t_ready[s], 2 * i + 2)
                        pe.wait_ge(ctx_n_loaded[s], 32 * i + 32)
                        nc.tensor.matmul(ps_a[s][:], p_t[s][0:G, SC * P:], ctx_last[s][:], start=True, stop=False,
                                         skip_group_check=True)
                        for c in range(SC):
                            for g in range(G):
                                mm = nc.tensor.matmul(ps_a[s][T * g:T * (g + 1), :],
                                                      p_t[s][:, c * P + T * g:c * P + T * (g + 1)], ctx_n[s][:, g, c, :],
                                                      start=False, stop=(c == SC - 1), skip_group_check=True)
                        mm.then_inc(v_done[s], 1)
                    turn(3, v_n, v_ready, 3 * i + 2)
                    for s in SLOTS:
                        pe.wait_ge(act_t_ready[s], 5 * i + 3)
                        product(s, ps_b, wcv).then_inc(mixed[s], 1)
                    turn(4, rows1, rows_ready, 4 * i + 3)
                    for s in SLOTS:
                        pe.wait_ge(act_t_ready[s], 5 * i + 4)
                        product(s, ps_c, w1).then_inc(f_done[s], 1)
                    turn(5, rows1, rows_ready, 4 * i + 4)
                    for s in SLOTS:
                        pe.wait_ge(act_t_ready[s], 5 * i + 5)
                        product_t(s, ps_b, wattn, D).then_inc(k_done[s], 1)
                        product_t(s, ps_a, wattn, 0).then_inc(q_done[s], 1)
                        product(s, ps_c, wattn, 2 * D).then_inc(v_done[s], 1)
                    for s in SLOTS:
                        pe.wait_ge(q_ready[s], 3 * i + 3)
                        pe.wait_ge(k_ready[s], 4 * i + 4)
                        for c in range(C):
                            for g in range(G):
                                mm = nc.tensor.matmul(ps_t[s][T * g:T * (g + 1), c * P:(c + 1) * P],
                                                      q_t[s][:, c, T * g:T * (g + 1)],
                                                      kbd[:, c, g, :, :].rearrange("p h k -> p (h k)"),
                                                      start=True, stop=True, skip_group_check=True)
                        mm.then_inc(scored[s], 1)
                    for s in SLOTS:
                        pe.wait_ge(pbd_ready[s], 4 * i + 4)
                        pe.wait_ge(v_ready[s], 3 * i + 3)
                        for c in range(C):
                            for h in range(HPC):
                                head = c * HPC + h
                                mm = nc.tensor.matmul(ps_a[s][HD * h:HD * (h + 1), c * P:(c + 1) * P],
                                                      v_n[s][:, HD * head:HD * (head + 1)],
                                                      pbd[:, head, :, :].rearrange("p g q -> p (g q)"),
                                                      start=True, stop=True, skip_group_check=True)
                        mm.then_inc(y_done[s], 1)
                    for s in SLOTS:
                        pe.wait_ge(y_ready[s], i + 1)
                        product(s, ps_b, wproj).then_inc(proj_done[s], 1)

        fs = ctx.enter_context(ExitStack())
        w12 = sb(fs, "w12", [P, C, 2 * H])
        w3 = sb(fs, "w3", [P, HC, D])
        ew12 = sb(fs, "ew12", [P, NE, C, 2 * H])
        ew3 = sb(fs, "ew3", [P, NE, HC, D])
        wg = sb(fs, "wg", [P, C, 1 + NE])
        b12 = sb(fs, "b12", [P, 2 * H])
        b3 = sb(fs, "b3", [P, D])
        ln_g = sb(fs, "ln_g", [P, H])
        ln_b = sb(fs, "ln_b", [P, H])
        sel_g = sb(fs, "sel_g", [P, H])
        sel_b = sb(fs, "sel_b", [P, H])
        bg = sb(fs, "bg", [P, 1 + NE])
        ebias = sb(fs, "ebias", [P, NE])
        eb12 = sb(fs, "eb12", [P, NE, 2 * H])
        eb3 = sb(fs, "eb3", [NE, D])
        falling = sb(fs, "falling", [P, NE])
        x2 = two(fs, "x2", [P, D])
        xn = two(fs, "xn", [P, D])
        xn_t = two(fs, "xn_t", [P, C, P])
        u = two(fs, "u", [P, 2 * H])
        gate = two(fs, "gate", [P, H])
        z = two(fs, "z", [P, H])
        z_t = two(fs, "z_t", [P, HC, P])
        shared = two(fs, "shared", [P, D])
        o = two(fs, "o", [P, D])
        logits = sb(fs, "logits", [P, 1 + NE])
        scores = sb(fs, "scores", [P, 1 + NE])
        pick = sb(fs, "pick", [P, 4, NE])
        one = sb(fs, "one", [P, 8])
        coef_t = sb(fs, "coef_t", [NE, P])

        main_loaded, experts_loaded = sem("main_loaded"), sem("experts_loaded")
        x2_loaded = pair("x2_loaded")
        m_var, m_rstd = pair("m_var"), pair("m_rstd")
        xn_ready, xn_turned, xn_t_ready = pair("xn_ready"), pair("xn_turned"), pair("xn_t_ready")
        u_done, u_ready, gate_ready = pair("u_done"), pair("u_ready"), pair("gate_ready")
        z_ready, z_turned, z_t_ready = pair("z_ready"), pair("z_turned"), pair("z_t_ready")
        shared_done, out_ready, out_stored = pair("shared_done"), pair("out_ready"), pair("out_stored")
        ffn_step = sem("ffn_step")
        logits_done, logits_ready, scores_ready = sem("logits_done"), sem("logits_ready"), sem("scores_ready")
        margin_ready, shares_ready = sem("margin_ready"), sem("shares_ready")
        coef_ready, coef_turned, coef_t_ready = sem("coef_ready"), sem("coef_turned"), sem("coef_t_ready")
        e_u_done, e_u_ready, e_gate_ready = sem("e_u_done"), sem("e_u_ready"), sem("e_gate_ready")
        e_var, e_rstd = sem("e_var"), sem("e_rstd")
        e_z_ready, e_z_turned, e_z_t_ready = sem("e_z_ready"), sem("e_z_turned"), sem("e_z_t_ready")
        e_sum_done, e_step = sem("e_sum_done"), sem("e_step")
        FFN_STEPS = 2 * 8
        E_STEPS = 10 + 5 * NE

        block = fs.enter_context(nc.Block())

        def skip(eng, n, counts):
            for q, k in counts:
                eng.wait_ge(q, k * n)
                eng.sem_inc(q, k)

        def selected(eng, i, s):
            return eng.value_load(flags[0:1, bass.ds(2 * i + s, 1)], min_val=0, max_val=P * M)

        pool_counts = ((e_rstd, NE),)
        act_counts = ((scores_ready, 1), (shares_ready, 2), (coef_t_ready, 1), (e_gate_ready, NE), (e_z_t_ready, NE))
        dve_counts = ((logits_ready, 1), (margin_ready, 1), (coef_ready, 1), (e_u_ready, NE), (e_var, NE),
                      (e_z_ready, NE), (e_step, E_STEPS))
        pe_counts = ((logits_done, 1), (coef_turned, 1), (e_u_done, NE), (e_z_turned, NE), (e_sum_done, 1))

        def start(eng, counts):
            for q, k in counts:
                eng.sem_inc(q, k)

        @block.sync
        def _(sp):
            start(sp, [(out_stored[s], 16) for s in SLOTS])

            def load(i, s, first):
                if not first:
                    sp.wait_ge(out_ready[s], i + 1)
                sp.dma_start(x2[s][:], a["x2"][bass.ds(2 * i + s, 1)].rearrange("a p d -> (a p) d")
                             ).then_inc(x2_loaded[s], 16)

            def store(i, s):
                sp.wait_ge(out_ready[s], i + 2)
                sp.dma_start(a["out"][bass.ds(2 * i + s, 1)].rearrange("a p d -> (a p) d"), o[s][:]
                             ).then_inc(out_stored[s], 16)

            for s in SLOTS:
                load(0, s, True)
            for name, dst in (("w12", w12), ("w3", w3)):
                sp.dma_start(dst[:], a[name]).then_inc(main_loaded, 16)
            for name, dst in (("b12", b12), ("b3", b3), ("ln_g", ln_g), ("ln_b", ln_b)):
                sp.dma_start(dst[:], a[name].partition_broadcast(P)).then_inc(main_loaded, 16)
            for name, dst in (("wg", wg), ("ew12", ew12), ("ew3", ew3), ("eb3", eb3)):
                sp.dma_start(dst[:], a[name]).then_inc(experts_loaded, 16)
            for name, dst in (("sel_g", sel_g), ("sel_b", sel_b), ("bg", bg), ("ebias", ebias), ("falling", falling)):
                sp.dma_start(dst[:], a[name].partition_broadcast(P)).then_inc(experts_loaded, 16)
            sp.dma_start(eb12[:], a["eb12"].partition_broadcast(P)).then_inc(experts_loaded, 16)
            with sp.Fori(1, PAIRS) as i:
                for s in SLOTS:
                    load(i, s, False)
                for s in SLOTS:
                    store(i - 1, s)
            for s in SLOTS:
                store(PAIRS - 1, s)
            for s in SLOTS:
                sp.wait_ge(out_stored[s], 16 * PAIRS + 16)
            sp.wait_ge(experts_loaded, 16 * 10)

        @block.gpsimd
        def _(pool):
            start(pool, pool_counts)
            with pool.Fori(0, PAIRS) as i:
                for n in (1, 2):
                    for s in SLOTS:
                        pool.wait_ge(m_var[s], 2 * i + n)
                        nc.gpsimd.tensor_tensor(rstd[s][:], var[s][:], mhalf[:], ALU.pow).then_inc(m_rstd[s], 1)
                for s in SLOTS:
                    n = 2 * i + s + 1
                    rows = selected(pool, i, s)
                    with pool.If(rows > 0):
                        for e in range(NE):
                            pool.wait_ge(e_var, NE * n + e + 1)
                            nc.gpsimd.tensor_tensor(rstd[s][:], var[s][:], mhalf[:], ALU.pow).then_inc(e_rstd, 1)
                    with pool.Else():
                        skip(pool, n, pool_counts)

        @block.scalar
        def _(act):
            start(act, act_counts)
            with act.Fori(0, PAIRS) as i:
                for s in SLOTS:
                    act.wait_ge(xn_turned[s], i + 1)
                    nc.scalar.copy(xn_t[s][:].rearrange("p c r -> p (c r)"), ps_t[s][:]).then_inc(xn_t_ready[s], 1)
                for s in SLOTS:
                    act.wait_ge(u_ready[s], i + 1)
                    nc.scalar.activation(gate[s][:], u[s][:, 0:H], ACT.Silu).then_inc(gate_ready[s], 1)
                for s in SLOTS:
                    act.wait_ge(z_turned[s], i + 1)
                    nc.scalar.copy(z_t[s][:].rearrange("p c r -> p (c r)"), ps_t[s][:, 0:H]).then_inc(z_t_ready[s], 1)
                for s in SLOTS:
                    n = 2 * i + s + 1
                    rows = selected(act, i, s)
                    with act.If(rows > 0):
                        act.wait_ge(logits_ready, n + 1)
                        nc.scalar.activation(scores[:], logits[:], ACT.Sigmoid).then_inc(scores_ready, 1)
                        act.wait_ge(margin_ready, n + 1)
                        nc.scalar.activation(one[:, 3:4], one[:, 2:3], ACT.Sigmoid, scale=-1.0).then_inc(shares_ready, 1)
                        nc.scalar.activation(one[:, 4:5], one[:, 2:3], ACT.Sigmoid).then_inc(shares_ready, 1)
                        act.wait_ge(coef_turned, n + 1)
                        nc.scalar.copy(coef_t[:], ps_b[s][0:NE, 0:P]).then_inc(coef_t_ready, 1)
                        for e in range(NE):
                            act.wait_ge(e_u_ready, NE * n + e + 1)
                            nc.scalar.activation(gate[s][:], u[s][:, 0:H], ACT.Silu).then_inc(e_gate_ready, 1)
                            act.wait_ge(e_z_turned, NE * n + e + 1)
                            nc.scalar.copy(z_t[s][:].rearrange("p c r -> p (c r)"), ps_t[s][:, 0:H]
                                           ).then_inc(e_z_t_ready, 1)
                    with act.Else():
                        skip(act, n, act_counts)

        @block.vector
        def _(dve):
            start(dve, dve_counts)
            start(dve, [(out_ready[s], 1) for s in SLOTS])
            dve.wait_ge(main_loaded, 16 * 6)
            with dve.Fori(0, PAIRS) as i:
                count = [0]

                def step(ins):
                    count[0] += 1
                    ins.then_inc(ffn_step, 1)
                    dve.wait_ge(ffn_step, FFN_STEPS * i + count[0])

                for s in SLOTS:
                    dve.wait_ge(x2_loaded[s], 16 * i + 16)
                    step(nc.vector.bn_stats(stats[s][:], x2[s][:]))
                    dve.sem_inc(stats_seen, 1)
                    step(nc.vector.bn_aggr(mv[s][:], stats[s][:]))
                    nc.vector.tensor_scalar(var[s][:], mv[s][:, 1:2], 1e-5, None, ALU.add).then_inc(m_var[s], 1)
                    dve.wait_ge(m_rstd[s], 2 * i + 1)
                    nc.vector.tensor_scalar(xn[s][:], x2[s][:], mv[s][:, 0:1], rstd[s][:], ALU.subtract, ALU.mult
                                            ).then_inc(xn_ready[s], 1)
                for s in SLOTS:
                    dve.wait_ge(u_done[s], i + 1)
                    nc.vector.tensor_tensor(u[s][:], ps_a[s][:], b12[:], ALU.add).then_inc(u_ready[s], 1)
                for s in SLOTS:
                    dve.wait_ge(gate_ready[s], i + 1)
                    step(nc.vector.tensor_tensor(z[s][:], gate[s][:], u[s][:, H:], ALU.mult))
                    step(nc.vector.bn_stats(stats[s][:], z[s][:]))
                    dve.sem_inc(stats_seen, 1)
                    step(nc.vector.bn_aggr(mv[s][:], stats[s][:]))
                    nc.vector.tensor_scalar(var[s][:], mv[s][:, 1:2], 1e-5, None, ALU.add).then_inc(m_var[s], 1)
                    dve.wait_ge(m_rstd[s], 2 * i + 2)
                    step(nc.vector.scalar_tensor_tensor(z[s][:], z[s][:], mv[s][:, 0:1], ln_g[:], ALU.subtract,
                                                        ALU.mult))
                    nc.vector.scalar_tensor_tensor(z[s][:], z[s][:], rstd[s][:], ln_b[:], ALU.mult, ALU.add
                                                   ).then_inc(z_ready[s], 1)
                for s in SLOTS:
                    n = 2 * i + s + 1
                    rows = selected(dve, i, s)
                    dve.wait_ge(shared_done[s], i + 1)
                    step(nc.vector.tensor_tensor(shared[s][:], ps_b[s][:], b3[:], ALU.add))
                    dve.wait_ge(out_stored[s], 16 * i + 16)
                    count[0] += 1
                    nc.vector.tensor_tensor(o[s][:], shared[s][:], x2[s][:], ALU.add).then_inc(ffn_step, 1)
                    with dve.If(rows > 0):
                        dve.wait_ge(ffn_step, FFN_STEPS * i + count[0])
                        e_count = [0]

                        def e_next(ins):
                            e_count[0] += 1
                            ins.then_inc(e_step, 1)
                            dve.wait_ge(e_step, E_STEPS * n + e_count[0])

                        dve.wait_ge(experts_loaded, 16 * 10)
                        dve.wait_ge(logits_done, n + 1)
                        nc.vector.tensor_tensor(logits[:], ps_c[s][:, 0:1 + NE], bg[:], ALU.add).then_inc(logits_ready, 1)
                        dve.wait_ge(scores_ready, n + 1)
                        e_next(nc.vector.tensor_tensor(pick[:, 0, :], scores[:, 1:], ebias[:], ALU.add))
                        e_next(nc.vector.reduce_max(one[:, 0:1], pick[:, 0, :], AX.X))
                        e_next(nc.vector.scalar_tensor_tensor(pick[:, 1, :], pick[:, 0, :], one[:, 0:1], falling[:],
                                                              ALU.is_ge, ALU.mult))
                        e_next(nc.vector.reduce_max(one[:, 1:2], pick[:, 1, :], AX.X))
                        e_next(nc.vector.tensor_scalar(pick[:, 2, :], falling[:], one[:, 1:2], None, ALU.is_equal))
                        e_next(nc.vector.tensor_tensor(pick[:, 3, :], pick[:, 2, :], scores[:, 1:], ALU.mult))
                        e_next(nc.vector.reduce_sum(one[:, 5:6], pick[:, 3, :], AX.X))
                        nc.vector.tensor_tensor(one[:, 2:3], one[:, 5:6], scores[:, 0:1], ALU.subtract
                                                ).then_inc(margin_ready, 1)
                        dve.wait_ge(shares_ready, 2 * n + 2)
                        mine = sel[:, bass.ds(2 * i + s, 1)]
                        e_next(nc.vector.tensor_tensor(one[:, 6:7], one[:, 4:5], mine, ALU.mult))
                        e_next(nc.vector.scalar_tensor_tensor(one[:, 7:8], one[:, 3:4], -1.0, mine, ALU.add, ALU.mult))
                        nc.vector.tensor_scalar(pick[:, 3, :], pick[:, 2, :], one[:, 6:7], None, ALU.mult
                                                ).then_inc(coef_ready, 1)
                        e_next(nc.vector.scalar_tensor_tensor(o[s][:], shared[s][:], one[:, 7:8], o[s][:], ALU.mult,
                                                              ALU.add))
                        dve.wait_ge(coef_ready, n + 1)
                        for e in range(NE):
                            dve.wait_ge(e_u_done, NE * n + e + 1)
                            if e:
                                dve.wait_ge(e_gate_ready, NE * n + e)
                            nc.vector.tensor_tensor(u[s][:], (ps_a, ps_c)[e % 2][s][:], eb12[:, e, :], ALU.add
                                                    ).then_inc(e_u_ready, 1)
                            dve.wait_ge(e_gate_ready, NE * n + e + 1)
                            if e:
                                dve.wait_ge(e_z_turned, NE * n + e)
                            e_next(nc.vector.tensor_tensor(z[s][:], gate[s][:], u[s][:, H:], ALU.mult))
                            e_next(nc.vector.bn_stats(stats[s][:], z[s][:]))
                            dve.sem_inc(stats_seen, 1)
                            e_next(nc.vector.bn_aggr(mv[s][:], stats[s][:]))
                            nc.vector.tensor_scalar(var[s][:], mv[s][:, 1:2], 1e-5, None, ALU.add).then_inc(e_var, 1)
                            dve.wait_ge(e_rstd, NE * n + e + 1)
                            e_next(nc.vector.scalar_tensor_tensor(z[s][:], z[s][:], mv[s][:, 0:1], sel_g[:],
                                                                  ALU.subtract, ALU.mult))
                            e_next(nc.vector.scalar_tensor_tensor(z[s][:], z[s][:], rstd[s][:], sel_b[:], ALU.mult,
                                                                  ALU.add))
                            nc.vector.tensor_scalar(z[s][:], z[s][:], pick[:, 3, e:e + 1], None, ALU.mult
                                                    ).then_inc(e_z_ready, 1)
                        assert e_count[0] == E_STEPS, e_count[0]
                        dve.wait_ge(e_sum_done, n + 1)
                        nc.vector.tensor_tensor(o[s][:], ps_b[s][:], o[s][:], ALU.add).then_inc(out_ready[s], 1)
                    with dve.Else():
                        dve.wait_ge(ffn_step, FFN_STEPS * i + count[0])
                        skip(dve, n, dve_counts)
                        skip(dve, i + 1, ((out_ready[s], 1),))
                assert count[0] == FFN_STEPS, count[0]

        @block.tensor
        def _(pe):
            start(pe, pe_counts)
            pe.wait_ge(main_loaded, 16 * 6)

            def product(out, w, s):
                for c in range(C):
                    mm = nc.tensor.matmul(out, xn_t[s][:, c, :], w[:, c, :], start=(c == 0), stop=(c == C - 1),
                                          skip_group_check=True)
                return mm

            with pe.Fori(0, PAIRS) as i:
                for s in SLOTS:
                    pe.wait_ge(xn_ready[s], i + 1)
                    for c in range(C):
                        mm = nc.tensor.transpose(ps_t[s][:, c * P:(c + 1) * P], xn[s][:, c * P:(c + 1) * P], ident[:])
                    mm.then_inc(xn_turned[s], 1)
                for s in SLOTS:
                    pe.wait_ge(xn_t_ready[s], i + 1)
                    product(ps_a[s][:], w12, s).then_inc(u_done[s], 1)
                for s in SLOTS:
                    pe.wait_ge(z_ready[s], i + 1)
                    for c in range(HC):
                        mm = nc.tensor.transpose(ps_t[s][:, c * P:(c + 1) * P], z[s][:, c * P:(c + 1) * P], ident[:])
                    mm.then_inc(z_turned[s], 1)
                for s in SLOTS:
                    pe.wait_ge(z_t_ready[s], i + 1)
                    for c in range(HC):
                        mm = nc.tensor.matmul(ps_b[s][:], z_t[s][:, c, :], w3[:, c, :], start=(c == 0),
                                              stop=(c == HC - 1))
                    mm.then_inc(shared_done[s], 1)
                for s in SLOTS:
                    n = 2 * i + s + 1
                    rows = selected(pe, i, s)
                    with pe.If(rows > 0):
                        pe.wait_ge(experts_loaded, 16 * 10)
                        product(ps_c[s][:, 0:1 + NE], wg, s).then_inc(logits_done, 1)
                        product(ps_a[s][:], ew12[:, 0], s).then_inc(e_u_done, 1)
                        pe.wait_ge(coef_ready, n + 1)
                        nc.tensor.transpose(ps_b[s][0:NE, 0:P], pick[:, 3, :], ident[:]).then_inc(coef_turned, 1)
                        pe.wait_ge(coef_t_ready, n + 1)
                        nc.tensor.matmul(ps_b[s][:], coef_t[:], eb3[:], start=True, stop=False, skip_group_check=True)
                        for e in range(NE):
                            if e + 1 < NE:
                                pe.wait_ge(e_u_ready, NE * n + e)
                                product((ps_a, ps_c)[(e + 1) % 2][s][:], ew12[:, e + 1], s).then_inc(e_u_done, 1)
                            pe.wait_ge(e_z_ready, NE * n + e + 1)
                            for c in range(HC):
                                mm = nc.tensor.transpose(ps_t[s][:, c * P:(c + 1) * P], z[s][:, c * P:(c + 1) * P],
                                                         ident[:])
                            mm.then_inc(e_z_turned, 1)
                            pe.wait_ge(e_z_t_ready, NE * n + e + 1)
                            for c in range(HC):
                                mm = nc.tensor.matmul(ps_b[s][:], z_t[s][:, c, :], ew3[:, e, c, :], start=False,
                                                      stop=(e == NE - 1 and c == HC - 1), skip_group_check=True)
                        mm.then_inc(e_sum_done, 1)
                    with pe.Else():
                        skip(pe, n, pe_counts)


def rows_on_partitions(w):
    return np.ascontiguousarray(w.reshape(-1, P, w.shape[-1]).transpose(1, 0, 2))


def layout(v):
    names = {k.replace("L0_", "", 1): np.asarray(x) for k, x in v.items()}
    cx = names["ctx_1024"].reshape(TILES, G, S, D)[::-1].reshape(B, S, D)
    w = {k[6:]: names[k] for k in names if k.startswith("xattn_")}
    f = {k[4:]: names[k] for k in names if k.startswith("ffn_")}
    at = {
        "x": names["x"].reshape(TILES, P, D)[::-1],
        "ctx_t": cx.reshape(TILES, G, S, C, P).transpose(0, 4, 3, 1, 2),
        "ctx_n": cx[:, :SC * P].reshape(TILES, G, SC, P, D).transpose(0, 3, 1, 2, 4),
        "ctx_last": cx[:, S - 1].reshape(TILES, G, D),
        "wq_t": rows_on_partitions(w["Wq"].T), "wk_t": rows_on_partitions(w["Wk"].T),
        "wcq_t": rows_on_partitions(w["Wcq"].T), "wck_t": rows_on_partitions(w["Wck"].T),
        "wv": rows_on_partitions(w["Wv"]), "wcv": rows_on_partitions(w["Wcv"]), "w1": rows_on_partitions(w["W1"]),
        "wattn": rows_on_partitions(names["attn_W_attn"]), "wproj": rows_on_partitions(names["attn_W_proj"]),
        "gamma": w["gamma"], "beta": w["beta"], "b1": w["b1"],
        "index_b": f["index_b"].reshape(P, MC), "index_t": f["index_t"].reshape(P, MC),
        "w12": rows_on_partitions(np.concatenate([f["sw1"], f["sw2"]]).T), "w3": rows_on_partitions(f["sw3"].T),
        "b12": np.concatenate([f["sb1"], f["sb2"]]), "b3": f["sb3"], "ln_g": f["s_ln_g"], "ln_b": f["s_ln_b"],
        "wg": rows_on_partitions(np.concatenate([f["sg_w"], f["eg_w"]]).T),
        "bg": np.concatenate([f["sg_b"], f["eg_b"]]), "ebias": f["exp_bias"],
        "ew12": np.concatenate([f["ew1"], f["ew2"]], axis=1).reshape(NE, 2 * H, C, P).transpose(3, 0, 2, 1),
        "ew3": f["ew3"].reshape(NE, D, HC, P).transpose(3, 0, 2, 1),
        "eb12": np.concatenate([f["eb1"], f["eb2"]], axis=1), "eb3": f["eb3"],
        "sel_g": f["sel_ln_g"], "sel_b": f["sel_ln_b"],
    }
    r = np.arange(P)
    at["ident"] = np.eye(P, dtype=np.float32)
    at["entry_of"] = np.arange(B, dtype=np.float32).reshape(TILES, G)[::-1].reshape(B)
    at["iota_t"] = np.arange(T, dtype=np.float32)
    at["mask_self"] = np.where((r[:, None] // T == r[None, :] // T) & (r[None, :] <= r[:, None]), 0.0, NEG)
    at["mask_head"] = np.where(r[None, :T] <= r[:, None] % T, 0.0, NEG)
    at["mask_entry"] = r[:, None] // T == np.arange(G)[None, :]
    at["falling"] = np.arange(NE, 0, -1)
    echoic, length = 16, 1024
    fading = 1.0 - np.linspace(0.0, 1.0, length - echoic + 1) ** (1.0 / np.e)
    weight = np.concatenate([np.ones(echoic - 1), fading])
    at["decay"] = weight[np.clip(r[:, None] % T - r[None, :T], 0, T - 1)]
    for k in ("mask_self", "mask_head", "mask_entry", "falling", "decay"):
        at[k] = at[k].astype(np.float32)
    return {k: np.ascontiguousarray(x) for k, x in at.items()}


def kernel(**inputs):
    import concourse.bacc as bacc
    from concourse.bass_utils import run_bass_kernel_spmd

    nc = bacc.Bacc("TRN2", target_bir_lowering=False, num_devices=1)
    arrays = {f"in_{k}": x for k, x in layout(inputs).items()}
    a = {k[3:]: nc.dram_tensor(k, x.shape, mybir.dt.from_np(x.dtype), kind="ExternalInput").ap()
         for k, x in arrays.items()}
    a["out"] = nc.dram_tensor("out_0", (TILES, P, D), F32, kind="ExternalOutput").ap()
    a["x2"] = nc.dram_tensor("x2_scratch", (TILES, P, D), F32, kind="Internal").ap()
    build(nc, a)
    r = run_bass_kernel_spmd(nc, [arrays], core_ids=[0])
    return np.ascontiguousarray(r.results[0]["out_0"][::-1]).reshape(B, T, D)
```

```python
from contextlib import ExitStack

import numpy as np

import concourse.bass as bass
from concourse import mybir

F32 = mybir.dt.float32
BF16 = mybir.dt.bfloat16
I32 = mybir.dt.int32
ALU = mybir.AluOpType
ACT = mybir.ActivationFunctionType
AX = mybir.AxisListType

P = 128
B, T, D = 128, 32, 512
S = 257
G = P // T
TILES = B // G
C = D // P
SC = (S - 1) // P
NH = 16
HD = D // NH
HPC = P // HD
H = 256
HC = H // P
NE = 8
M = 1024
MC = M // P
NEG = -1.0e30
XSCALE = float(D) ** -0.5
HSCALE = float(HD) ** -0.5
SLOTN = 3
SLOTS = tuple(range(SLOTN))
N_WEIGHTS = 19



ORDER = [
    (2, "head_scores"), (1, "turn_w"), (0, "turn_xn"), (1, "context_out"), (0, "project_self"), (2, "head_mix"),
    (0, "self_scores"), (1, "turn_h2"), (2, "project_out"), (0, "turn_p"), (1, "hidden"), (0, "self_mix"),
    (2, "turn_x2n"), (2, "ffn_in"), (0, "turn_h"), (0, "project_query"), (2, "turn_z"), (0, "context_scores"),
    (2, "ffn_out"), (1, "turn_x1n"), (0, "turn_pc"), (1, "project_heads"), (0, "context_mix"),
]
STEPS = {"xn": 2, "self_scores": 2, "self_mix": 5, "context_scores": 1, "context_out": 4, "hidden": 8,
         "head_scores": 5, "project_out": 2, "silu": 4, "ffn_out": 1}


def run_pipeline(eng, order, work):
    lags = [lag for lag, name in order if name in work]
    full = (TILES - max(lags)) // SLOTN * SLOTN

    def step(n, base, i):
        for lag, name in order:
            if name in work:
                tile = n - lag
                if i is not None or 0 <= tile < TILES:
                    round_, at = (tile // SLOTN, tile) if i is None else (i + tile // SLOTN, SLOTN * i + tile)
                    work[name](tile % SLOTN, round_, at)

    for n in range(min(lags), max(lags)):
        step(n, 0, None)
    with eng.Fori(0, full // SLOTN) as i:
        for n in range(max(lags), max(lags) + SLOTN):
            step(n, 0, i)
    for n in range(max(lags) + full, TILES + max(lags)):
        step(n, 0, None)


def build(nc, a):
    ctx = ExitStack()
    with ctx:
        def sem(name):
            return ctx.enter_context(nc.semaphore(name))

        def sems(name):
            return [sem(f"{name}{s}") for s in SLOTS]

        def sb(stack, name, shape, dt=F32):
            return stack.enter_context(nc.sbuf_tensor(name, shape, dt))

        def slots(stack, name, shape, dt=F32):
            return [sb(stack, f"{name}{s}", shape, dt) for s in SLOTS]

        ps_t = [ctx.enter_context(nc.psum_tensor(f"ps_t{s}", [P, 512], F32)) for s in SLOTS]
        ps_a = [ctx.enter_context(nc.psum_tensor(f"ps_a{s}", [P, 512], F32)) for s in SLOTS]
        ps_v = ctx.enter_context(nc.psum_tensor("ps_v", [P, 512], F32))
        ps_e = ctx.enter_context(nc.psum_tensor("ps_e", [P, 512], F32))

        ident = sb(ctx, "ident", [P, P])
        sel = sb(ctx, "sel", [P, TILES])
        redo = sb(ctx, "redo", [1, 1 + TILES], I32)
        mhalf = sb(ctx, "mhalf", [P, 1])
        w12 = sb(ctx, "w12", [P, C, 2 * H])
        w3 = sb(ctx, "w3", [P, HC, D])
        b12 = sb(ctx, "b12", [P, 2 * H])
        b3 = sb(ctx, "b3", [P, D])
        ln_g = sb(ctx, "ln_g", [P, H])
        ln_b = sb(ctx, "ln_b", [P, H])
        stats = slots(ctx, "stats", [P, 6])
        mv = slots(ctx, "mv", [P, 2])
        var = slots(ctx, "var", [P, 1])
        rstd = slots(ctx, "rstd", [P, 1])

        weights_loaded = sem("weights_loaded")
        consts_ready = sem("consts_ready")
        stats_seen = sem("stats_seen")
        at = ExitStack()
        with at:
            wqk = sb(at, "wqk", [P, C, D])
            wcqk = sb(at, "wcqk", [P, C, D])
            wv = sb(at, "wv", [P, C, D])
            wcv = sb(at, "wcv", [P, C, D])
            w1 = sb(at, "w1", [P, C, D])
            wattn = sb(at, "wattn", [P, C, 3 * D])
            wproj = sb(at, "wproj", [P, C, D])
            gamma = sb(at, "gamma", [P, D])
            beta = sb(at, "beta", [P, D])
            b1 = sb(at, "b1", [P, D])
            mask_self = sb(at, "mask_self", [P, P])
            mask_head = sb(at, "mask_head", [P, T])
            decay = sb(at, "decay", [P, T])
            mask_entry = sb(at, "mask_entry", [P, G])
            kbd = sb(at, "kbd", [P, C, G, HPC, T])
            pbd = sb(at, "pbd", [P, NH, G, T])

            qk_loaded = [sem("wqk_loaded"), sem("wcqk_loaded")]
            idx_loaded, idx_step = sem("idx_loaded"), sem("idx_step")
            onehots_ready, sel_counted, sel_ready = sem("onehots_ready"), sem("sel_counted"), sem("sel_ready")
            product_done, product_copied = sem("product_done"), sem("product_copied")
            list_step = sem("list_step")
            with ExitStack() as st:
                wq_t = [sb(st, f"wq_t{n}", [P, C, D]) for n in range(2)]
                wk_t = [sb(st, f"wk_t{n}", [P, C, D]) for n in range(2)]
                entry_of = sb(st, "entry_of", [P, B])
                iota_t = sb(st, "iota_t", [P, T])
                idx_i = sb(st, "idx_i", [P, 2, MC], I32)
                idx = sb(st, "idx", [P, 2, MC])
                idx_neg = sb(st, "idx_neg", [P, 2, MC])
                hot_b = sb(st, "hot_b", [P, MC, B], BF16)
                hot_t = sb(st, "hot_t", [P, MC, T], BF16)
                ones = sb(st, "ones", [P, 1])
                any_row = sb(st, "any_row", [TILES, 1])
                upto = sb(st, "upto", [TILES, TILES])
                nth = sb(st, "nth", [TILES, TILES])
                nth_hot = sb(st, "nth_hot", [TILES, TILES])
                tile_id = sb(st, "tile_id", [TILES, 1])

                block = st.enter_context(nc.Block())

                @block.sync
                def _(sp):
                    sp.dma_start(wq_t[0][:], a["wq_t"]).then_inc(qk_loaded[0], 16)
                    sp.dma_start(wk_t[0][:], a["wk_t"]).then_inc(qk_loaded[0], 16)
                    sp.dma_start(idx_i[:, 0, :], a["index_b"]).then_inc(idx_loaded, 16)
                    sp.dma_start(idx_i[:, 1, :], a["index_t"]).then_inc(idx_loaded, 16)
                    sp.dma_start(entry_of[:], a["entry_of"].partition_broadcast(P)).then_inc(idx_loaded, 16)
                    sp.dma_start(iota_t[:], a["iota_t"].partition_broadcast(P)).then_inc(idx_loaded, 16)
                    sp.dma_start(upto[:], a["upto"]).then_inc(idx_loaded, 16)
                    sp.dma_start(nth[:], a["nth"].partition_broadcast(TILES)).then_inc(idx_loaded, 16)
                    sp.dma_start(tile_id[:], a["tile_id"]).then_inc(idx_loaded, 16)
                    sp.dma_start(wq_t[1][:], a["wcq_t"]).then_inc(qk_loaded[1], 16)
                    sp.dma_start(wk_t[1][:], a["wck_t"]).then_inc(qk_loaded[1], 16)
                    for name, dst in (("ident", ident), ("wv", wv), ("wcv", wcv), ("w1", w1),
                                      ("wattn", wattn), ("wproj", wproj), ("mask_self", mask_self),
                                      ("mask_head", mask_head), ("decay", decay), ("mask_entry", mask_entry),
                                      ("w12", w12), ("w3", w3)):
                        sp.dma_start(dst[:], a[name]).then_inc(weights_loaded, 16)
                    for name, dst in (("gamma", gamma), ("beta", beta), ("b1", b1), ("b12", b12), ("b3", b3), ("ln_g", ln_g),
                                      ("ln_b", ln_b)):
                        sp.dma_start(dst[:], a[name].partition_broadcast(P)).then_inc(weights_loaded, 16)
                    sp.wait_ge(weights_loaded, 16 * N_WEIGHTS)

                @block.gpsimd
                def _(pool):
                    nc.gpsimd.memset(kbd[:], 0.0).then_inc(consts_ready, 1)
                    nc.gpsimd.memset(pbd[:], 0.0).then_inc(consts_ready, 1)
                    nc.gpsimd.memset(mhalf[:], -0.5).then_inc(consts_ready, 1)
                    pool.wait_ge(consts_ready, 4)

                @block.vector
                def _(dve):
                    steps = [0]

                    def step(ins):
                        steps[0] += 1
                        ins.then_inc(idx_step, 1)
                        dve.wait_ge(idx_step, steps[0])

                    nc.vector.memset(ones[:], 1.0).then_inc(consts_ready, 1)
                    dve.wait_ge(idx_loaded, 16 * 7)
                    step(nc.vector.tensor_copy(idx[:], idx_i[:]))
                    for k, size in ((0, B), (1, T)):
                        step(nc.vector.tensor_scalar(idx_neg[:, k, :], idx[:, k, :], 0.0, float(size), ALU.is_lt, ALU.mult))
                    step(nc.vector.tensor_tensor(idx[:], idx[:], idx_neg[:], ALU.add))
                    for k, hot, values, size in ((0, hot_b, entry_of, B), (1, hot_t, iota_t, T)):
                        nc.vector.tensor_tensor(hot[:], values[:].unsqueeze(1).to_broadcast([P, MC, size]),
                                                idx[:, k, :].unsqueeze(2).to_broadcast([P, MC, size]),
                                                ALU.is_equal).then_inc(onehots_ready, 1)
                    dve.wait_ge(sel_counted, 1)
                    nc.vector.tensor_scalar(sel[:], ps_v[:, 0:TILES], 0.0, None, ALU.is_gt).then_inc(sel_ready, 1)
                    dve.wait_ge(list_step, 1)
                    nc.vector.tensor_scalar(any_row[:], ps_e[0:TILES, 0:1], 0.0, None, ALU.is_gt).then_inc(list_step, 1)
                    dve.wait_ge(list_step, 4)
                    nc.vector.scalar_tensor_tensor(nth_hot[:], nth[:], ps_e[0:TILES, 1:2],
                                                   any_row[:].to_broadcast([TILES, TILES]), ALU.is_equal, ALU.mult
                                                   ).then_inc(list_step, 1)
                    dve.wait_ge(list_step, 6)
                    nc.vector.tensor_scalar(redo[:, 0:1], ps_e[0:1, 2:3], 1.0, None, ALU.max)
                    nc.vector.tensor_copy(redo[:, 1:], ps_e[0:1, 4:4 + TILES])

                @block.scalar
                def _(act):
                    for n, w in ((0, wqk), (1, wcqk)):
                        for c in range(C):
                            act.wait_ge(product_done, n * C + c + 1)
                            nc.scalar.copy(w[:, c, :], (ps_a[0], ps_a[1], ps_t[0], ps_t[1])[c][:]).then_inc(product_copied, 1)

                @block.tensor
                def _(pe):
                    def product(n):
                        pe.wait_ge(qk_loaded[n], 32)
                        for c in range(C):
                            if n:
                                pe.wait_ge(product_copied, c + 1)
                            for d in range(C):
                                mm = nc.tensor.matmul((ps_a[0], ps_a[1], ps_t[0], ps_t[1])[c][:], wq_t[n][:, d, c * P:(c + 1) * P],
                                                      wk_t[n][:, d, :], start=(d == 0), stop=(d == C - 1))
                            mm.then_inc(product_done, 1)

                    product(0)
                    pe.wait_ge(onehots_ready, 2)
                    for g in range(G):
                        for c in range(MC):
                            mm = nc.tensor.matmul(ps_v[T * g:T * (g + 1), 0:TILES], hot_t[:, c, :], hot_b[:, c, g::G],
                                                  start=(c == 0), stop=(c == MC - 1), skip_group_check=True)
                    mm.then_inc(sel_counted, 1)
                    product(1)
                    pe.wait_ge(sel_ready, 1)
                    pe.wait_ge(consts_ready, 4)
                    nc.tensor.matmul(ps_e[0:TILES, 0:1], sel[:], ones[:], start=True, stop=True).then_inc(list_step, 1)
                    pe.wait_ge(list_step, 2)
                    nc.tensor.matmul(ps_e[0:TILES, 1:2], upto[:], any_row[:], start=True, stop=True
                                     ).then_inc(list_step, 1)
                    nc.tensor.matmul(ps_e[0:1, 2:3], ones[0:TILES, :], any_row[:], start=True, stop=True
                                     ).then_inc(list_step, 1)
                    pe.wait_ge(list_step, 5)
                    nc.tensor.matmul(ps_e[0:1, 4:4 + TILES], tile_id[:], nth_hot[:], start=True, stop=True
                                     ).then_inc(list_step, 1)


            ctx_t = sb(at, "ctx_t", [P, C, G, S])
            ctx_n = sb(at, "ctx_n", [P, G, SC, D])
            ctx_last = sb(at, "ctx_last", [G, D])
            x_in = slots(at, "x_in", [P, D])
            rows1 = slots(at, "rows1", [P, D])
            rows2 = slots(at, "rows2", [P, D])
            rows3 = slots(at, "rows3", [P, D])
            act_t = slots(at, "act_t", [P, C, P])
            q_t = slots(at, "q_t", [P, C, P])
            v_n = slots(at, "v_n", [P, D])
            p_n = slots(at, "p_n", [P, S + G])
            p_t = slots(at, "p_t", [P, SC * P + P])
            top = slots(at, "top", [P, NH])
            ntop = slots(at, "ntop", [P, 1])
            total = slots(at, "total", [P, NH])
            inv = slots(at, "inv", [P, NH])

            x_loaded, x_used = sems("x_loaded"), sems("x_used")
            ctx_t_loaded, ctx_n_loaded = sem("ctx_t_loaded"), sem("ctx_n_loaded")
            var_ready, rstd_ready = sems("var_ready"), sems("rstd_ready")
            rows_ready = sems("rows_ready")
            turned = sems("turned")
            act_t_ready = sems("act_t_ready")
            q_done, q_ready = sems("q_done"), sems("q_ready")
            v_done, v_ready = sems("v_done"), sems("v_ready")
            scored = sems("scored")
            ntop_ready = sems("ntop_ready")
            p_ready = sems("p_ready")
            p4_ready = sems("p4_ready")
            p_turned, p_t_ready = sems("p_turned"), sems("p_t_ready")
            rows_done = sems("rows_done")
            k_done, k_ready = sems("k_done"), sems("k_ready")
            heads_shifted = sems("heads_shifted")
            decayed, pbd_ready, y_done, y_ready = sems("decayed"), sems("pbd_ready"), sems("y_done"), sems("y_ready")
            u_ready, gate_ready = sems("u_ready"), sems("gate_ready")
            x2_ready, x2_stored = sems("x2_ready"), sems("x2_stored")
            out_ready, out_stored = sems("out_ready"), sems("out_stored")
            dve_step = sems("dve_step")
            steps_before, steps_in_all = {}, 0
            for name in STEPS:
                steps_before[name] = steps_in_all
                steps_in_all += STEPS[name]

            block = at.enter_context(nc.Block())

            @block.sync
            def _(sp):
                def plane(ap, tile):
                    if isinstance(tile, int):
                        return ap[tile]
                    names = "abcde"[:len(ap.shape)]
                    return ap[bass.ds(tile, 1)].rearrange(f"{' '.join(names)} -> ({names[0]} {names[1]}) {' '.join(names[2:])}")

                def load_x(s, r, tile):
                    sp.wait_ge(x_used[s], r + 1)
                    sp.dma_start(x_in[s][:], plane(a["x"], tile)).then_inc(x_loaded[s], 16)

                def load_ctx(s, r, tile):
                    before = (s - 1) % SLOTN, r - (s == 0)
                    if not (isinstance(tile, int) and tile == 0):
                        sp.wait_ge(scored[before[0]], 3 * before[1] + 2)
                    sp.dma_start(ctx_t[:], plane(a["ctx_t"], tile)).then_inc(ctx_t_loaded, 16)
                    if not (isinstance(tile, int) and tile == 0):
                        sp.wait_ge(v_done[before[0]], 3 * before[1] + 2)
                    sp.dma_start(ctx_n[:], plane(a["ctx_n"], tile)).then_inc(ctx_n_loaded, 16)
                    sp.dma_start(ctx_last[:], plane(a["ctx_last"], tile)).then_inc(ctx_n_loaded, 16)

                def store(s, r, tile):
                    sp.wait_ge(x2_ready[s], r + 1)
                    sp.dma_start(plane(a["x2"], tile), rows3[s][:]).then_inc(x2_stored[s], 16)
                    sp.wait_ge(out_ready[s], r + 1)
                    sp.dma_start(plane(a["out"], tile), rows1[s][:]).then_inc(out_stored[s], 16)

                for s in SLOTS:
                    sp.sem_inc(x2_stored[s], 16)
                    sp.sem_inc(out_stored[s], 16)
                run_pipeline(sp, [(0, "load_x"), (0, "load_ctx"), (3, "store")],
                             {"load_x": load_x, "load_ctx": load_ctx, "store": store})
                for s in SLOTS:
                    sp.wait_ge(x2_stored[s], 16 * (1 + len(range(s, TILES, SLOTN))))
                    sp.wait_ge(out_stored[s], 16 * (1 + len(range(s, TILES, SLOTN))))

            @block.gpsimd
            def _(pool):
                def inverse_std(n):
                    def unit(s, r, tile):
                        pool.wait_ge(var_ready[s], 7 * r + n)
                        nc.gpsimd.tensor_tensor(rstd[s][:], var[s][:], mhalf[:], ALU.pow).then_inc(rstd_ready[s], 1)
                    return unit

                def hidden(s, r, tile):
                    inverse_std(4)(s, r, tile)
                    inverse_std(5)(s, r, tile)

                def head_scores(s, r, tile):
                    pool.wait_ge(p_ready[s], 3 * r + 3)
                    nc.gpsimd.tensor_tensor(rows3[s][:].rearrange("p (h k) -> p h k", k=T),
                                            rows1[s][:].rearrange("p (h k) -> p h k", k=T),
                                            decay[:].unsqueeze(1).to_broadcast([P, NH, T]), ALU.mult
                                            ).then_inc(decayed[s], 1)

                run_pipeline(pool, ORDER, {
                    "turn_xn": inverse_std(1), "self_mix": inverse_std(2), "context_out": inverse_std(3),
                    "hidden": hidden, "head_scores": head_scores, "project_out": inverse_std(6),
                    "ffn_in": inverse_std(7)})

            @block.scalar
            def _(act):
                def copy_turned(n, bank):
                    def unit(s, r, tile):
                        act.wait_ge(turned[s], 7 * r + n)
                        nc.scalar.copy(act_t[s][:].rearrange("p c r -> p (c r)"), bank[s][:]).then_inc(act_t_ready[s], 1)
                    return unit

                def project_self(s, r, tile):
                    act.wait_ge(v_done[s], 3 * r + 1)
                    nc.scalar.copy(v_n[s][:], ps_t[s][:]).then_inc(v_ready[s], 1)

                def self_scores(s, r, tile):
                    act.wait_ge(ntop_ready[s], 2 * r + 1)
                    nc.scalar.activation(p_n[s][:, 0:P], rows3[s][:, 0:P], ACT.Exp, bias=ntop[s][:], scale=XSCALE,
                                         accum_out=total[s][:, 0:1]).then_inc(p_ready[s], 1)

                def turn_p(s, r, tile):
                    act.wait_ge(p_turned[s], 2 * r + 1)
                    nc.scalar.copy(p_t[s][:, 0:P], ps_a[s][:, 0:P]).then_inc(p_t_ready[s], 1)

                def project_query(s, r, tile):
                    act.wait_ge(q_done[s], 3 * r + 2)
                    nc.scalar.copy(q_t[s][:].rearrange("p c r -> p (c r)"), ps_t[s][:]).then_inc(q_ready[s], 1)

                def context_scores(s, r, tile):
                    act.wait_ge(ntop_ready[s], 2 * r + 2)
                    nc.scalar.activation(p_n[s][:, 0:S], ps_a[s][:, 0:S], ACT.Exp, bias=ntop[s][:], scale=XSCALE,
                                         accum_out=total[s][:, 0:1]).then_inc(p_ready[s], 1)

                def turn_pc(s, r, tile):
                    act.wait_ge(p_turned[s], 2 * r + 2)
                    nc.scalar.copy(p_t[s][:, 0:SC * P], ps_t[s][:, 0:SC * P])
                    nc.scalar.copy(p_t[s][0:G, SC * P:], ps_t[s][0:G, SC * P:SC * P + P]).then_inc(p_t_ready[s], 1)

                def context_mix(s, r, tile):
                    act.wait_ge(v_done[s], 3 * r + 2)
                    act.wait_ge(p4_ready[s], 2 * r + 2)
                    nc.scalar.activation(v_n[s][:], ps_a[s][:], ACT.Copy, scale=inv[s][:, 0:1]).then_inc(v_ready[s], 1)

                def project_heads(s, r, tile):
                    act.wait_ge(k_done[s], r + 1)
                    for h in (0, 1):
                        nc.scalar.copy(kbd[HD * h:HD * (h + 1), :, :, h, :],
                                       ps_a[s][HD * h:HD * (h + 1), :].rearrange("p (c g k) -> p c g k", c=C, g=G)
                                       ).then_inc(k_ready[s], 1)
                    act.wait_ge(q_done[s], 3 * r + 3)
                    nc.scalar.copy(q_t[s][:].rearrange("p c r -> p (c r)"), ps_t[s][:]).then_inc(q_ready[s], 1)
                    act.wait_ge(v_done[s], 3 * r + 3)
                    nc.scalar.copy(v_n[s][:], ps_v[:]).then_inc(v_ready[s], 1)

                def head_scores(s, r, tile):
                    act.wait_ge(heads_shifted[s], r + 1)
                    nc.scalar.activation(rows1[s][:], rows3[s][:], ACT.Exp, scale=HSCALE).then_inc(p_ready[s], 1)

                def head_mix(s, r, tile):
                    act.wait_ge(y_done[s], r + 1)
                    nc.scalar.copy(act_t[s][:].rearrange("p c r -> p (c r)"), ps_t[s][:]).then_inc(y_ready[s], 1)

                def ffn_in(s, r, tile):
                    act.wait_ge(u_ready[s], r + 1)
                    nc.scalar.activation(v_n[s][:, 0:H], rows2[s][:, 0:H], ACT.Silu).then_inc(gate_ready[s], 1)

                def turn_z(s, r, tile):
                    act.wait_ge(turned[s], 7 * r + 7)
                    nc.scalar.copy(p_t[s][:, 0:H], ps_t[s][:, 0:H]).then_inc(act_t_ready[s], 1)

                run_pipeline(act, ORDER, {
                    "turn_xn": copy_turned(1, ps_t), "project_self": project_self, "self_scores": self_scores,
                    "turn_p": turn_p, "turn_h": copy_turned(2, ps_a), "project_query": project_query,
                    "context_scores": context_scores, "turn_pc": turn_pc, "context_mix": context_mix,
                    "turn_w": copy_turned(3, ps_t), "turn_h2": copy_turned(4, ps_t), "turn_x1n": copy_turned(5, ps_t),
                    "project_heads": project_heads, "head_scores": head_scores, "head_mix": head_mix,
                    "turn_x2n": copy_turned(6, ps_t), "ffn_in": ffn_in, "turn_z": turn_z})

            @block.vector
            def _(dve):
                dve.wait_ge(weights_loaded, 16 * N_WEIGHTS)

                class Chain:

                    def __init__(self, unit, s, r):
                        self.unit, self.s, self.r, self.count = unit, s, r, 0

                    def __call__(self, ins):
                        self.count += 1
                        assert self.count <= STEPS[self.unit]
                        ins.then_inc(dve_step[self.s], 1)
                        dve.wait_ge(dve_step[self.s], steps_in_all * self.r + steps_before[self.unit] + self.count)

                    def end(self):
                        assert self.count == STEPS[self.unit], (self.unit, self.count)

                def moments(chain, s, r, n, rows, eps):
                    chain(nc.vector.bn_stats(stats[s][:], rows))
                    dve.sem_inc(stats_seen, 1)
                    chain(nc.vector.bn_aggr(mv[s][:], stats[s][:]))
                    nc.vector.tensor_scalar(var[s][:], mv[s][:, 1:2], eps, None, ALU.add).then_inc(var_ready[s], 1)
                    dve.wait_ge(rstd_ready[s], 7 * r + n)

                def plain_norm(s, out, rows):
                    return nc.vector.tensor_scalar(out, rows, mv[s][:, 0:1], rstd[s][:], ALU.subtract, ALU.mult)

                def affine_norm(chain, s, out, rows, g, b):
                    chain(nc.vector.scalar_tensor_tensor(out, rows, mv[s][:, 0:1], g, ALU.subtract, ALU.mult))
                    return nc.vector.scalar_tensor_tensor(out, out, rstd[s][:], b, ALU.mult, ALU.add)

                def xn(s, r, tile):
                    chain = Chain("xn", s, r)
                    dve.wait_ge(x_loaded[s], 16 * r + 16)
                    dve.wait_ge(out_stored[s], 16 * r + 16)
                    moments(chain, s, r, 1, x_in[s][:], 1e-5)
                    plain_norm(s, rows1[s][:], x_in[s][:]).then_inc(rows_ready[s], 1)
                    chain.end()

                def project_self(s, r, tile):
                    dve.wait_ge(q_done[s], 3 * r + 1)
                    nc.vector.tensor_copy(q_t[s][:].rearrange("p c r -> p (c r)"), ps_a[s][:]).then_inc(q_ready[s], 1)

                def self_scores(s, r, tile):
                    chain = Chain("self_scores", s, r)
                    dve.wait_ge(scored[s], 3 * r + 1)
                    dve.wait_ge(x2_stored[s], 16 * r + 16)
                    chain(nc.vector.tensor_tensor(rows3[s][:, 0:P], ps_a[s][:, 0:P], mask_self[:], ALU.add))
                    chain(nc.vector.reduce_max(top[s][:, 0:1], rows3[s][:, 0:P], AX.X))
                    nc.vector.tensor_scalar(ntop[s][:], top[s][:, 0:1], -XSCALE, None, ALU.mult
                                            ).then_inc(ntop_ready[s], 1)
                    chain.end()

                def self_mix(s, r, tile):
                    chain = Chain("self_mix", s, r)
                    dve.wait_ge(p_ready[s], 3 * r + 1)
                    chain(nc.vector.reciprocal(inv[s][:, 0:1], total[s][:, 0:1]))
                    dve.wait_ge(rows_done[s], 6 * r + 1)
                    chain(nc.vector.scalar_tensor_tensor(rows2[s][:], ps_t[s][:], inv[s][:, 0:1], rows1[s][:],
                                                         ALU.mult, ALU.add))
                    moments(chain, s, r, 2, rows2[s][:], 1e-3)
                    affine_norm(chain, s, rows2[s][:], rows2[s][:], gamma[:], beta[:]).then_inc(rows_ready[s], 1)
                    chain.end()

                def context_scores(s, r, tile):
                    chain = Chain("context_scores", s, r)
                    dve.wait_ge(scored[s], 3 * r + 2)
                    chain(nc.vector.reduce_max(top[s][:, 0:1], ps_a[s][:, 0:S], AX.X))
                    nc.vector.tensor_scalar(ntop[s][:], top[s][:, 0:1], -XSCALE, None, ALU.mult
                                            ).then_inc(ntop_ready[s], 1)
                    dve.wait_ge(p_ready[s], 3 * r + 2)
                    nc.vector.tensor_scalar(p_n[s][:, S:S + G], mask_entry[:], p_n[s][:, S - 1:S], None, ALU.mult
                                            ).then_inc(p4_ready[s], 1)
                    nc.vector.reciprocal(inv[s][:, 0:1], total[s][:, 0:1]).then_inc(p4_ready[s], 1)
                    chain.end()

                def context_out(s, r, tile):
                    chain = Chain("context_out", s, r)
                    dve.wait_ge(rows_done[s], 6 * r + 2)
                    chain(nc.vector.tensor_tensor(rows3[s][:], ps_a[s][:], rows2[s][:], ALU.add))
                    moments(chain, s, r, 3, rows3[s][:], 1e-3)
                    affine_norm(chain, s, rows1[s][:], rows3[s][:], gamma[:], beta[:]).then_inc(rows_ready[s], 1)
                    chain.end()

                def hidden(s, r, tile):
                    chain = Chain("hidden", s, r)
                    dve.wait_ge(rows_done[s], 6 * r + 3)
                    chain(nc.vector.tensor_tensor(rows3[s][:], ps_a[s][:], b1[:], ALU.add))
                    chain(nc.vector.scalar_tensor_tensor(rows3[s][:], rows3[s][:], 0.0, rows1[s][:], ALU.max, ALU.add))
                    moments(chain, s, r, 4, rows3[s][:], 1e-3)
                    chain(affine_norm(chain, s, rows2[s][:], rows3[s][:], gamma[:], beta[:]))
                    nc.vector.scalar_tensor_tensor(rows2[s][:], rows2[s][:], 0.0, x_in[s][:], ALU.max, ALU.add
                                                   ).then_inc(x_used[s], 1)
                    dve.wait_ge(x_used[s], r + 2)
                    moments(chain, s, r, 5, rows2[s][:], 1e-5)
                    plain_norm(s, rows1[s][:], rows2[s][:]).then_inc(rows_ready[s], 1)
                    chain.end()

                def project_heads(s, r, tile):
                    dve.wait_ge(k_done[s], r + 1)
                    for h in (2, 3):
                        nc.vector.tensor_copy(kbd[HD * h:HD * (h + 1), :, :, h, :],
                                              ps_a[s][HD * h:HD * (h + 1), :].rearrange("p (c g k) -> p c g k", c=C, g=G)
                                              ).then_inc(k_ready[s], 1)

                def by_head(ap):
                    return ap.rearrange("p (h k) -> p h k", k=T)

                def per_head(ap):
                    return ap.unsqueeze(2).to_broadcast([P, NH, T])

                def head_scores(s, r, tile):
                    chain = Chain("head_scores", s, r)
                    dve.wait_ge(scored[s], 3 * r + 3)
                    sc = by_head(rows3[s][:])
                    chain(nc.vector.tensor_tensor(sc, by_head(ps_a[s][:]),
                                                  mask_head[:].unsqueeze(1).to_broadcast([P, NH, T]), ALU.add))
                    chain(nc.vector.tensor_reduce(top[s][:], sc, AX.X, ALU.max))
                    nc.vector.tensor_tensor(sc, sc, per_head(top[s][:]), ALU.subtract).then_inc(heads_shifted[s], 1)
                    dve.wait_ge(p_ready[s], 3 * r + 3)
                    chain(nc.vector.tensor_reduce(total[s][:], by_head(rows1[s][:]), AX.X, ALU.add))
                    chain(nc.vector.reciprocal(inv[s][:], total[s][:]))
                    dve.wait_ge(decayed[s], r + 1)
                    chain(nc.vector.tensor_tensor(by_head(rows1[s][:]), sc, per_head(inv[s][:]), ALU.mult))
                    for g in range(G):
                        rows = slice(T * g, T * (g + 1))
                        nc.vector.transpose(pbd[rows, :, g, :], by_head(rows1[s][rows, :])).then_inc(pbd_ready[s], 1)
                    chain.end()

                def project_out(s, r, tile):
                    chain = Chain("project_out", s, r)
                    dve.wait_ge(rows_done[s], 6 * r + 4)
                    nc.vector.tensor_tensor(rows3[s][:], ps_a[s][:], rows2[s][:], ALU.add).then_inc(x2_ready[s], 1)
                    dve.wait_ge(x2_ready[s], r + 1)
                    moments(chain, s, r, 6, rows3[s][:], 1e-5)
                    plain_norm(s, rows1[s][:], rows3[s][:]).then_inc(rows_ready[s], 1)
                    chain.end()

                def ffn_in(s, r, tile):
                    chain = Chain("silu", s, r)
                    dve.wait_ge(rows_done[s], 6 * r + 5)
                    nc.vector.tensor_tensor(rows2[s][:], ps_a[s][:], b12[:], ALU.add).then_inc(u_ready[s], 1)
                    dve.wait_ge(gate_ready[s], r + 1)
                    z = v_n[s][:, H:]
                    chain(nc.vector.tensor_tensor(z, v_n[s][:, 0:H], rows2[s][:, H:], ALU.mult))
                    moments(chain, s, r, 7, z, 1e-5)
                    affine_norm(chain, s, z, z, ln_g[:], ln_b[:]).then_inc(rows_ready[s], 1)
                    chain.end()

                def ffn_out(s, r, tile):
                    dve.wait_ge(rows_done[s], 6 * r + 6)
                    chain = Chain("ffn_out", s, r)
                    chain(nc.vector.tensor_tensor(rows1[s][:], ps_a[s][:], b3[:], ALU.add))
                    nc.vector.tensor_tensor(rows1[s][:], rows1[s][:], rows3[s][:], ALU.add).then_inc(out_ready[s], 1)
                    chain.end()

                run_pipeline(dve, ORDER, {
                    "turn_xn": xn, "project_self": project_self, "self_scores": self_scores, "self_mix": self_mix,
                    "context_scores": context_scores, "context_out": context_out, "hidden": hidden,
                    "project_heads": project_heads, "head_scores": head_scores, "project_out": project_out,
                    "ffn_in": ffn_in, "ffn_out": ffn_out})

            @block.tensor
            def _(pe):
                for s in SLOTS:
                    pe.sem_inc(x_used[s], 1)

                def turn(out, rows, ready, k, n, chunks=C, lo=0):
                    def unit(s, r, tile):
                        pe.wait_ge(ready[s], k * r + n)
                        for c in range(chunks):
                            mm = nc.tensor.transpose(out[s][:, c * P:(c + 1) * P],
                                                     rows[s][:, lo + c * P:lo + (c + 1) * P], ident[:])
                        mm.then_inc(turned[s], 1)
                    return unit

                def product(out, left, w, lo=0, chunks=C):
                    for c in range(chunks):
                        mm = nc.tensor.matmul(out, left[:, c, :], w[:, c, lo:lo + D], start=(c == 0),
                                              stop=(c == chunks - 1))
                    return mm

                def product_t(out, left, w, lo=0):
                    for n in range(C):
                        for c in range(C):
                            mm = nc.tensor.matmul(out[:, n * P:(n + 1) * P], w[:, c, lo + n * P:lo + (n + 1) * P],
                                                  left[:, c, :], start=(c == 0), stop=(c == C - 1))
                    return mm

                def project_self(s, r, tile):
                    pe.wait_ge(act_t_ready[s], 7 * r + 1)
                    product_t(ps_a[s], act_t[s], wqk).then_inc(q_done[s], 1)
                    product(ps_t[s][:], act_t[s], wv).then_inc(v_done[s], 1)

                def self_scores(s, r, tile):
                    pe.wait_ge(q_ready[s], 3 * r + 1)
                    for c in range(C):
                        mm = nc.tensor.matmul(ps_a[s][:, 0:P], q_t[s][:, c, :], act_t[s][:, c, :],
                                              start=(c == 0), stop=(c == C - 1))
                    mm.then_inc(scored[s], 1)

                def turn_p(s, r, tile):
                    pe.wait_ge(p_ready[s], 3 * r + 1)
                    nc.tensor.transpose(ps_a[s][:, 0:P], p_n[s][:, 0:P], ident[:]).then_inc(p_turned[s], 1)

                def self_mix(s, r, tile):
                    pe.wait_ge(p_t_ready[s], 2 * r + 1)
                    pe.wait_ge(v_ready[s], 3 * r + 1)
                    nc.tensor.matmul(ps_t[s][:], p_t[s][:, 0:P], v_n[s][:], start=True, stop=True
                                     ).then_inc(rows_done[s], 1)

                def project_query(s, r, tile):
                    pe.wait_ge(act_t_ready[s], 7 * r + 2)
                    product_t(ps_t[s], act_t[s], wcqk).then_inc(q_done[s], 1)

                def context_scores(s, r, tile):
                    pe.wait_ge(q_ready[s], 3 * r + 2)
                    pe.wait_ge(ctx_t_loaded, 16 * tile + 16)
                    for c in range(C):
                        for g in range(G):
                            mm = nc.tensor.matmul(ps_a[s][T * g:T * (g + 1), 0:S], q_t[s][:, c, T * g:T * (g + 1)],
                                                  ctx_t[:, c, g, :], start=(c == 0), stop=(c == C - 1),
                                                  skip_group_check=True)
                    mm.then_inc(scored[s], 1)

                def turn_pc(s, r, tile):
                    pe.wait_ge(p_ready[s], 3 * r + 2)
                    for c in range(SC):
                        nc.tensor.transpose(ps_t[s][:, c * P:(c + 1) * P], p_n[s][:, c * P:(c + 1) * P], ident[:])
                    pe.wait_ge(p4_ready[s], 2 * r + 1)
                    nc.tensor.transpose(ps_t[s][0:G, SC * P:SC * P + P], p_n[s][:, S:S + G], ident[:]
                                        ).then_inc(p_turned[s], 1)

                def context_mix(s, r, tile):
                    pe.wait_ge(p_t_ready[s], 2 * r + 2)
                    pe.wait_ge(ctx_n_loaded, 32 * tile + 32)
                    nc.tensor.matmul(ps_a[s][:], p_t[s][0:G, SC * P:], ctx_last[:], start=True, stop=False,
                                     skip_group_check=True)
                    for c in range(SC):
                        for g in range(G):
                            mm = nc.tensor.matmul(ps_a[s][T * g:T * (g + 1), :],
                                                  p_t[s][:, c * P + T * g:c * P + T * (g + 1)], ctx_n[:, g, c, :],
                                                  start=False, stop=(c == SC - 1), skip_group_check=True)
                    mm.then_inc(v_done[s], 1)

                def context_out(s, r, tile):
                    pe.wait_ge(act_t_ready[s], 7 * r + 3)
                    product(ps_a[s][:], act_t[s], wcv).then_inc(rows_done[s], 1)

                def hidden(s, r, tile):
                    pe.wait_ge(act_t_ready[s], 7 * r + 4)
                    product(ps_a[s][:], act_t[s], w1).then_inc(rows_done[s], 1)

                def project_heads(s, r, tile):
                    pe.wait_ge(act_t_ready[s], 7 * r + 5)
                    product_t(ps_a[s], act_t[s], wattn, D).then_inc(k_done[s], 1)
                    product_t(ps_t[s], act_t[s], wattn, 0).then_inc(q_done[s], 1)
                    product(ps_v[:], act_t[s], wattn, 2 * D).then_inc(v_done[s], 1)

                def head_scores(s, r, tile):
                    pe.wait_ge(q_ready[s], 3 * r + 3)
                    pe.wait_ge(k_ready[s], 4 * r + 4)
                    for c in range(C):
                        for g in range(G):
                            mm = nc.tensor.matmul(ps_a[s][T * g:T * (g + 1), c * P:(c + 1) * P],
                                                  q_t[s][:, c, T * g:T * (g + 1)],
                                                  kbd[:, c, g, :, :].rearrange("p h k -> p (h k)"),
                                                  start=True, stop=True, skip_group_check=True)
                    mm.then_inc(scored[s], 1)

                def head_mix(s, r, tile):
                    pe.wait_ge(pbd_ready[s], 4 * r + 4)
                    pe.wait_ge(v_ready[s], 3 * r + 3)
                    for c in range(C):
                        for h in range(HPC):
                            head = c * HPC + h
                            mm = nc.tensor.matmul(ps_t[s][HD * h:HD * (h + 1), c * P:(c + 1) * P],
                                                  v_n[s][:, HD * head:HD * (head + 1)],
                                                  pbd[:, head, :, :].rearrange("p g q -> p (g q)"),
                                                  start=True, stop=True, skip_group_check=True)
                    mm.then_inc(y_done[s], 1)

                def project_out(s, r, tile):
                    pe.wait_ge(y_ready[s], r + 1)
                    product(ps_a[s][:], act_t[s], wproj).then_inc(rows_done[s], 1)

                def ffn_in(s, r, tile):
                    pe.wait_ge(act_t_ready[s], 7 * r + 6)
                    product(ps_a[s][:], act_t[s], w12).then_inc(rows_done[s], 1)

                def ffn_out(s, r, tile):
                    pe.wait_ge(act_t_ready[s], 7 * r + 7)
                    for c in range(HC):
                        mm = nc.tensor.matmul(ps_a[s][:], p_t[s][:, c * P:(c + 1) * P], w3[:, c, :], start=(c == 0),
                                              stop=(c == HC - 1))
                    mm.then_inc(rows_done[s], 1)

                run_pipeline(pe, ORDER, {
                    "turn_xn": turn(ps_t, rows1, rows_ready, 6, 1), "project_self": project_self,
                    "self_scores": self_scores, "turn_p": turn_p, "self_mix": self_mix,
                    "turn_h": turn(ps_a, rows2, rows_ready, 6, 2), "project_query": project_query,
                    "context_scores": context_scores, "turn_pc": turn_pc, "context_mix": context_mix,
                    "turn_w": turn(ps_t, v_n, v_ready, 3, 2), "context_out": context_out,
                    "turn_h2": turn(ps_t, rows1, rows_ready, 6, 3), "hidden": hidden,
                    "turn_x1n": turn(ps_t, rows1, rows_ready, 6, 4), "project_heads": project_heads,
                    "head_scores": head_scores, "head_mix": head_mix, "project_out": project_out,
                    "turn_x2n": turn(ps_t, rows1, rows_ready, 6, 5), "ffn_in": ffn_in,
                    "turn_z": turn(ps_t, v_n, rows_ready, 6, 6, HC, H), "ffn_out": ffn_out})

        fs = ctx.enter_context(ExitStack())
        ew12 = sb(fs, "ew12", [P, NE, C, 2 * H])
        ew3 = sb(fs, "ew3", [P, NE, HC, D])
        wg = sb(fs, "wg", [P, C, 1 + NE])
        sel_g = sb(fs, "sel_g", [P, H])
        sel_b = sb(fs, "sel_b", [P, H])
        bg = sb(fs, "bg", [P, 1 + NE])
        ebias = sb(fs, "ebias", [P, NE])
        eb12 = sb(fs, "eb12", [P, NE, 2 * H])
        eb3 = sb(fs, "eb3", [NE, D])
        falling = sb(fs, "falling", [P, NE])
        x2 = sb(fs, "e_x2", [P, D])
        xn = sb(fs, "e_xn", [P, D])
        xn_t = sb(fs, "e_xn_t", [P, C, P])
        u = sb(fs, "e_u", [P, 2 * H])
        gate = sb(fs, "e_gate", [P, H])
        z = sb(fs, "e_z", [P, H])
        z_t = sb(fs, "e_z_t", [P, HC, P])
        shared = sb(fs, "e_shared", [P, D])
        o = sb(fs, "e_o", [P, D])
        logits = sb(fs, "logits", [P, 1 + NE])
        scores = sb(fs, "scores", [P, 1 + NE])
        pick = sb(fs, "pick", [P, 4, NE])
        one = sb(fs, "one", [P, 8])
        coef_t = sb(fs, "coef_t", [NE, P])
        ps_u = ps_a[0:2]
        ps_turn, ps_gate, ps_sum, ps_shared, ps_coef = ps_t[0], ps_t[1], ps_a[2], ps_v, ps_e

        gates_loaded = sem("gates_loaded")
        ew_loaded = [sem(f"ew_loaded{e}") for e in range(NE)]
        e_x2_loaded, e_out_ready, e_out_stored = sem("e_x2_loaded"), sem("e_out_ready"), sem("e_out_stored")
        e_var, e_rstd = sem("e_var"), sem("e_rstd")
        xn_ready, xn_turned, xn_t_ready = sem("xn_ready"), sem("xn_turned"), sem("xn_t_ready")
        e_u_done, e_u_ready, e_gate_ready = sem("e_u_done"), sem("e_u_ready"), sem("e_gate_ready")
        e_z_ready, e_z_turned, e_z_t_ready = sem("e_z_ready"), sem("e_z_turned"), sem("e_z_t_ready")
        logits_done, logits_ready, scores_ready = sem("logits_done"), sem("logits_ready"), sem("scores_ready")
        margin_ready, shares_ready = sem("margin_ready"), sem("shares_ready")
        coef_ready, coef_turned, coef_t_ready = sem("coef_ready"), sem("coef_turned"), sem("coef_t_ready")
        shared_done, e_sum_done, e_step = sem("shared_done"), sem("e_sum_done"), sem("e_step")
        GLUS = 1 + NE
        E_STEPS = 16 + 5 * NE + 2

        block = fs.enter_context(nc.Block())

        def tiles_to_do(eng):
            return eng.value_load(redo[0:1, 0:1], min_val=1, max_val=TILES)

        def tile_of(eng, i):
            return eng.value_load(redo[0:1, bass.ds(i + 1, 1)], min_val=0, max_val=TILES - 1)

        @block.sync
        def _(sp):
            count = tiles_to_do(sp)
            for name, dst in (("sel_g", sel_g), ("sel_b", sel_b), ("bg", bg), ("ebias", ebias), ("falling", falling)):
                sp.dma_start(dst[:], a[name].partition_broadcast(P)).then_inc(gates_loaded, 16)
            for name, dst in (("wg", wg), ("eb3", eb3)):
                sp.dma_start(dst[:], a[name]).then_inc(gates_loaded, 16)
            sp.dma_start(eb12[:], a["eb12"].partition_broadcast(P)).then_inc(gates_loaded, 16)
            for e in range(NE):
                sp.dma_start(ew12[:, e], a["ew12"][:, e]).then_inc(ew_loaded[e], 16)
                sp.dma_start(ew3[:, e], a["ew3"][:, e]).then_inc(ew_loaded[e], 16)
            with sp.Fori(0, count) as i:
                tile = tile_of(sp, i)
                sp.dma_start(x2[:], a["x2"][bass.ds(tile, 1)].rearrange("a p d -> (a p) d")).then_inc(e_x2_loaded, 16)
                sp.wait_ge(e_out_ready, i + 1)
                sp.dma_start(a["out"][bass.ds(tile, 1)].rearrange("a p d -> (a p) d"), o[:]).then_inc(e_out_stored, 16)
                sp.wait_ge(e_out_stored, 16 * i + 16)
                sp.sem_inc(stats_seen, 1)
            sp.wait_ge(gates_loaded, 16 * 8)
            for e in range(NE):
                sp.wait_ge(ew_loaded[e], 32)

        @block.gpsimd
        def _(pool):
            count = tiles_to_do(pool)
            with pool.Fori(0, count) as i:
                for k in range(1 + GLUS):
                    pool.wait_ge(e_var, (1 + GLUS) * i + k + 1)
                    nc.gpsimd.tensor_tensor(rstd[0][:], var[0][:], mhalf[:], ALU.pow).then_inc(e_rstd, 1)

        @block.scalar
        def _(act):
            count = tiles_to_do(act)

            def gated(i, k):
                act.wait_ge(e_u_ready, GLUS * i + k + 1)
                nc.scalar.activation(gate[:], u[:, 0:H], ACT.Silu).then_inc(e_gate_ready, 1)

            def turned_z(i, k):
                act.wait_ge(e_z_turned, GLUS * i + k + 1)
                nc.scalar.copy(z_t[:].rearrange("p c r -> p (c r)"), ps_turn[:, 0:H]).then_inc(e_z_t_ready, 1)

            with act.Fori(0, count) as i:
                act.wait_ge(xn_turned, i + 1)
                nc.scalar.copy(xn_t[:].rearrange("p c r -> p (c r)"), ps_turn[:]).then_inc(xn_t_ready, 1)
                gated(i, 0)
                turned_z(i, 0)
                act.wait_ge(logits_ready, i + 1)
                nc.scalar.activation(scores[:], logits[:], ACT.Sigmoid).then_inc(scores_ready, 1)
                act.wait_ge(margin_ready, i + 1)
                nc.scalar.activation(one[:, 3:4], one[:, 2:3], ACT.Sigmoid, scale=-1.0).then_inc(shares_ready, 1)
                nc.scalar.activation(one[:, 4:5], one[:, 2:3], ACT.Sigmoid).then_inc(shares_ready, 1)
                act.wait_ge(coef_turned, i + 1)
                nc.scalar.copy(coef_t[:], ps_coef[0:NE, 0:P]).then_inc(coef_t_ready, 1)
                for k in range(1, GLUS):
                    gated(i, k)
                    turned_z(i, k)

        @block.vector
        def _(dve):
            count = tiles_to_do(dve)
            dve.wait_ge(gates_loaded, 16 * 8)
            with dve.Fori(0, count) as i:
                tile = tile_of(dve, i)
                steps = [0]

                def step(ins):
                    steps[0] += 1
                    ins.then_inc(e_step, 1)
                    dve.wait_ge(e_step, E_STEPS * i + steps[0])

                def moments(n, rows):
                    step(nc.vector.bn_stats(stats[0][:], rows))
                    dve.sem_inc(stats_seen, 1)
                    step(nc.vector.bn_aggr(mv[0][:], stats[0][:]))
                    nc.vector.tensor_scalar(var[0][:], mv[0][:, 1:2], 1e-5, None, ALU.add).then_inc(e_var, 1)
                    dve.wait_ge(e_rstd, (1 + GLUS) * i + n)

                def gated(k, bias):
                    dve.wait_ge(e_u_done, GLUS * i + k + 1)
                    if k:
                        dve.wait_ge(e_gate_ready, GLUS * i + k)
                    nc.vector.tensor_tensor(u[:], ps_u[k % 2][:], bias, ALU.add).then_inc(e_u_ready, 1)
                    dve.wait_ge(e_gate_ready, GLUS * i + k + 1)
                    if k:
                        dve.wait_ge(e_z_turned, GLUS * i + k)
                    step(nc.vector.tensor_tensor(z[:], gate[:], u[:, H:], ALU.mult))
                    moments(2 + k, z[:])

                dve.wait_ge(e_x2_loaded, 16 * i + 16)
                moments(1, x2[:])
                nc.vector.tensor_scalar(xn[:], x2[:], mv[0][:, 0:1], rstd[0][:], ALU.subtract, ALU.mult
                                        ).then_inc(xn_ready, 1)
                gated(0, b12[:])
                step(nc.vector.scalar_tensor_tensor(z[:], z[:], mv[0][:, 0:1], ln_g[:], ALU.subtract, ALU.mult))
                nc.vector.scalar_tensor_tensor(z[:], z[:], rstd[0][:], ln_b[:], ALU.mult, ALU.add
                                               ).then_inc(e_z_ready, 1)
                dve.wait_ge(shared_done, i + 1)
                step(nc.vector.tensor_tensor(shared[:], ps_shared[:], b3[:], ALU.add))
                step(nc.vector.tensor_tensor(o[:], shared[:], x2[:], ALU.add))
                dve.wait_ge(logits_done, i + 1)
                nc.vector.tensor_tensor(logits[:], ps_gate[:, 0:1 + NE], bg[:], ALU.add).then_inc(logits_ready, 1)
                dve.wait_ge(scores_ready, i + 1)
                step(nc.vector.tensor_tensor(pick[:, 0, :], scores[:, 1:], ebias[:], ALU.add))
                step(nc.vector.reduce_max(one[:, 0:1], pick[:, 0, :], AX.X))
                step(nc.vector.scalar_tensor_tensor(pick[:, 1, :], pick[:, 0, :], one[:, 0:1], falling[:],
                                                    ALU.is_ge, ALU.mult))
                step(nc.vector.reduce_max(one[:, 1:2], pick[:, 1, :], AX.X))
                step(nc.vector.tensor_scalar(pick[:, 2, :], falling[:], one[:, 1:2], None, ALU.is_equal))
                step(nc.vector.tensor_tensor(pick[:, 3, :], pick[:, 2, :], scores[:, 1:], ALU.mult))
                step(nc.vector.reduce_sum(one[:, 5:6], pick[:, 3, :], AX.X))
                nc.vector.tensor_tensor(one[:, 2:3], one[:, 5:6], scores[:, 0:1], ALU.subtract
                                        ).then_inc(margin_ready, 1)
                dve.wait_ge(shares_ready, 2 * i + 2)
                mine = sel[:, bass.ds(tile, 1)]
                step(nc.vector.tensor_tensor(one[:, 6:7], one[:, 4:5], mine, ALU.mult))
                step(nc.vector.scalar_tensor_tensor(one[:, 7:8], one[:, 3:4], -1.0, mine, ALU.add, ALU.mult))
                nc.vector.tensor_scalar(pick[:, 3, :], pick[:, 2, :], one[:, 6:7], None, ALU.mult
                                        ).then_inc(coef_ready, 1)
                step(nc.vector.scalar_tensor_tensor(o[:], shared[:], one[:, 7:8], o[:], ALU.mult, ALU.add))
                dve.wait_ge(coef_ready, i + 1)
                for k in range(1, GLUS):
                    gated(k, eb12[:, k - 1, :])
                    step(nc.vector.scalar_tensor_tensor(z[:], z[:], mv[0][:, 0:1], sel_g[:], ALU.subtract, ALU.mult))
                    step(nc.vector.scalar_tensor_tensor(z[:], z[:], rstd[0][:], sel_b[:], ALU.mult, ALU.add))
                    nc.vector.tensor_scalar(z[:], z[:], pick[:, 3, k - 1:k], None, ALU.mult).then_inc(e_z_ready, 1)
                assert steps[0] == E_STEPS, steps[0]
                dve.wait_ge(e_sum_done, i + 1)
                nc.vector.tensor_tensor(o[:], ps_sum[:], o[:], ALU.add).then_inc(e_out_ready, 1)

        @block.tensor
        def _(pe):
            count = tiles_to_do(pe)
            pe.wait_ge(gates_loaded, 16 * 8)

            def product(out, w):
                for c in range(C):
                    mm = nc.tensor.matmul(out, xn_t[:, c, :], w[:, c, :], start=(c == 0), stop=(c == C - 1))
                return mm

            def turn_z(i, k):
                pe.wait_ge(e_z_ready, GLUS * i + k + 1)
                for c in range(HC):
                    mm = nc.tensor.transpose(ps_turn[:, c * P:(c + 1) * P], z[:, c * P:(c + 1) * P], ident[:])
                mm.then_inc(e_z_turned, 1)
                pe.wait_ge(e_z_t_ready, GLUS * i + k + 1)

            with pe.Fori(0, count) as i:
                pe.wait_ge(xn_ready, i + 1)
                for c in range(C):
                    mm = nc.tensor.transpose(ps_turn[:, c * P:(c + 1) * P], xn[:, c * P:(c + 1) * P], ident[:])
                mm.then_inc(xn_turned, 1)
                pe.wait_ge(xn_t_ready, i + 1)
                product(ps_u[0][:], w12).then_inc(e_u_done, 1)
                product(ps_gate[:, 0:1 + NE], wg).then_inc(logits_done, 1)
                pe.wait_ge(ew_loaded[0], 32)
                product(ps_u[1][:], ew12[:, 0]).then_inc(e_u_done, 1)
                turn_z(i, 0)
                for c in range(HC):
                    mm = nc.tensor.matmul(ps_shared[:], z_t[:, c, :], w3[:, c, :], start=(c == 0), stop=(c == HC - 1))
                mm.then_inc(shared_done, 1)
                pe.wait_ge(coef_ready, i + 1)
                nc.tensor.transpose(ps_coef[0:NE, 0:P], pick[:, 3, :], ident[:]).then_inc(coef_turned, 1)
                pe.wait_ge(coef_t_ready, i + 1)
                nc.tensor.matmul(ps_sum[:], coef_t[:], eb3[:], start=True, stop=False, skip_group_check=True)
                for k in range(1, GLUS):
                    if k + 1 < GLUS:
                        pe.wait_ge(ew_loaded[k], 32)
                        pe.wait_ge(e_u_ready, GLUS * i + k)
                        product(ps_u[(k + 1) % 2][:], ew12[:, k]).then_inc(e_u_done, 1)
                    turn_z(i, k)
                    for c in range(HC):
                        mm = nc.tensor.matmul(ps_sum[:], z_t[:, c, :], ew3[:, k - 1, c, :], start=False,
                                              stop=(k == NE and c == HC - 1), skip_group_check=True)
                mm.then_inc(e_sum_done, 1)


def rows_on_partitions(w):
    return np.ascontiguousarray(w.reshape(-1, P, w.shape[-1]).transpose(1, 0, 2))


def layout(v):
    names = {k.replace("L0_", "", 1): np.asarray(x) for k, x in v.items()}
    cx = names["ctx_1024"].reshape(TILES, G, S, D)[::-1].reshape(B, S, D)
    w = {k[6:]: names[k] for k in names if k.startswith("xattn_")}
    f = {k[4:]: names[k] for k in names if k.startswith("ffn_")}
    at = {
        "x": names["x"].reshape(TILES, P, D)[::-1],
        "ctx_t": cx.reshape(TILES, G, S, C, P).transpose(0, 4, 3, 1, 2),
        "ctx_n": cx[:, :SC * P].reshape(TILES, G, SC, P, D).transpose(0, 3, 1, 2, 4),
        "ctx_last": cx[:, S - 1].reshape(TILES, G, D),
        "wq_t": rows_on_partitions(w["Wq"].T), "wk_t": rows_on_partitions(w["Wk"].T),
        "wcq_t": rows_on_partitions(w["Wcq"].T), "wck_t": rows_on_partitions(w["Wck"].T),
        "wv": rows_on_partitions(w["Wv"]), "wcv": rows_on_partitions(w["Wcv"]), "w1": rows_on_partitions(w["W1"]),
        "wattn": rows_on_partitions(names["attn_W_attn"]), "wproj": rows_on_partitions(names["attn_W_proj"]),
        "gamma": w["gamma"], "beta": w["beta"], "b1": w["b1"],
        "index_b": f["index_b"].reshape(P, MC), "index_t": f["index_t"].reshape(P, MC),
        "w12": rows_on_partitions(np.concatenate([f["sw1"], f["sw2"]]).T), "w3": rows_on_partitions(f["sw3"].T),
        "b12": np.concatenate([f["sb1"], f["sb2"]]), "b3": f["sb3"], "ln_g": f["s_ln_g"], "ln_b": f["s_ln_b"],
        "wg": rows_on_partitions(np.concatenate([f["sg_w"], f["eg_w"]]).T),
        "bg": np.concatenate([f["sg_b"], f["eg_b"]]), "ebias": f["exp_bias"],
        "ew12": np.concatenate([f["ew1"], f["ew2"]], axis=1).reshape(NE, 2 * H, C, P).transpose(3, 0, 2, 1),
        "ew3": f["ew3"].reshape(NE, D, HC, P).transpose(3, 0, 2, 1),
        "eb12": np.concatenate([f["eb1"], f["eb2"]], axis=1), "eb3": f["eb3"],
        "sel_g": f["sel_ln_g"], "sel_b": f["sel_ln_b"],
    }
    r = np.arange(P)
    at["ident"] = np.eye(P, dtype=np.float32)
    at["entry_of"] = np.arange(B, dtype=np.float32).reshape(TILES, G)[::-1].reshape(B)
    at["upto"] = np.triu(np.ones((TILES, TILES), np.float32))
    at["nth"] = np.arange(1, TILES + 1, dtype=np.float32)
    at["tile_id"] = np.arange(TILES, dtype=np.float32).reshape(TILES, 1)
    at["iota_t"] = np.arange(T, dtype=np.float32)
    at["mask_self"] = np.where((r[:, None] // T == r[None, :] // T) & (r[None, :] <= r[:, None]), 0.0, NEG)
    at["mask_head"] = np.where(r[None, :T] <= r[:, None] % T, 0.0, NEG)
    at["mask_entry"] = r[:, None] // T == np.arange(G)[None, :]
    at["falling"] = np.arange(NE, 0, -1)
    echoic, length = 16, 1024
    fading = 1.0 - np.linspace(0.0, 1.0, length - echoic + 1) ** (1.0 / np.e)
    weight = np.concatenate([np.ones(echoic - 1), fading])
    at["decay"] = weight[np.clip(r[:, None] % T - r[None, :T], 0, T - 1)]
    for k in ("mask_self", "mask_head", "mask_entry", "falling", "decay"):
        at[k] = at[k].astype(np.float32)
    return {k: np.ascontiguousarray(x) for k, x in at.items()}


def kernel(**inputs):
    import concourse.bacc as bacc
    from concourse.bass_utils import run_bass_kernel_spmd

    nc = bacc.Bacc("TRN2", target_bir_lowering=False, num_devices=1)
    arrays = {f"in_{k}": x for k, x in layout(inputs).items()}
    a = {k[3:]: nc.dram_tensor(k, x.shape, mybir.dt.from_np(x.dtype), kind="ExternalInput").ap()
         for k, x in arrays.items()}
    a["out"] = nc.dram_tensor("out_0", (TILES, P, D), F32, kind="ExternalOutput").ap()
    a["x2"] = nc.dram_tensor("x2_scratch", (TILES, P, D), F32, kind="Internal").ap()
    build(nc, a)
    r = run_bass_kernel_spmd(nc, [arrays], core_ids=[0])
    return np.ascontiguousarray(r.results[0]["out_0"][::-1]).reshape(B, T, D)
```

```python
from contextlib import ExitStack

import numpy as np

import concourse.bass as bass
from concourse import mybir

F32 = mybir.dt.float32
BF16 = mybir.dt.bfloat16
F16 = mybir.dt.float16
I32 = mybir.dt.int32
ALU = mybir.AluOpType
ACT = mybir.ActivationFunctionType
AX = mybir.AxisListType

P = 128
B, T, D = 128, 32, 512
S = 257
G = P // T
TILES = B // G
C = D // P
SC = (S - 1) // P
NH = 16
HD = D // NH
HPC = P // HD
H = 256
HC = H // P
NE = 8
M = 1024
MC = M // P
NEG = -1.0e30
XSCALE = float(D) ** -0.5
HSCALE = float(HD) ** -0.5
SLOTN = 3
SLOTS = tuple(range(SLOTN))
K_WQK, K_WV, K_WATTN, K_W12, K_W1, K_W3, K_PLAIN, K_AFFINE, K_Z, K_WCQK = range(10)
NSCALE = 10
SCALED_TOP = 14
EXPONENT = 0x7F800000



ORDER = {
    "pe": [(0, "turn_xn"), (2, "project_v"), (0, "project_self"), (1, "context_out"), (0, "self_scores"),
        (0, "value_self"), (0, "turn_p"), (2, "head_mix"), (0, "self_mix"), (1, "turn_h2"), (2, "project_out"),
        (0, "turn_h"), (1, "hidden"), (2, "turn_x2n"), (0, "project_query"), (2, "ffn_in"), (0, "context_scores"),
        (1, "turn_x1n"), (1, "project_k"), (2, "turn_z"), (1, "project_q"), (0, "turn_pc"), (2, "ffn_out"),
        (0, "context_mix"), (1, "head_scores"), (0, "turn_w")],
    "dve": [(0, "turn_xn"), (2, "head_scores"), (0, "project_self"), (0, "self_scores"), (1, "context_out"),
        (0, "self_mix"), (2, "project_out"), (1, "hidden"), (2, "ffn_in"), (0, "context_scores"), (1, "project_k"),
        (2, "ffn_out")],
    "act": [(0, "turn_xn"), (2, "head_scores"), (0, "self_scores"), (2, "project_v"), (0, "value_self"),
        (0, "turn_p"), (2, "head_mix"), (1, "turn_h2"), (0, "turn_h"), (2, "turn_x2n"), (0, "project_query"),
        (2, "ffn_in"), (1, "turn_x1n"), (0, "context_scores"), (1, "project_k"), (2, "turn_z"), (1, "project_q"),
        (0, "turn_pc"), (0, "context_mix"), (0, "turn_w")],
    "pool": [(0, "turn_xn"), (2, "head_scores"), (1, "context_out"), (0, "self_mix"), (1, "turn_h2"),
        (2, "project_out"), (0, "turn_h"), (2, "turn_x2n"), (1, "hidden"), (1, "turn_x1n"), (2, "ffn_in"),
        (2, "turn_z")],
}
STEPS = {"xn": 2, "self_scores": 2, "self_mix": 5, "context_scores": 1, "context_out": 4, "hidden": 8,
         "head_scores": 5, "project_out": 2, "silu": 4, "ffn_out": 1}


def run_pipeline(eng, order, work):
    lags = [lag for lag, name in order if name in work]
    full = (TILES - max(lags)) // SLOTN * SLOTN

    def step(n, i):
        for lag, name in order:
            if name in work:
                tile = n - lag
                if i is not None or 0 <= tile < TILES:
                    round_, at = (tile // SLOTN, tile) if i is None else (i + tile // SLOTN, SLOTN * i + tile)
                    work[name](tile % SLOTN, round_, at)

    for n in range(min(lags), max(lags)):
        step(n, None)
    with eng.Fori(0, full // SLOTN) as i:
        for n in range(max(lags), max(lags) + SLOTN):
            step(n, i)
    for n in range(max(lags) + full, TILES + max(lags)):
        step(n, None)


def build(nc, a):
    ctx = ExitStack()
    with ctx:
        def sem(name):
            return ctx.enter_context(nc.semaphore(name))

        def sems(name):
            return [sem(f"{name}{s}") for s in SLOTS]

        def sb(stack, name, shape, dt=F32):
            return stack.enter_context(nc.sbuf_tensor(name, shape, dt))

        def slots(stack, name, shape, dt=F32):
            return [sb(stack, f"{name}{s}", shape, dt) for s in SLOTS]

        ps_t = [ctx.enter_context(nc.psum_tensor(f"ps_t{s}", [P, 512], F32)) for s in SLOTS]
        ps_a = [ctx.enter_context(nc.psum_tensor(f"ps_a{s}", [P, 512], F32)) for s in SLOTS]
        ps_v = ctx.enter_context(nc.psum_tensor("ps_v", [P, 512], F32))
        ps_e = ctx.enter_context(nc.psum_tensor("ps_e", [P, 512], F32))

        ident = sb(ctx, "ident", [P, P])
        sel = sb(ctx, "sel", [P, TILES])
        redo = sb(ctx, "redo", [1, 2 + TILES], I32)
        mhalf = sb(ctx, "mhalf", [P, 1])
        b12 = sb(ctx, "b12", [P, 2 * H])
        b3 = sb(ctx, "b3", [P, D])
        ln_g = sb(ctx, "ln_g", [P, H])
        ln_b = sb(ctx, "ln_b", [P, H])
        stats = slots(ctx, "stats", [P, 6])
        mv = slots(ctx, "mv", [P, 2])
        var = slots(ctx, "var", [P, 1])
        rstd = slots(ctx, "rstd", [P, 1])

        late_loaded = sem("late_loaded")
        consts_ready = sem("consts_ready")
        stats_seen = sem("stats_seen")
        at = ExitStack()
        with at:
            wqk = sb(at, "wqk", [P, 2, C, D], F16)
            wcqk = sb(at, "wcqk", [P, 2, C, D], F16)
            wv = sb(at, "wv", [P, 2, C, D], F16)
            w1 = sb(at, "w1", [P, 2, C, D], F16)
            wattn = sb(at, "wattn", [P, 2, C, 3 * D], F16)
            w12 = sb(at, "w12_parts", [P, 2, C, 2 * H], F16)
            w3 = sb(at, "w3_parts", [P, 2, HC, D], F16)
            scale = sb(at, "scale", [P, NSCALE])
            unscale = sb(at, "unscale", [P, NSCALE])
            wcv = sb(at, "wcv", [P, C, D])
            wproj = sb(at, "wproj", [P, C, D])
            gamma = sb(at, "gamma", [P, D])
            beta = sb(at, "beta", [P, D])
            b1 = sb(at, "b1", [P, D])
            mask_self = sb(at, "mask_self", [P, P])
            mask_head = sb(at, "mask_head", [P, T])
            decay = sb(at, "decay", [P, T])
            mask_entry = sb(at, "mask_entry", [P, G])
            kbd = sb(at, "kbd", [P, C, G, HPC, T])
            pbd = sb(at, "pbd", [P, NH, G, T])

            qk_loaded = [sem("wqk_loaded"), sem("wcqk_loaded")]
            idx_loaded, idx_step = sem("idx_loaded"), sem("idx_step")
            onehots_ready, sel_counted, sel_ready = sem("onehots_ready"), sem("sel_counted"), sem("sel_ready")
            product_done, product_copied = sem("product_done"), sem("product_copied")
            peaks_ready, scale_step, halved = sem("peaks_ready"), sem("scale_step"), sem("halved")
            rows_loaded, wv_w1_loaded = sem("rows_loaded"), sem("wv_w1_loaded")
            wattn_w3_loaded, w12_loaded = sem("wattn_w3_loaded"), sem("w12_loaded")
            list_step = sem("list_step")
            with ExitStack() as st:
                wqk_f = sb(st, "wqk_f", [P, C, D])
                wv_f = sb(st, "wv_f", [P, C, D])
                w1_f = sb(st, "w1_f", [P, C, D])
                wattn_f = sb(st, "wattn_f", [P, C, 3 * D])
                w3_f = sb(st, "w3_f", [P, HC, D])
                peak = sb(st, "peak", [P, NSCALE + 2])
                spot = sb(st, "spot", [NSCALE, 2])
                diag = sb(st, "diag", [NSCALE, NSCALE])
                ones_wide = sb(st, "ones_wide", [NSCALE, P])
                power = sb(st, "power", [P, NSCALE])
                wq_t = [sb(st, f"wq_t{n}", [P, C, D]) for n in range(2)]
                wk_t = [sb(st, f"wk_t{n}", [P, C, D]) for n in range(2)]
                wcqk_f, w12_f = wq_t[0], wk_t[0]
                entry_of = sb(st, "entry_of", [P, B])
                iota_t = sb(st, "iota_t", [P, T])
                idx_i = sb(st, "idx_i", [P, 2, MC], I32)
                idx = sb(st, "idx", [P, 2, MC])
                idx_neg = sb(st, "idx_neg", [P, 2, MC])
                hot_b = sb(st, "hot_b", [P, MC, B], BF16)
                hot_t = sb(st, "hot_t", [P, MC, T], BF16)
                ones = sb(st, "ones", [P, 1])
                any_row = sb(st, "any_row", [TILES, 1])
                upto = sb(st, "upto", [TILES, TILES])
                nth = sb(st, "nth", [TILES, TILES])
                nth_hot = sb(st, "nth_hot", [TILES, TILES])
                tile_id = sb(st, "tile_id", [TILES, 1])

                PRODUCT_BANKS = (ps_a[0], ps_a[1], ps_t[0], ps_t[1])
                PART_BATCHES = (((K_WQK, wqk_f, wqk), (K_WV, wv_f, wv), (K_W1, w1_f, w1), (K_WATTN, wattn_f, wattn),
                                 (K_W12, w12_f, w12), (K_W3, w3_f, w3)), ((K_WCQK, wcqk_f, wcqk),))

                block = st.enter_context(nc.Block())

                @block.sync
                def _(sp):
                    sp.dma_start(wq_t[0][:], a["wq_t"]).then_inc(qk_loaded[0], 16)
                    sp.dma_start(wk_t[0][:], a["wk_t"]).then_inc(qk_loaded[0], 16)
                    sp.dma_start(idx_i[:, 0, :], a["index_b"]).then_inc(idx_loaded, 16)
                    sp.dma_start(idx_i[:, 1, :], a["index_t"]).then_inc(idx_loaded, 16)
                    sp.dma_start(entry_of[:], a["entry_of"].partition_broadcast(P)).then_inc(idx_loaded, 16)
                    sp.dma_start(iota_t[:], a["iota_t"].partition_broadcast(P)).then_inc(idx_loaded, 16)
                    sp.dma_start(upto[:], a["upto"]).then_inc(idx_loaded, 16)
                    sp.dma_start(nth[:], a["nth"].partition_broadcast(TILES)).then_inc(idx_loaded, 16)
                    sp.dma_start(tile_id[:], a["tile_id"]).then_inc(idx_loaded, 16)
                    for name, dst in (("gamma", gamma), ("beta", beta), ("ln_g", ln_g), ("ln_b", ln_b)):
                        sp.dma_start(dst[:], a[name].partition_broadcast(P)).then_inc(rows_loaded, 16)
                    sp.dma_start(ident[:], a["ident"]).then_inc(rows_loaded, 16)
                    sp.dma_start(wv_f[:], a["wv"]).then_inc(wv_w1_loaded, 16)
                    sp.dma_start(w1_f[:], a["w1"]).then_inc(wv_w1_loaded, 16)
                    sp.dma_start(wq_t[1][:], a["wcq_t"]).then_inc(qk_loaded[1], 16)
                    sp.dma_start(wk_t[1][:], a["wck_t"]).then_inc(qk_loaded[1], 16)
                    sp.dma_start(wattn_f[:], a["wattn"]).then_inc(wattn_w3_loaded, 16)
                    sp.dma_start(w3_f[:], a["w3"]).then_inc(wattn_w3_loaded, 16)
                    sp.wait_ge(product_done, C)
                    sp.dma_start(w12_f[:], a["w12"]).then_inc(w12_loaded, 16)
                    for name, dst in (("wcv", wcv), ("wproj", wproj), ("mask_self", mask_self),
                                      ("mask_head", mask_head), ("decay", decay), ("mask_entry", mask_entry)):
                        sp.dma_start(dst[:], a[name]).then_inc(late_loaded, 16)
                    for name, dst in (("b1", b1), ("b12", b12), ("b3", b3)):
                        sp.dma_start(dst[:], a[name].partition_broadcast(P)).then_inc(late_loaded, 16)

                @block.gpsimd
                def _(pool):
                    nc.gpsimd.memset(kbd[:], 0.0).then_inc(consts_ready, 1)
                    nc.gpsimd.memset(pbd[:], 0.0).then_inc(consts_ready, 1)
                    nc.gpsimd.memset(mhalf[:], -0.5).then_inc(consts_ready, 1)
                    nc.gpsimd.memset(ones_wide[:], 1.0).then_inc(consts_ready, 1)
                    pool.wait_ge(consts_ready, 5)

                @block.vector
                def _(dve):
                    steps = [0]

                    def step(ins):
                        steps[0] += 1
                        ins.then_inc(idx_step, 1)
                        dve.wait_ge(idx_step, steps[0])

                    nc.vector.memset(ones[:], 1.0).then_inc(consts_ready, 1)
                    nc.vector.memset(redo[:, 1 + TILES:], 0)
                    dve.wait_ge(idx_loaded, 16 * 7)
                    step(nc.vector.tensor_copy(idx[:], idx_i[:]))
                    for k, size in ((0, B), (1, T)):
                        step(nc.vector.tensor_scalar(idx_neg[:, k, :], idx[:, k, :], 0.0, float(size), ALU.is_lt,
                                                     ALU.mult))
                    step(nc.vector.tensor_tensor(idx[:], idx[:], idx_neg[:], ALU.add))
                    for k, hot, values, size in ((0, hot_b, entry_of, B), (1, hot_t, iota_t, T)):
                        nc.vector.tensor_tensor(hot[:], values[:].unsqueeze(1).to_broadcast([P, MC, size]),
                                                idx[:, k, :].unsqueeze(2).to_broadcast([P, MC, size]),
                                                ALU.is_equal).then_inc(onehots_ready, 1)
                    def largest(column, w):
                        return nc.vector.tensor_reduce(peak[:, column:column + 1], w, AX.X, ALU.max,
                                                       apply_absolute_value=True)

                    def flat(w):
                        return w[:].rearrange("p c n -> p (c n)")

                    nc.vector.memset(peak[:, K_PLAIN:K_PLAIN + 1], D ** 0.5)
                    dve.wait_ge(rows_loaded, 16 * 5)
                    for column, w in ((K_AFFINE, gamma), (NSCALE, beta), (K_Z, ln_g), (NSCALE + 1, ln_b)):
                        last = largest(column, w[:])
                    step(last)
                    nc.vector.scalar_tensor_tensor(peak[:, K_AFFINE:K_AFFINE + 1], peak[:, K_AFFINE:K_AFFINE + 1],
                                                   D ** 0.5, peak[:, NSCALE:NSCALE + 1], ALU.mult, ALU.add)
                    nc.vector.scalar_tensor_tensor(peak[:, K_Z:K_Z + 1], peak[:, K_Z:K_Z + 1],
                                                   H ** 0.5, peak[:, NSCALE + 1:NSCALE + 2], ALU.mult, ALU.add)
                    dve.wait_ge(wv_w1_loaded, 32)
                    largest(K_WV, flat(wv_f))
                    largest(K_W1, flat(w1_f))
                    dve.wait_ge(product_copied, C)
                    largest(K_WQK, flat(wqk_f))
                    dve.wait_ge(wattn_w3_loaded, 32)
                    largest(K_WATTN, flat(wattn_f))
                    largest(K_W3, flat(w3_f))
                    dve.wait_ge(w12_loaded, 16)
                    largest(K_W12, flat(w12_f)).then_inc(peaks_ready, 1)

                    def powers(lo, hi, seen):
                        n = hi - lo
                        dve.wait_ge(scale_step, seen + 1)
                        nc.vector.reduce_max(spot[0:n, 0:1], ps_e[0:n, P:2 * P], AX.X).then_inc(scale_step, 1)
                        dve.wait_ge(scale_step, seen + 2)
                        nc.vector.tensor_scalar(diag[0:n, 0:n], ident[0:n, 0:n], spot[0:n, 0:1], None, ALU.mult
                                                ).then_inc(scale_step, 1)
                        dve.wait_ge(scale_step, seen + 4)
                        here = slice(lo, hi)
                        step(nc.vector.tensor_scalar(power[:, here], ps_e[:, 2 * P:2 * P + n], 1e-30, None, ALU.max))
                        step(nc.vector.tensor_scalar(power[:, here].bitcast(I32), power[:, here].bitcast(I32), EXPONENT,
                                                     None, ALU.bitwise_and))
                        step(nc.vector.tensor_scalar(scale[:, here].bitcast(I32), power[:, here].bitcast(I32), -1.0,
                                                     float((2 * 127 + SCALED_TOP) << 23), ALU.mult, ALU.add))
                        step(nc.vector.tensor_scalar(unscale[:, here].bitcast(I32), scale[:, here].bitcast(I32), -1.0,
                                                     float((2 * 127) << 23), ALU.mult, ALU.add))

                    def with_rows(lo, hi, rows):
                        return nc.vector.tensor_scalar(unscale[:, lo:hi], unscale[:, lo:hi], unscale[:, rows:rows + 1],
                                                       None, ALU.mult)

                    def remainders(batch, seen):
                        for n, (k, w_f, parts) in enumerate(batch):
                            dve.wait_ge(halved, seen + n + 1)
                            nc.vector.scalar_tensor_tensor(parts[:, 1], w_f[:], scale[:, k:k + 1], parts[:, 0],
                                                           ALU.mult, ALU.subtract)

                    powers(0, K_WCQK, 0)
                    with_rows(K_WQK, K_W1, K_PLAIN)
                    with_rows(K_W1, K_W3, K_AFFINE)
                    with_rows(K_W3, K_PLAIN, K_Z).then_inc(scale_step, 1)
                    dve.wait_ge(product_copied, 2 * C)
                    largest(K_WCQK, flat(wcqk_f)).then_inc(peaks_ready, 1)
                    powers(K_WCQK, NSCALE, 5)
                    with_rows(K_WCQK, NSCALE, K_AFFINE).then_inc(scale_step, 1)
                    remainders(PART_BATCHES[0], 0)
                    remainders(PART_BATCHES[1], len(PART_BATCHES[0]))
                    dve.wait_ge(sel_counted, 1)
                    nc.vector.tensor_scalar(sel[:], ps_v[:, 0:TILES], 0.0, None, ALU.is_gt).then_inc(sel_ready, 1)
                    dve.wait_ge(list_step, 1)
                    nc.vector.tensor_scalar(any_row[:], ps_e[0:TILES, 0:1], 0.0, None, ALU.is_gt).then_inc(list_step, 1)
                    dve.wait_ge(list_step, 4)
                    nc.vector.scalar_tensor_tensor(nth_hot[:], nth[:], ps_e[0:TILES, 1:2],
                                                   any_row[:].to_broadcast([TILES, TILES]), ALU.is_equal, ALU.mult
                                                   ).then_inc(list_step, 1)
                    dve.wait_ge(list_step, 6)
                    nc.vector.tensor_scalar(redo[:, 0:1], ps_e[0:1, 2:3], 1.0, None, ALU.max)
                    nc.vector.tensor_copy(redo[:, 1:1 + TILES], ps_e[0:1, 4:4 + TILES])

                @block.scalar
                def _(act):
                    for n, w in ((0, wqk_f), (1, wcqk_f)):
                        for c in range(C):
                            act.wait_ge(product_done, n * C + c + 1)
                            nc.scalar.copy(w[:, c, :], PRODUCT_BANKS[c][:]).then_inc(product_copied, 1)
                    for batch in PART_BATCHES:
                        for k, w_f, parts in batch:
                            act.wait_ge(scale_step, 5 if k != K_WCQK else 10)
                            nc.scalar.activation(parts[:, 0], w_f[:], ACT.Copy, scale=scale[:, k:k + 1]
                                                 ).then_inc(halved, 1)

                @block.tensor
                def _(pe):
                    def product(n):
                        pe.wait_ge(qk_loaded[n], 32)
                        for c in range(C):
                            if n:
                                pe.wait_ge(product_copied, c + 1)
                            for d in range(C):
                                mm = nc.tensor.matmul(PRODUCT_BANKS[c][:], wq_t[n][:, d, c * P:(c + 1) * P],
                                                      wk_t[n][:, d, :], start=(d == 0), stop=(d == C - 1))
                            mm.then_inc(product_done, 1)

                    product(0)
                    pe.wait_ge(onehots_ready, 2)
                    for g in range(G):
                        for c in range(MC):
                            mm = nc.tensor.matmul(ps_v[T * g:T * (g + 1), 0:TILES], hot_t[:, c, :], hot_b[:, c, g::G],
                                                  start=(c == 0), stop=(c == MC - 1), skip_group_check=True)
                    mm.then_inc(sel_counted, 1)
                    product(1)

                    def spread(lo, hi, seen):
                        n = hi - lo
                        nc.tensor.transpose(ps_e[0:n, P:2 * P], peak[:, lo:hi], ident[:]).then_inc(scale_step, 1)
                        pe.wait_ge(scale_step, seen + 3)
                        nc.tensor.matmul(ps_e[:, 2 * P:2 * P + n], ones_wide[0:n, :], diag[0:n, 0:n], start=True,
                                         stop=True).then_inc(scale_step, 1)

                    pe.wait_ge(consts_ready, 5)
                    pe.wait_ge(peaks_ready, 1)
                    spread(0, K_WCQK, 0)
                    pe.wait_ge(peaks_ready, 2)
                    spread(K_WCQK, NSCALE, 5)
                    pe.wait_ge(sel_ready, 1)
                    pe.wait_ge(consts_ready, 5)
                    nc.tensor.matmul(ps_e[0:TILES, 0:1], sel[:], ones[:], start=True, stop=True).then_inc(list_step, 1)
                    pe.wait_ge(list_step, 2)
                    nc.tensor.matmul(ps_e[0:TILES, 1:2], upto[:], any_row[:], start=True, stop=True
                                     ).then_inc(list_step, 1)
                    nc.tensor.matmul(ps_e[0:1, 2:3], ones[0:TILES, :], any_row[:], start=True, stop=True
                                     ).then_inc(list_step, 1)
                    pe.wait_ge(list_step, 5)
                    nc.tensor.matmul(ps_e[0:1, 4:4 + TILES], tile_id[:], nth_hot[:], start=True, stop=True
                                     ).then_inc(list_step, 1)


            ctx_t = sb(at, "ctx_t", [P, C, G, S])
            ctx_n = sb(at, "ctx_n", [P, G, SC, D])
            ctx_last = sb(at, "ctx_last", [G, D])
            x_in = slots(at, "x_in", [P, D])
            rows1 = slots(at, "rows1", [P, D])
            rows2 = slots(at, "rows2", [P, D])
            rows3 = slots(at, "rows3", [P, D])
            act_h = slots(at, "act_h", [P, C, P], F16)
            act_l = slots(at, "act_l", [P, C, P], F16)
            act_t = slots(at, "act_t", [P, C, P])
            q_t = slots(at, "q_t", [P, C, P])
            v_n = slots(at, "v_n", [P, D])
            p_n = slots(at, "p_n", [P, S + G])
            p_t = slots(at, "p_t", [P, SC * P + P])
            top = slots(at, "top", [P, NH])
            ntop = slots(at, "ntop", [P, 1])
            total = slots(at, "total", [P, NH])
            inv = slots(at, "inv", [P, NH])

            x_loaded, x_used = sems("x_loaded"), sems("x_used")
            ctx_t_loaded, ctx_n_loaded = sem("ctx_t_loaded"), sem("ctx_n_loaded")
            var_ready, rstd_ready = sems("var_ready"), sems("rstd_ready")
            rows_ready = sems("rows_ready")
            turned = sems("turned")
            act_h_ready, act_l_ready = sems("act_h_ready"), sems("act_l_ready")
            act_t_ready = sems("act_t_ready")
            q_done, q_ready = sems("q_done"), sems("q_ready")
            v_done, v_ready = sems("v_done"), sems("v_ready")
            scored = sems("scored")
            ntop_ready = sems("ntop_ready")
            p_ready = sems("p_ready")
            p4_ready = sems("p4_ready")
            p_turned, p_t_ready = sems("p_turned"), sems("p_t_ready")
            rows_done = sems("rows_done")
            k_done, k_ready = sems("k_done"), sems("k_ready")
            heads_shifted = sems("heads_shifted")
            decayed, pbd_ready, y_done, y_ready = sems("decayed"), sems("pbd_ready"), sems("y_done"), sems("y_ready")
            u_ready, gate_ready = sems("u_ready"), sems("gate_ready")
            x2_ready, x2_stored = sems("x2_ready"), sems("x2_stored")
            out_ready, out_stored = sems("out_ready"), sems("out_stored")
            dve_step = sems("dve_step")
            steps_before, steps_in_all = {}, 0
            for name in STEPS:
                steps_before[name] = steps_in_all
                steps_in_all += STEPS[name]

            block = at.enter_context(nc.Block())

            @block.sync
            def _(sp):
                def plane(ap, tile):
                    if isinstance(tile, int):
                        return ap[tile]
                    names = "abcde"[:len(ap.shape)]
                    rest = " ".join(names[2:])
                    return ap[bass.ds(tile, 1)].rearrange(f"{' '.join(names)} -> ({names[0]} {names[1]}) {rest}")

                def load_x(s, r, tile):
                    sp.wait_ge(x_used[s], r + 1)
                    sp.dma_start(x_in[s][:], plane(a["x"], tile)).then_inc(x_loaded[s], 16)

                def load_ctx_t(s, r, tile):
                    if not (isinstance(tile, int) and tile == 0):
                        sp.wait_ge(scored[(s - 1) % SLOTN], 3 * (r - (s == 0)) + 2)
                    sp.dma_start(ctx_t[:], plane(a["ctx_t"], tile)).then_inc(ctx_t_loaded, 16)

                def load_ctx_n(s, r, tile):
                    if not (isinstance(tile, int) and tile == 0):
                        sp.wait_ge(v_done[(s - 1) % SLOTN], 3 * (r - (s == 0)) + 2)
                    sp.dma_start(ctx_n[:], plane(a["ctx_n"], tile)).then_inc(ctx_n_loaded, 16)
                    sp.dma_start(ctx_last[:], plane(a["ctx_last"], tile)).then_inc(ctx_n_loaded, 16)

                def store(s, r, tile):
                    sp.wait_ge(x2_ready[s], r + 1)
                    sp.dma_start(plane(a["x2"], tile), rows3[s][:]).then_inc(x2_stored[s], 16)
                    sp.wait_ge(out_ready[s], r + 1)
                    sp.dma_start(plane(a["out"], tile), rows2[s][:]).then_inc(out_stored[s], 16)

                for s in SLOTS:
                    sp.sem_inc(x2_stored[s], 16)
                    sp.sem_inc(out_stored[s], 16)
                run_pipeline(sp, [(0, "load_x"), (0, "load_ctx_t"), (3, "store"), (0, "load_ctx_n")],
                             {"load_x": load_x, "load_ctx_t": load_ctx_t, "load_ctx_n": load_ctx_n, "store": store})
                for s in SLOTS:
                    sp.wait_ge(x2_stored[s], 16 * (1 + len(range(s, TILES, SLOTN))))
                    sp.wait_ge(out_stored[s], 16 * (1 + len(range(s, TILES, SLOTN))))

            @block.gpsimd
            def _(pool):
                def inverse_std(n):
                    def unit(s, r, tile):
                        pool.wait_ge(var_ready[s], 7 * r + n)
                        nc.gpsimd.tensor_tensor(rstd[s][:], var[s][:], mhalf[:], ALU.pow).then_inc(rstd_ready[s], 1)
                    return unit

                def remainder(n, width=D):
                    def unit(s, r, tile):
                        pool.wait_ge(act_h_ready[s], 6 * r + n)
                        pool.wait_ge(act_t_ready[s], 7 * r + (n if n < 3 else n + 1))
                        chunks = slice(0, width // P)
                        nc.gpsimd.tensor_tensor(act_l[s][:, chunks], act_t[s][:, chunks], act_h[s][:, chunks],
                                                ALU.subtract).then_inc(act_l_ready[s], 1)
                    return unit

                def turn_xn(s, r, tile):
                    inverse_std(1)(s, r, tile)
                    remainder(1)(s, r, tile)

                def hidden(s, r, tile):
                    inverse_std(4)(s, r, tile)
                    inverse_std(5)(s, r, tile)

                def head_scores(s, r, tile):
                    pool.wait_ge(p_ready[s], 3 * r + 3)
                    nc.gpsimd.tensor_tensor(rows3[s][:].rearrange("p (h k) -> p h k", k=T),
                                            rows1[s][:].rearrange("p (h k) -> p h k", k=T),
                                            decay[:].unsqueeze(1).to_broadcast([P, NH, T]), ALU.mult
                                            ).then_inc(decayed[s], 1)

                run_pipeline(pool, ORDER["pool"], {
                    "turn_xn": turn_xn, "turn_h": remainder(2), "turn_h2": remainder(3),
                    "turn_x1n": remainder(4), "turn_x2n": remainder(5),
                    "turn_z": remainder(6, H), "self_mix": inverse_std(2), "context_out": inverse_std(3),
                    "hidden": hidden, "head_scores": head_scores, "project_out": inverse_std(6),
                    "ffn_in": inverse_std(7)})

            @block.scalar
            def _(act):
                def copy_hi(n, bank, k, width=D):
                    def unit(s, r, tile):
                        act.wait_ge(turned[s], 7 * r + n)
                        for copies, ready in ((act_h, act_h_ready), (act_t, act_t_ready)):
                            nc.scalar.activation(copies[s][:, 0:width // P].rearrange("p c r -> p (c r)"),
                                                 bank[s][:, 0:width], ACT.Copy, scale=scale[:, k:k + 1]
                                                 ).then_inc(ready[s], 1)
                    return unit

                def turn_w(s, r, tile):
                    act.wait_ge(turned[s], 7 * r + 3)
                    nc.scalar.copy(act_t[s][:].rearrange("p c r -> p (c r)"), ps_t[s][:]).then_inc(act_t_ready[s], 1)

                def value_self(s, r, tile):
                    act.wait_ge(v_done[s], 3 * r + 1)
                    nc.scalar.activation(v_n[s][:], ps_t[s][:], ACT.Copy, scale=unscale[:, K_WV:K_WV + 1]
                                         ).then_inc(v_ready[s], 1)

                def self_scores(s, r, tile):
                    act.wait_ge(ntop_ready[s], 2 * r + 1)
                    nc.scalar.activation(p_n[s][:, 0:P], rows3[s][:, 0:P], ACT.Exp, bias=ntop[s][:], scale=XSCALE,
                                         accum_out=total[s][:, 0:1]).then_inc(p_ready[s], 1)

                def turn_p(s, r, tile):
                    act.wait_ge(p_turned[s], 2 * r + 1)
                    nc.scalar.copy(p_t[s][:, 0:P], ps_a[s][:, 0:P]).then_inc(p_t_ready[s], 1)

                def project_query(s, r, tile):
                    act.wait_ge(q_done[s], 3 * r + 2)
                    nc.scalar.activation(q_t[s][:].rearrange("p c r -> p (c r)"), ps_t[s][:], ACT.Copy,
                                         scale=unscale[:, K_WCQK:K_WCQK + 1]).then_inc(q_ready[s], 1)

                def context_scores(s, r, tile):
                    act.wait_ge(ntop_ready[s], 2 * r + 2)
                    nc.scalar.activation(p_n[s][:, 0:S], ps_a[s][:, 0:S], ACT.Exp, bias=ntop[s][:], scale=XSCALE,
                                         accum_out=total[s][:, 0:1]).then_inc(p_ready[s], 1)

                def turn_pc(s, r, tile):
                    act.wait_ge(p_turned[s], 2 * r + 2)
                    nc.scalar.copy(p_t[s][:, 0:SC * P], ps_t[s][:, 0:SC * P])
                    nc.scalar.copy(p_t[s][0:G, SC * P:], ps_t[s][0:G, SC * P:SC * P + P]).then_inc(p_t_ready[s], 1)

                def context_mix(s, r, tile):
                    act.wait_ge(v_done[s], 3 * r + 2)
                    act.wait_ge(p4_ready[s], 2 * r + 2)
                    nc.scalar.activation(v_n[s][:], ps_a[s][:], ACT.Copy, scale=inv[s][:, 0:1]).then_inc(v_ready[s], 1)

                def project_k(s, r, tile):
                    act.wait_ge(k_done[s], r + 1)
                    for h in (0, 1):
                        rows = slice(HD * h, HD * (h + 1))
                        nc.scalar.activation(kbd[rows, :, :, h, :],
                                             ps_a[s][rows, :].rearrange("p (c g k) -> p c g k", c=C, g=G), ACT.Copy,
                                             scale=unscale[rows, K_WATTN:K_WATTN + 1]).then_inc(k_ready[s], 1)

                def project_q(s, r, tile):
                    act.wait_ge(q_done[s], 3 * r + 3)
                    nc.scalar.activation(q_t[s][:].rearrange("p c r -> p (c r)"), ps_t[s][:], ACT.Copy,
                                         scale=unscale[:, K_WATTN:K_WATTN + 1]).then_inc(q_ready[s], 1)

                def project_v(s, r, tile):
                    act.wait_ge(v_done[s], 3 * r + 3)
                    nc.scalar.activation(v_n[s][:], ps_v[:], ACT.Copy, scale=unscale[:, K_WATTN:K_WATTN + 1]
                                         ).then_inc(v_ready[s], 1)

                def head_scores(s, r, tile):
                    act.wait_ge(heads_shifted[s], r + 1)
                    nc.scalar.activation(rows1[s][:], rows3[s][:], ACT.Exp, scale=HSCALE).then_inc(p_ready[s], 1)

                def head_mix(s, r, tile):
                    act.wait_ge(y_done[s], r + 1)
                    nc.scalar.copy(act_t[s][:].rearrange("p c r -> p (c r)"), ps_t[s][:]).then_inc(y_ready[s], 1)

                def ffn_in(s, r, tile):
                    act.wait_ge(u_ready[s], r + 1)
                    nc.scalar.activation(v_n[s][:, 0:H], rows2[s][:, 0:H], ACT.Silu).then_inc(gate_ready[s], 1)

                run_pipeline(act, ORDER["act"], {
                    "turn_xn": copy_hi(1, ps_t, K_PLAIN), "value_self": value_self, "self_scores": self_scores,
                    "turn_p": turn_p, "turn_h": copy_hi(2, ps_a, K_AFFINE), "project_query": project_query,
                    "context_scores": context_scores, "turn_pc": turn_pc, "context_mix": context_mix,
                    "turn_w": turn_w, "turn_h2": copy_hi(4, ps_t, K_AFFINE), "turn_x1n": copy_hi(5, ps_t, K_PLAIN),
                    "project_k": project_k, "project_q": project_q, "project_v": project_v,
                    "head_scores": head_scores, "head_mix": head_mix, "turn_x2n": copy_hi(6, ps_t, K_PLAIN), "ffn_in": ffn_in,
                    "turn_z": copy_hi(7, ps_t, K_Z, H)})

            @block.vector
            def _(dve):
                dve.wait_ge(late_loaded, 16 * 9)

                class Chain:

                    def __init__(self, unit, s, r):
                        self.unit, self.s, self.r, self.count = unit, s, r, 0

                    def __call__(self, ins):
                        self.count += 1
                        assert self.count <= STEPS[self.unit]
                        ins.then_inc(dve_step[self.s], 1)
                        dve.wait_ge(dve_step[self.s], steps_in_all * self.r + steps_before[self.unit] + self.count)

                    def end(self):
                        assert self.count == STEPS[self.unit], (self.unit, self.count)

                def moments(chain, s, r, n, rows, eps):
                    chain(nc.vector.bn_stats(stats[s][:], rows))
                    dve.sem_inc(stats_seen, 1)
                    chain(nc.vector.bn_aggr(mv[s][:], stats[s][:]))
                    nc.vector.tensor_scalar(var[s][:], mv[s][:, 1:2], eps, None, ALU.add).then_inc(var_ready[s], 1)
                    dve.wait_ge(rstd_ready[s], 7 * r + n)

                def plain_norm(s, out, rows):
                    return nc.vector.tensor_scalar(out, rows, mv[s][:, 0:1], rstd[s][:], ALU.subtract, ALU.mult)

                def affine_norm(chain, s, out, rows, g, b):
                    chain(nc.vector.scalar_tensor_tensor(out, rows, mv[s][:, 0:1], g, ALU.subtract, ALU.mult))
                    return nc.vector.scalar_tensor_tensor(out, out, rstd[s][:], b, ALU.mult, ALU.add)

                def xn(s, r, tile):
                    chain = Chain("xn", s, r)
                    dve.wait_ge(x_loaded[s], 16 * r + 16)
                    moments(chain, s, r, 1, x_in[s][:], 1e-5)
                    plain_norm(s, rows1[s][:], x_in[s][:]).then_inc(rows_ready[s], 1)
                    chain.end()

                def project_self(s, r, tile):
                    dve.wait_ge(q_done[s], 3 * r + 1)
                    nc.vector.tensor_scalar(q_t[s][:].rearrange("p c r -> p (c r)"), ps_a[s][:],
                                            unscale[:, K_WQK:K_WQK + 1], None, ALU.mult).then_inc(q_ready[s], 1)

                def self_scores(s, r, tile):
                    chain = Chain("self_scores", s, r)
                    dve.wait_ge(scored[s], 3 * r + 1)
                    dve.wait_ge(x2_stored[s], 16 * r + 16)
                    chain(nc.vector.scalar_tensor_tensor(rows3[s][:, 0:P], ps_a[s][:, 0:P],
                                                         unscale[:, K_PLAIN:K_PLAIN + 1], mask_self[:], ALU.mult,
                                                         ALU.add))
                    chain(nc.vector.reduce_max(top[s][:, 0:1], rows3[s][:, 0:P], AX.X))
                    nc.vector.tensor_scalar(ntop[s][:], top[s][:, 0:1], -XSCALE, None, ALU.mult
                                            ).then_inc(ntop_ready[s], 1)
                    chain.end()

                def self_mix(s, r, tile):
                    chain = Chain("self_mix", s, r)
                    dve.wait_ge(p_ready[s], 3 * r + 1)
                    chain(nc.vector.reciprocal(inv[s][:, 0:1], total[s][:, 0:1]))
                    dve.wait_ge(rows_done[s], 6 * r + 1)
                    dve.wait_ge(out_stored[s], 16 * r + 16)
                    chain(nc.vector.scalar_tensor_tensor(rows2[s][:], ps_t[s][:], inv[s][:, 0:1], rows1[s][:],
                                                         ALU.mult, ALU.add))
                    moments(chain, s, r, 2, rows2[s][:], 1e-3)
                    affine_norm(chain, s, rows2[s][:], rows2[s][:], gamma[:], beta[:]).then_inc(rows_ready[s], 1)
                    chain.end()

                def context_scores(s, r, tile):
                    chain = Chain("context_scores", s, r)
                    dve.wait_ge(scored[s], 3 * r + 2)
                    chain(nc.vector.reduce_max(top[s][:, 0:1], ps_a[s][:, 0:S], AX.X))
                    nc.vector.tensor_scalar(ntop[s][:], top[s][:, 0:1], -XSCALE, None, ALU.mult
                                            ).then_inc(ntop_ready[s], 1)
                    dve.wait_ge(p_ready[s], 3 * r + 2)
                    nc.vector.tensor_scalar(p_n[s][:, S:S + G], mask_entry[:], p_n[s][:, S - 1:S], None, ALU.mult
                                            ).then_inc(p4_ready[s], 1)
                    nc.vector.reciprocal(inv[s][:, 0:1], total[s][:, 0:1]).then_inc(p4_ready[s], 1)
                    chain.end()

                def context_out(s, r, tile):
                    chain = Chain("context_out", s, r)
                    dve.wait_ge(rows_done[s], 6 * r + 2)
                    chain(nc.vector.tensor_tensor(rows3[s][:], ps_a[s][:], rows2[s][:], ALU.add))
                    moments(chain, s, r, 3, rows3[s][:], 1e-3)
                    affine_norm(chain, s, rows1[s][:], rows3[s][:], gamma[:], beta[:]).then_inc(rows_ready[s], 1)
                    chain.end()

                def hidden(s, r, tile):
                    chain = Chain("hidden", s, r)
                    dve.wait_ge(rows_done[s], 6 * r + 3)
                    chain(nc.vector.scalar_tensor_tensor(rows3[s][:], ps_a[s][:], unscale[:, K_W1:K_W1 + 1], b1[:],
                                                         ALU.mult, ALU.add))
                    chain(nc.vector.scalar_tensor_tensor(rows3[s][:], rows3[s][:], 0.0, rows1[s][:], ALU.max, ALU.add))
                    moments(chain, s, r, 4, rows3[s][:], 1e-3)
                    chain(affine_norm(chain, s, rows2[s][:], rows3[s][:], gamma[:], beta[:]))
                    nc.vector.scalar_tensor_tensor(rows2[s][:], rows2[s][:], 0.0, x_in[s][:], ALU.max, ALU.add
                                                   ).then_inc(x_used[s], 1)
                    dve.wait_ge(x_used[s], r + 2)
                    moments(chain, s, r, 5, rows2[s][:], 1e-5)
                    plain_norm(s, rows1[s][:], rows2[s][:]).then_inc(rows_ready[s], 1)
                    chain.end()

                def project_k(s, r, tile):
                    dve.wait_ge(k_done[s], r + 1)
                    for h in (2, 3):
                        rows = slice(HD * h, HD * (h + 1))
                        nc.vector.tensor_scalar(kbd[rows, :, :, h, :],
                                                ps_a[s][rows, :].rearrange("p (c g k) -> p c g k", c=C, g=G),
                                                unscale[rows, K_WATTN:K_WATTN + 1], None, ALU.mult
                                                ).then_inc(k_ready[s], 1)

                def by_head(ap):
                    return ap.rearrange("p (h k) -> p h k", k=T)

                def per_head(ap):
                    return ap.unsqueeze(2).to_broadcast([P, NH, T])

                def head_scores(s, r, tile):
                    chain = Chain("head_scores", s, r)
                    dve.wait_ge(scored[s], 3 * r + 3)
                    sc = by_head(rows3[s][:])
                    chain(nc.vector.tensor_tensor(sc, by_head(ps_a[s][:]),
                                                  mask_head[:].unsqueeze(1).to_broadcast([P, NH, T]), ALU.add))
                    chain(nc.vector.tensor_reduce(top[s][:], sc, AX.X, ALU.max))
                    nc.vector.tensor_tensor(sc, sc, per_head(top[s][:]), ALU.subtract).then_inc(heads_shifted[s], 1)
                    dve.wait_ge(p_ready[s], 3 * r + 3)
                    chain(nc.vector.tensor_reduce(total[s][:], by_head(rows1[s][:]), AX.X, ALU.add))
                    chain(nc.vector.reciprocal(inv[s][:], total[s][:]))
                    dve.wait_ge(decayed[s], r + 1)
                    chain(nc.vector.tensor_tensor(by_head(rows1[s][:]), sc, per_head(inv[s][:]), ALU.mult))
                    for g in range(G):
                        rows = slice(T * g, T * (g + 1))
                        nc.vector.transpose(pbd[rows, :, g, :], by_head(rows1[s][rows, :])).then_inc(pbd_ready[s], 1)
                    chain.end()

                def project_out(s, r, tile):
                    chain = Chain("project_out", s, r)
                    dve.wait_ge(rows_done[s], 6 * r + 4)
                    nc.vector.tensor_tensor(rows3[s][:], ps_a[s][:], rows2[s][:], ALU.add).then_inc(x2_ready[s], 1)
                    dve.wait_ge(x2_ready[s], r + 1)
                    moments(chain, s, r, 6, rows3[s][:], 1e-5)
                    plain_norm(s, rows1[s][:], rows3[s][:]).then_inc(rows_ready[s], 1)
                    chain.end()

                def ffn_in(s, r, tile):
                    chain = Chain("silu", s, r)
                    dve.wait_ge(rows_done[s], 6 * r + 5)
                    nc.vector.scalar_tensor_tensor(rows2[s][:], ps_a[s][:], unscale[:, K_W12:K_W12 + 1], b12[:],
                                                   ALU.mult, ALU.add).then_inc(u_ready[s], 1)
                    dve.wait_ge(gate_ready[s], r + 1)
                    z = v_n[s][:, H:]
                    chain(nc.vector.tensor_tensor(z, v_n[s][:, 0:H], rows2[s][:, H:], ALU.mult))
                    moments(chain, s, r, 7, z, 1e-5)
                    affine_norm(chain, s, z, z, ln_g[:], ln_b[:]).then_inc(rows_ready[s], 1)
                    chain.end()

                def ffn_out(s, r, tile):
                    dve.wait_ge(rows_done[s], 6 * r + 6)
                    chain = Chain("ffn_out", s, r)
                    chain(nc.vector.scalar_tensor_tensor(rows2[s][:], ps_a[s][:], unscale[:, K_W3:K_W3 + 1], b3[:],
                                                         ALU.mult, ALU.add))
                    nc.vector.tensor_tensor(rows2[s][:], rows2[s][:], rows3[s][:], ALU.add).then_inc(out_ready[s], 1)
                    chain.end()

                run_pipeline(dve, ORDER["dve"], {
                    "turn_xn": xn, "project_self": project_self, "self_scores": self_scores, "self_mix": self_mix,
                    "context_scores": context_scores, "context_out": context_out, "hidden": hidden,
                    "project_k": project_k, "head_scores": head_scores, "project_out": project_out,
                    "ffn_in": ffn_in, "ffn_out": ffn_out})

            @block.tensor
            def _(pe):
                pe.wait_ge(late_loaded, 16 * 9)
                for s in SLOTS:
                    pe.sem_inc(x_used[s], 1)

                def turn(out, rows, ready, k, n, chunks=C, lo=0):
                    def unit(s, r, tile):
                        pe.wait_ge(ready[s], k * r + n)
                        for c in range(chunks):
                            mm = nc.tensor.transpose(out[s][:, c * P:(c + 1) * P],
                                                     rows[s][:, lo + c * P:lo + (c + 1) * P], ident[:])
                        mm.then_inc(turned[s], 1)
                    return unit

                def product32(out, left, w):
                    for c in range(C):
                        mm = nc.tensor.matmul(out, left[:, c, :], w[:, c, :], start=(c == 0), stop=(c == C - 1))
                    return mm

                def product(out, s, r, n, w, lo=0, chunks=C):
                    pe.wait_ge(act_h_ready[s], 6 * r + n)
                    for c in range(chunks):
                        for part in (0, 1):
                            nc.tensor.matmul(out, act_h[s][:, c, :], w[:, part, c, lo:lo + D],
                                             start=(c == 0 and part == 0), stop=False, skip_group_check=True)
                    pe.wait_ge(act_l_ready[s], 6 * r + n)
                    for c in range(chunks):
                        mm = nc.tensor.matmul(out, act_l[s][:, c, :], w[:, 0, c, lo:lo + D], start=False,
                                              stop=(c == chunks - 1), skip_group_check=True)
                    return mm

                def product_t(out, s, r, n, w, lo=0):
                    pe.wait_ge(act_h_ready[s], 6 * r + n)
                    for m in range(C):
                        for c in range(C):
                            for part in (0, 1):
                                nc.tensor.matmul(out[:, m * P:(m + 1) * P], w[:, part, c, lo + m * P:lo + (m + 1) * P],
                                                 act_h[s][:, c, :], start=(m == 0 and c == 0 and part == 0), stop=False,
                                                 skip_group_check=True)
                    pe.wait_ge(act_l_ready[s], 6 * r + n)
                    for m in range(C):
                        for c in range(C):
                            mm = nc.tensor.matmul(out[:, m * P:(m + 1) * P], w[:, 0, c, lo + m * P:lo + (m + 1) * P],
                                                  act_l[s][:, c, :], start=False, stop=(c == C - 1),
                                                  skip_group_check=True)
                    return mm

                def project_self(s, r, tile):
                    product_t(ps_a[s], s, r, 1, wqk).then_inc(q_done[s], 1)

                def value_self(s, r, tile):
                    pe.wait_ge(act_t_ready[s], 7 * r + 1)
                    product(ps_t[s][:], s, r, 1, wv).then_inc(v_done[s], 1)

                def self_scores(s, r, tile):
                    pe.wait_ge(q_ready[s], 3 * r + 1)
                    pe.wait_ge(act_t_ready[s], 7 * r + 1)
                    for c in range(C):
                        mm = nc.tensor.matmul(ps_a[s][:, 0:P], q_t[s][:, c, :], act_t[s][:, c, :],
                                              start=(c == 0), stop=(c == C - 1))
                    mm.then_inc(scored[s], 1)

                def turn_p(s, r, tile):
                    pe.wait_ge(p_ready[s], 3 * r + 1)
                    nc.tensor.transpose(ps_a[s][:, 0:P], p_n[s][:, 0:P], ident[:]).then_inc(p_turned[s], 1)

                def self_mix(s, r, tile):
                    pe.wait_ge(p_t_ready[s], 2 * r + 1)
                    pe.wait_ge(v_ready[s], 3 * r + 1)
                    nc.tensor.matmul(ps_t[s][:], p_t[s][:, 0:P], v_n[s][:], start=True, stop=True
                                     ).then_inc(rows_done[s], 1)

                def project_query(s, r, tile):
                    product_t(ps_t[s], s, r, 2, wcqk).then_inc(q_done[s], 1)

                def context_scores(s, r, tile):
                    pe.wait_ge(q_ready[s], 3 * r + 2)
                    pe.wait_ge(ctx_t_loaded, 16 * tile + 16)
                    for c in range(C):
                        for g in range(G):
                            mm = nc.tensor.matmul(ps_a[s][T * g:T * (g + 1), 0:S], q_t[s][:, c, T * g:T * (g + 1)],
                                                  ctx_t[:, c, g, :], start=(c == 0), stop=(c == C - 1),
                                                  skip_group_check=True)
                    mm.then_inc(scored[s], 1)

                def turn_pc(s, r, tile):
                    pe.wait_ge(p_ready[s], 3 * r + 2)
                    for c in range(SC):
                        nc.tensor.transpose(ps_t[s][:, c * P:(c + 1) * P], p_n[s][:, c * P:(c + 1) * P], ident[:])
                    pe.wait_ge(p4_ready[s], 2 * r + 1)
                    nc.tensor.transpose(ps_t[s][0:G, SC * P:SC * P + P], p_n[s][:, S:S + G], ident[:]
                                        ).then_inc(p_turned[s], 1)

                def context_mix(s, r, tile):
                    pe.wait_ge(p_t_ready[s], 2 * r + 2)
                    pe.wait_ge(ctx_n_loaded, 32 * tile + 32)
                    nc.tensor.matmul(ps_a[s][:], p_t[s][0:G, SC * P:], ctx_last[:], start=True, stop=False,
                                     skip_group_check=True)
                    for c in range(SC):
                        for g in range(G):
                            mm = nc.tensor.matmul(ps_a[s][T * g:T * (g + 1), :],
                                                  p_t[s][:, c * P + T * g:c * P + T * (g + 1)], ctx_n[:, g, c, :],
                                                  start=False, stop=(c == SC - 1), skip_group_check=True)
                    mm.then_inc(v_done[s], 1)

                def context_out(s, r, tile):
                    pe.wait_ge(act_t_ready[s], 7 * r + 3)
                    product32(ps_a[s][:], act_t[s], wcv).then_inc(rows_done[s], 1)

                def hidden(s, r, tile):
                    product(ps_a[s][:], s, r, 3, w1).then_inc(rows_done[s], 1)

                def project_k(s, r, tile):
                    product_t(ps_a[s], s, r, 4, wattn, D).then_inc(k_done[s], 1)

                def project_q(s, r, tile):
                    product_t(ps_t[s], s, r, 4, wattn, 0).then_inc(q_done[s], 1)

                def project_v(s, r, tile):
                    product(ps_v[:], s, r, 4, wattn, 2 * D).then_inc(v_done[s], 1)

                def head_scores(s, r, tile):
                    pe.wait_ge(q_ready[s], 3 * r + 3)
                    pe.wait_ge(k_ready[s], 4 * r + 4)
                    for c in range(C):
                        for g in range(G):
                            mm = nc.tensor.matmul(ps_a[s][T * g:T * (g + 1), c * P:(c + 1) * P],
                                                  q_t[s][:, c, T * g:T * (g + 1)],
                                                  kbd[:, c, g, :, :].rearrange("p h k -> p (h k)"),
                                                  start=True, stop=True, skip_group_check=True)
                    mm.then_inc(scored[s], 1)

                def head_mix(s, r, tile):
                    pe.wait_ge(pbd_ready[s], 4 * r + 4)
                    pe.wait_ge(v_ready[s], 3 * r + 3)
                    for c in range(C):
                        for h in range(HPC):
                            head = c * HPC + h
                            mm = nc.tensor.matmul(ps_t[s][HD * h:HD * (h + 1), c * P:(c + 1) * P],
                                                  v_n[s][:, HD * head:HD * (head + 1)],
                                                  pbd[:, head, :, :].rearrange("p g q -> p (g q)"),
                                                  start=True, stop=True, skip_group_check=True)
                    mm.then_inc(y_done[s], 1)

                def project_out(s, r, tile):
                    pe.wait_ge(y_ready[s], r + 1)
                    product32(ps_a[s][:], act_t[s], wproj).then_inc(rows_done[s], 1)

                def ffn_in(s, r, tile):
                    product(ps_a[s][:], s, r, 5, w12).then_inc(rows_done[s], 1)

                def ffn_out(s, r, tile):
                    product(ps_a[s][:], s, r, 6, w3, chunks=HC).then_inc(rows_done[s], 1)

                run_pipeline(pe, ORDER["pe"], {
                    "turn_xn": turn(ps_t, rows1, rows_ready, 6, 1), "project_self": project_self, "value_self": value_self,
                    "self_scores": self_scores, "turn_p": turn_p, "self_mix": self_mix,
                    "turn_h": turn(ps_a, rows2, rows_ready, 6, 2), "project_query": project_query,
                    "context_scores": context_scores, "turn_pc": turn_pc, "context_mix": context_mix,
                    "turn_w": turn(ps_t, v_n, v_ready, 3, 2), "context_out": context_out,
                    "turn_h2": turn(ps_t, rows1, rows_ready, 6, 3), "hidden": hidden,
                    "turn_x1n": turn(ps_t, rows1, rows_ready, 6, 4),
                    "project_k": project_k, "project_q": project_q, "project_v": project_v,
                    "head_scores": head_scores, "head_mix": head_mix, "project_out": project_out,
                    "turn_x2n": turn(ps_t, rows1, rows_ready, 6, 5), "ffn_in": ffn_in,
                    "turn_z": turn(ps_t, v_n, rows_ready, 6, 6, HC, H), "ffn_out": ffn_out})

        fs = ctx.enter_context(ExitStack())
        w12 = sb(fs, "w12", [P, C, 2 * H])
        w3 = sb(fs, "w3", [P, HC, D])
        ew12 = sb(fs, "ew12", [P, NE, C, 2 * H])
        ew3 = sb(fs, "ew3", [P, NE, HC, D])
        wg = sb(fs, "wg", [P, C, 1 + NE])
        sel_g = sb(fs, "sel_g", [P, H])
        sel_b = sb(fs, "sel_b", [P, H])
        bg = sb(fs, "bg", [P, 1 + NE])
        ebias = sb(fs, "ebias", [P, NE])
        eb12 = sb(fs, "eb12", [P, NE, 2 * H])
        eb3 = sb(fs, "eb3", [NE, D])
        falling = sb(fs, "falling", [P, NE])
        x2 = sb(fs, "e_x2", [P, D])
        xn = sb(fs, "e_xn", [P, D])
        xn_t = sb(fs, "e_xn_t", [P, C, P])
        u = [sb(fs, f"e_u{k}", [P, 2 * H]) for k in (0, 1)]
        gate = [sb(fs, f"e_gate{k}", [P, H]) for k in (0, 1)]
        z = sb(fs, "e_z", [P, H])
        z_t = sb(fs, "e_z_t", [P, HC, P])
        shared = sb(fs, "e_shared", [P, D])
        o = sb(fs, "e_o", [P, D])
        logits = sb(fs, "logits", [P, 1 + NE])
        scores = sb(fs, "scores", [P, 1 + NE])
        pick = sb(fs, "pick", [P, 4, NE])
        one = sb(fs, "one", [P, 8])
        coef_t = sb(fs, "coef_t", [NE, P])
        ps_u = ps_a[0:2]
        ps_turn, ps_gate, ps_sum, ps_shared, ps_coef = ps_t[0], ps_t[1], ps_a[2], ps_v, ps_e

        shared_loaded, gates_loaded = sem("shared_loaded"), sem("gates_loaded")
        ew_loaded = [sem(f"ew_loaded{q}") for q in range(4)]
        EW_PART = (0, 1, 1, 2, 2, 3, 3, 3)
        EW_COUNTS = [2 * 16 * EW_PART.count(q) for q in range(4)]
        e_x2_loaded, e_out_ready, e_out_stored = sem("e_x2_loaded"), sem("e_out_ready"), sem("e_out_stored")
        e_var, e_rstd = sem("e_var"), sem("e_rstd")
        xn_ready, xn_turned, xn_t_ready = sem("xn_ready"), sem("xn_turned"), sem("xn_t_ready")
        e_u_done, e_u_ready, e_gate_ready = sem("e_u_done"), sem("e_u_ready"), sem("e_gate_ready")
        e_z_ready, e_z_turned, e_z_t_ready = sem("e_z_ready"), sem("e_z_turned"), sem("e_z_t_ready")
        logits_done, logits_ready, scores_ready = sem("logits_done"), sem("logits_ready"), sem("scores_ready")
        margin_ready, shares_ready = sem("margin_ready"), sem("shares_ready")
        coef_ready, coef_turned, coef_t_ready = sem("coef_ready"), sem("coef_turned"), sem("coef_t_ready")
        shared_done, e_sum_done, e_step = sem("shared_done"), sem("e_sum_done"), sem("e_step")
        GLUS = 1 + NE
        E_STEPS = 16 + 5 * NE + 2

        block = fs.enter_context(nc.Block())

        def tiles_to_do(eng):
            return eng.value_load(redo[0:1, 0:1], min_val=1, max_val=TILES)

        def tile_of(eng, i):
            return eng.value_load(redo[0:1, bass.ds(i + 1, 1)], min_val=0, max_val=TILES - 1)

        @block.sync
        def _(sp):
            count = tiles_to_do(sp)

            def load_x2(i):
                tile = tile_of(sp, i)
                sp.dma_start(x2[:], a["x2"][bass.ds(tile, 1)].rearrange("a p d -> (a p) d")).then_inc(e_x2_loaded, 16)
                return tile

            load_x2(0)
            for name, dst in (("w12", w12), ("w3", w3), ("wg", wg)):
                sp.dma_start(dst[:], a[name]).then_inc(shared_loaded, 16)
            for name, dst in (("sel_g", sel_g), ("sel_b", sel_b), ("bg", bg), ("ebias", ebias), ("falling", falling)):
                sp.dma_start(dst[:], a[name].partition_broadcast(P)).then_inc(gates_loaded, 16)
            sp.dma_start(eb3[:], a["eb3"]).then_inc(gates_loaded, 16)
            sp.dma_start(eb12[:], a["eb12"].partition_broadcast(P)).then_inc(gates_loaded, 16)
            for e in range(NE):
                sp.dma_start(ew12[:, e], a["ew12"][:, e]).then_inc(ew_loaded[EW_PART[e]], 16)
                sp.dma_start(ew3[:, e], a["ew3"][:, e]).then_inc(ew_loaded[EW_PART[e]], 16)
            with sp.Fori(0, count) as i:
                tile = tile_of(sp, i)
                sp.wait_ge(e_out_ready, i + 1)
                sp.dma_start(a["out"][bass.ds(tile, 1)].rearrange("a p d -> (a p) d"), o[:]).then_inc(e_out_stored, 16)
                sp.wait_ge(e_out_stored, 16 * i + 16)
                sp.sem_inc(stats_seen, 1)
                load_x2(i + 1)
                sp.wait_ge(e_x2_loaded, 16 * i + 32)
                sp.sem_inc(stats_seen, 1)
            sp.wait_ge(shared_loaded, 16 * 3)
            sp.wait_ge(gates_loaded, 16 * 7)
            for q in range(4):
                sp.wait_ge(ew_loaded[q], EW_COUNTS[q])

        @block.gpsimd
        def _(pool):
            count = tiles_to_do(pool)
            with pool.Fori(0, count) as i:
                for k in range(1 + GLUS):
                    pool.wait_ge(e_var, (1 + GLUS) * i + k + 1)
                    nc.gpsimd.tensor_tensor(rstd[0][:], var[0][:], mhalf[:], ALU.pow).then_inc(e_rstd, 1)

        @block.scalar
        def _(act):
            count = tiles_to_do(act)

            def gated(i, k):
                act.wait_ge(e_u_ready, GLUS * i + k + 1)
                nc.scalar.activation(gate[k % 2][:], u[k % 2][:, 0:H], ACT.Silu).then_inc(e_gate_ready, 1)

            def turned_z(i, k):
                act.wait_ge(e_z_turned, GLUS * i + k + 1)
                nc.scalar.copy(z_t[:].rearrange("p c r -> p (c r)"), ps_turn[:, 0:H]).then_inc(e_z_t_ready, 1)

            with act.Fori(0, count) as i:
                act.wait_ge(xn_turned, i + 1)
                nc.scalar.copy(xn_t[:].rearrange("p c r -> p (c r)"), ps_turn[:]).then_inc(xn_t_ready, 1)
                gated(i, 0)
                turned_z(i, 0)
                act.wait_ge(logits_ready, i + 1)
                nc.scalar.activation(scores[:], logits[:], ACT.Sigmoid).then_inc(scores_ready, 1)
                act.wait_ge(margin_ready, i + 1)
                nc.scalar.activation(one[:, 3:4], one[:, 2:3], ACT.Sigmoid, scale=-1.0).then_inc(shares_ready, 1)
                nc.scalar.activation(one[:, 4:5], one[:, 2:3], ACT.Sigmoid).then_inc(shares_ready, 1)
                act.wait_ge(coef_turned, i + 1)
                nc.scalar.copy(coef_t[:], ps_coef[0:NE, 0:P]).then_inc(coef_t_ready, 1)
                gated(i, 1)
                for k in range(1, GLUS):
                    if k + 1 < GLUS:
                        gated(i, k + 1)
                    turned_z(i, k)

        @block.vector
        def _(dve):
            count = tiles_to_do(dve)
            with dve.Fori(0, count) as i:
                tile = tile_of(dve, i)
                steps = [0]

                def step(ins):
                    steps[0] += 1
                    ins.then_inc(e_step, 1)
                    dve.wait_ge(e_step, E_STEPS * i + steps[0])

                def moments(n, rows):
                    step(nc.vector.bn_stats(stats[0][:], rows))
                    dve.sem_inc(stats_seen, 1)
                    step(nc.vector.bn_aggr(mv[0][:], stats[0][:]))
                    nc.vector.tensor_scalar(var[0][:], mv[0][:, 1:2], 1e-5, None, ALU.add).then_inc(e_var, 1)
                    dve.wait_ge(e_rstd, (1 + GLUS) * i + n)

                def biased(k, bias):
                    dve.wait_ge(e_u_done, GLUS * i + k + 1)
                    nc.vector.tensor_tensor(u[k % 2][:], ps_u[k % 2][:], bias, ALU.add).then_inc(e_u_ready, 1)

                def gated(k):
                    dve.wait_ge(e_gate_ready, GLUS * i + k + 1)
                    if k:
                        dve.wait_ge(e_z_turned, GLUS * i + k)
                    step(nc.vector.tensor_tensor(z[:], gate[k % 2][:], u[k % 2][:, H:], ALU.mult))
                    if 0 < k < NE:
                        biased(k + 1, eb12[:, k, :])
                    moments(2 + k, z[:])

                dve.wait_ge(e_x2_loaded, 16 * i + 16)
                moments(1, x2[:])
                nc.vector.tensor_scalar(xn[:], x2[:], mv[0][:, 0:1], rstd[0][:], ALU.subtract, ALU.mult
                                        ).then_inc(xn_ready, 1)
                biased(0, b12[:])
                gated(0)
                step(nc.vector.scalar_tensor_tensor(z[:], z[:], mv[0][:, 0:1], ln_g[:], ALU.subtract, ALU.mult))
                nc.vector.scalar_tensor_tensor(z[:], z[:], rstd[0][:], ln_b[:], ALU.mult, ALU.add
                                               ).then_inc(e_z_ready, 1)
                dve.wait_ge(shared_done, i + 1)
                step(nc.vector.tensor_tensor(shared[:], ps_shared[:], b3[:], ALU.add))
                step(nc.vector.tensor_tensor(o[:], shared[:], x2[:], ALU.add))
                dve.wait_ge(gates_loaded, 16 * 7)
                dve.wait_ge(logits_done, i + 1)
                nc.vector.tensor_tensor(logits[:], ps_gate[:, 0:1 + NE], bg[:], ALU.add).then_inc(logits_ready, 1)
                dve.wait_ge(scores_ready, i + 1)
                step(nc.vector.tensor_tensor(pick[:, 0, :], scores[:, 1:], ebias[:], ALU.add))
                step(nc.vector.reduce_max(one[:, 0:1], pick[:, 0, :], AX.X))
                step(nc.vector.scalar_tensor_tensor(pick[:, 1, :], pick[:, 0, :], one[:, 0:1], falling[:],
                                                    ALU.is_ge, ALU.mult))
                step(nc.vector.reduce_max(one[:, 1:2], pick[:, 1, :], AX.X))
                step(nc.vector.tensor_scalar(pick[:, 2, :], falling[:], one[:, 1:2], None, ALU.is_equal))
                step(nc.vector.tensor_tensor(pick[:, 3, :], pick[:, 2, :], scores[:, 1:], ALU.mult))
                step(nc.vector.reduce_sum(one[:, 5:6], pick[:, 3, :], AX.X))
                nc.vector.tensor_tensor(one[:, 2:3], one[:, 5:6], scores[:, 0:1], ALU.subtract
                                        ).then_inc(margin_ready, 1)
                dve.wait_ge(shares_ready, 2 * i + 2)
                mine = sel[:, bass.ds(tile, 1)]
                step(nc.vector.tensor_tensor(one[:, 6:7], one[:, 4:5], mine, ALU.mult))
                step(nc.vector.scalar_tensor_tensor(one[:, 7:8], one[:, 3:4], -1.0, mine, ALU.add, ALU.mult))
                nc.vector.tensor_scalar(pick[:, 3, :], pick[:, 2, :], one[:, 6:7], None, ALU.mult
                                        ).then_inc(coef_ready, 1)
                step(nc.vector.scalar_tensor_tensor(o[:], shared[:], one[:, 7:8], o[:], ALU.mult, ALU.add))
                dve.wait_ge(coef_ready, i + 1)
                biased(1, eb12[:, 0, :])
                for k in range(1, GLUS):
                    gated(k)
                    step(nc.vector.scalar_tensor_tensor(z[:], z[:], mv[0][:, 0:1], sel_g[:], ALU.subtract, ALU.mult))
                    step(nc.vector.scalar_tensor_tensor(z[:], z[:], rstd[0][:], sel_b[:], ALU.mult, ALU.add))
                    nc.vector.tensor_scalar(z[:], z[:], pick[:, 3, k - 1:k], None, ALU.mult).then_inc(e_z_ready, 1)
                assert steps[0] == E_STEPS, steps[0]
                dve.wait_ge(e_sum_done, i + 1)
                nc.vector.tensor_tensor(o[:], ps_sum[:], o[:], ALU.add).then_inc(e_out_ready, 1)

        @block.tensor
        def _(pe):
            count = tiles_to_do(pe)
            pe.wait_ge(shared_loaded, 16 * 3)

            def product(out, w):
                for c in range(C):
                    mm = nc.tensor.matmul(out, xn_t[:, c, :], w[:, c, :], start=(c == 0), stop=(c == C - 1))
                return mm

            def turn_z(i, k):
                pe.wait_ge(e_z_ready, GLUS * i + k + 1)
                for c in range(HC):
                    mm = nc.tensor.transpose(ps_turn[:, c * P:(c + 1) * P], z[:, c * P:(c + 1) * P], ident[:])
                mm.then_inc(e_z_turned, 1)
                pe.wait_ge(e_z_t_ready, GLUS * i + k + 1)

            with pe.Fori(0, count) as i:
                pe.wait_ge(xn_ready, i + 1)
                for c in range(C):
                    mm = nc.tensor.transpose(ps_turn[:, c * P:(c + 1) * P], xn[:, c * P:(c + 1) * P], ident[:])
                mm.then_inc(xn_turned, 1)
                pe.wait_ge(xn_t_ready, i + 1)
                product(ps_u[0][:], w12).then_inc(e_u_done, 1)
                product(ps_gate[:, 0:1 + NE], wg).then_inc(logits_done, 1)
                turn_z(i, 0)
                for c in range(HC):
                    mm = nc.tensor.matmul(ps_shared[:], z_t[:, c, :], w3[:, c, :], start=(c == 0), stop=(c == HC - 1))
                mm.then_inc(shared_done, 1)
                pe.wait_ge(ew_loaded[0], EW_COUNTS[0])
                product(ps_u[1][:], ew12[:, 0]).then_inc(e_u_done, 1)
                pe.wait_ge(ew_loaded[1], EW_COUNTS[1])
                pe.wait_ge(e_u_ready, GLUS * i + 1)
                product(ps_u[0][:], ew12[:, 1]).then_inc(e_u_done, 1)
                pe.wait_ge(coef_ready, i + 1)
                nc.tensor.transpose(ps_coef[0:NE, 0:P], pick[:, 3, :], ident[:]).then_inc(coef_turned, 1)
                pe.wait_ge(coef_t_ready, i + 1)
                pe.wait_ge(gates_loaded, 16 * 7)
                nc.tensor.matmul(ps_sum[:], coef_t[:], eb3[:], start=True, stop=False, skip_group_check=True)
                for k in range(1, GLUS):
                    if k + 2 < GLUS:
                        pe.wait_ge(ew_loaded[EW_PART[k + 1]], EW_COUNTS[EW_PART[k + 1]])
                        pe.wait_ge(e_u_ready, GLUS * i + k + 1)
                        product(ps_u[k % 2][:], ew12[:, k + 1]).then_inc(e_u_done, 1)
                    turn_z(i, k)
                    for c in range(HC):
                        mm = nc.tensor.matmul(ps_sum[:], z_t[:, c, :], ew3[:, k - 1, c, :], start=False,
                                              stop=(k == NE and c == HC - 1), skip_group_check=True)
                mm.then_inc(e_sum_done, 1)


def rows_on_partitions(w):
    return np.ascontiguousarray(w.reshape(-1, P, w.shape[-1]).transpose(1, 0, 2))


def layout(v):
    names = {k.replace("L0_", "", 1): np.asarray(x) for k, x in v.items()}
    cx = names["ctx_1024"].reshape(TILES, G, S, D)[::-1].reshape(B, S, D)
    w = {k[6:]: names[k] for k in names if k.startswith("xattn_")}
    f = {k[4:]: names[k] for k in names if k.startswith("ffn_")}
    at = {
        "x": names["x"].reshape(TILES, P, D)[::-1],
        "ctx_t": cx.reshape(TILES, G, S, C, P).transpose(0, 4, 3, 1, 2),
        "ctx_n": cx[:, :SC * P].reshape(TILES, G, SC, P, D).transpose(0, 3, 1, 2, 4),
        "ctx_last": cx[:, S - 1].reshape(TILES, G, D),
        "wq_t": rows_on_partitions(w["Wq"].T), "wk_t": rows_on_partitions(w["Wk"].T),
        "wcq_t": rows_on_partitions(w["Wcq"].T), "wck_t": rows_on_partitions(w["Wck"].T),
        "wv": rows_on_partitions(w["Wv"]), "wcv": rows_on_partitions(w["Wcv"]), "w1": rows_on_partitions(w["W1"]),
        "wattn": rows_on_partitions(names["attn_W_attn"]), "wproj": rows_on_partitions(names["attn_W_proj"]),
        "gamma": w["gamma"], "beta": w["beta"], "b1": w["b1"],
        "index_b": f["index_b"].reshape(P, MC), "index_t": f["index_t"].reshape(P, MC),
        "w12": rows_on_partitions(np.concatenate([f["sw1"], f["sw2"]]).T), "w3": rows_on_partitions(f["sw3"].T),
        "b12": np.concatenate([f["sb1"], f["sb2"]]), "b3": f["sb3"], "ln_g": f["s_ln_g"], "ln_b": f["s_ln_b"],
        "wg": rows_on_partitions(np.concatenate([f["sg_w"], f["eg_w"]]).T),
        "bg": np.concatenate([f["sg_b"], f["eg_b"]]), "ebias": f["exp_bias"],
        "ew12": np.concatenate([f["ew1"], f["ew2"]], axis=1).reshape(NE, 2 * H, C, P).transpose(3, 0, 2, 1),
        "ew3": f["ew3"].reshape(NE, D, HC, P).transpose(3, 0, 2, 1),
        "eb12": np.concatenate([f["eb1"], f["eb2"]], axis=1), "eb3": f["eb3"],
        "sel_g": f["sel_ln_g"], "sel_b": f["sel_ln_b"],
    }
    r = np.arange(P)
    at["ident"] = np.eye(P, dtype=np.float32)
    at["entry_of"] = np.arange(B, dtype=np.float32).reshape(TILES, G)[::-1].reshape(B)
    at["upto"] = np.triu(np.ones((TILES, TILES), np.float32))
    at["nth"] = np.arange(1, TILES + 1, dtype=np.float32)
    at["tile_id"] = np.arange(TILES, dtype=np.float32).reshape(TILES, 1)
    at["iota_t"] = np.arange(T, dtype=np.float32)
    at["mask_self"] = np.where((r[:, None] // T == r[None, :] // T) & (r[None, :] <= r[:, None]), 0.0, NEG)
    at["mask_head"] = np.where(r[None, :T] <= r[:, None] % T, 0.0, NEG)
    at["mask_entry"] = r[:, None] // T == np.arange(G)[None, :]
    at["falling"] = np.arange(NE, 0, -1)
    echoic, length = 16, 1024
    fading = 1.0 - np.linspace(0.0, 1.0, length - echoic + 1) ** (1.0 / np.e)
    weight = np.concatenate([np.ones(echoic - 1), fading])
    at["decay"] = weight[np.clip(r[:, None] % T - r[None, :T], 0, T - 1)]
    for k in ("mask_self", "mask_head", "mask_entry", "falling", "decay"):
        at[k] = at[k].astype(np.float32)
    return {k: np.ascontiguousarray(x) for k, x in at.items()}


def kernel(**inputs):
    import concourse.bacc as bacc
    from concourse.bass_utils import run_bass_kernel_spmd

    nc = bacc.Bacc("TRN2", target_bir_lowering=False, num_devices=1)
    arrays = {f"in_{k}": x for k, x in layout(inputs).items()}
    a = {k[3:]: nc.dram_tensor(k, x.shape, mybir.dt.from_np(x.dtype), kind="ExternalInput").ap()
         for k, x in arrays.items()}
    a["out"] = nc.dram_tensor("out_0", (TILES, P, D), F32, kind="ExternalOutput").ap()
    a["x2"] = nc.dram_tensor("x2_scratch", (TILES, P, D), F32, kind="Internal").ap()
    build(nc, a)
    r = run_bass_kernel_spmd(nc, [arrays], core_ids=[0])
    return np.ascontiguousarray(r.results[0]["out_0"][::-1]).reshape(B, T, D)
```
